# Optimizing a Trainium2 kernel written in Bass

```python
import numpy as np
import jax
import jax.numpy as jnp

def _softmax(x, axis=-1):
    return jax.nn.softmax(x, axis=axis)

def _gelu(x):
    return jax.nn.gelu(x, approximate=True)

def _silu(x):
    return jax.nn.silu(x)

def _sigmoid(x):
    return jax.nn.sigmoid(x)

def _layernorm(x, axis=-1, eps=1e-05):
    m = jnp.mean(x, axis=axis, keepdims=True)
    v = jnp.var(x, axis=axis, keepdims=True)
    return (x - m) / jnp.sqrt(v + eps)

def _scatter_add(tgt, idx, src, axis=0):
    return tgt.at[idx].add(src)

def _segment_sum(src, seg, n):
    return jax.ops.segment_sum(src, seg, n)
kernel_name = 'mk_perceiver_d1_seqx_r4_237093'

def setup_inputs(seed: int=0):
    np.random.seed(seed)
    _w = jnp.asarray

    def _rec_inputs():
        import jax
        import jax.numpy as jnp
        _rk = jax.random.key(seed)
        x = -0.0002928 + 1 * jax.random.normal(jax.random.fold_in(_rk, 1), (4, 256, 256), jnp.float32)
        _lenS = 256 - jax.random.randint(jax.random.fold_in(_rk, 7), (4,), 0, max(1, 256 // 4) + 1, jnp.int32)
        _lenS2 = 4096 - jax.random.randint(jax.random.fold_in(_rk, 8), (4,), 0, max(1, 4096 // 4) + 1, jnp.int32)
        _ctx_768P = jax.random.normal(jax.random.fold_in(_rk, 11), (4, 16, 192), jnp.float32)
        _ctx_768c = jax.random.dirichlet(jax.random.fold_in(_rk, 511), 0.3 * jnp.ones((16,), jnp.float32), (4, 4096))
        _ctx_768t = jnp.einsum('bsk,bkd->bsd', _ctx_768c, _ctx_768P)
        _ctx_768t = _ctx_768t * jax.lax.rsqrt(jnp.mean(jnp.square(_ctx_768t)) + 1e-12) * 0.953939
        ctx_768 = -0.00055796 + 0.999787 * (_ctx_768t + 0.3 * jax.random.normal(jax.random.fold_in(_rk, 611), (4, 4096, 192), jnp.float32))
        return (x, ctx_768)
    x, ctx_768 = _rec_inputs()

    def _L0_xattn_setup():
        import jax, jax.numpy as jnp
        import numpy as np
        HEADS = 16
        DIM_HEAD = 64
        key = jax.random.key(seed)
        ks = jax.random.split(key, 7)
        b, n, m = (2, 512, 256)
        query_dim, context_dim = (256, 192)
        inner = HEADS * DIM_HEAD
        s_q = 1.0 / np.sqrt(query_dim)
        s_c = 1.0 / np.sqrt(context_dim)
        s_i = 1.0 / np.sqrt(inner)
        return {'x': jax.random.normal(ks[0], (b, n, query_dim), jnp.float32), 'context': jax.random.normal(ks[1], (b, m, context_dim), jnp.float32), 'Wq': jax.random.normal(ks[2], (query_dim, inner), jnp.float32) * s_q, 'Wk': jax.random.normal(ks[3], (context_dim, inner), jnp.float32) * s_c, 'Wv': jax.random.normal(ks[4], (context_dim, inner), jnp.float32) * s_c, 'Wo': jax.random.normal(ks[5], (inner, query_dim), jnp.float32) * s_i, 'bo': jax.random.normal(ks[6], (query_dim,), jnp.float32) * 0.01}
    _L0_xattn_all = _L0_xattn_setup()
    _L0_xattn_in = {k: v for k, v in _L0_xattn_all.items() if k in ('Wq', 'Wk', 'Wv', 'Wo', 'bo')}
    del _L0_xattn_all

    def _L0_attn_setup():
        import jax, jax.numpy as jnp
        import numpy as np
        B, T, HS, H, R = (4, 512, 256, 16, 16)
        D = HS // H
        LOGIT_01 = float(np.log(0.1 / 0.9))
        LOGIT_098 = float(np.log(0.98 / 0.02))

        def _rope_cos_sin(seq_len, dim, base=10000.0):
            half = dim // 2
            inv_freq = 1.0 / base ** (jnp.arange(half, dtype=jnp.float32) / half)
            freqs = jnp.arange(seq_len, dtype=jnp.float32)[:, None] * inv_freq[None, :]
            return (jnp.cos(freqs), jnp.sin(freqs))

        def _apply_rope(x, cos, sin):
            c = cos[None, :, None, :]
            s = sin[None, :, None, :]
            x1 = x[..., 0::2]
            x2 = x[..., 1::2]
            r1 = x1 * c - x2 * s
            r2 = x1 * s + x2 * c
            return jnp.stack((r1, r2), axis=-1).reshape(x.shape)
        key = jax.random.key(seed)
        ks = jax.random.split(key, 10)

        def rn(k, shape, s=0.02):
            return jax.random.normal(k, shape, dtype=jnp.float32) * s
        return {'x': jax.random.normal(ks[0], (B, T, HS), dtype=jnp.float32), 'q_w': rn(ks[1], (HS, HS)), 'k_w': rn(ks[2], (HS, HS)), 'v_w': rn(ks[3], (HS, HS)), 'Wq': rn(ks[4], (H, R, D), 0.05), 'Wk': rn(ks[5], (H, R, D), 0.05), 'g_w': rn(ks[6], (H * R, HS)), 'g_b': jnp.full((H * R,), LOGIT_01, dtype=jnp.float32), 'base_decay_logits': jnp.full((H, R), LOGIT_098, dtype=jnp.float32), 'out_w': rn(ks[7], (HS, HS)), 'out_b': jnp.zeros((HS,), dtype=jnp.float32), 'ln_g': jnp.ones((HS,), dtype=jnp.float32), 'ln_b': jnp.zeros((HS,), dtype=jnp.float32)}
    _L0_attn_all = _L0_attn_setup()
    _L0_attn_in = {k: v for k, v in _L0_attn_all.items() if k in ('q_w', 'k_w', 'v_w', 'Wq', 'Wk', 'g_w', 'g_b', 'base_decay_logits', 'out_w', 'out_b', 'ln_g', 'ln_b')}
    del _L0_attn_all

    def _L0_ffn_setup():
        import jax, jax.numpy as jnp
        import numpy as np
        D = 256
        H = 256
        E = 8
        K = 2
        I = 2 * 256
        ROUTE_SCALE = 1.0
        key = jax.random.key(seed)
        ks = jax.random.split(key, 12)
        s = lambda *sh: 1.0 / np.sqrt(sh[-1])
        return {'x': jax.random.normal(ks[0], (1, 512, D), jnp.float32), 'gate_w': jax.random.normal(ks[1], (E, D), jnp.float32) * s(E, D), 'w1': jax.random.normal(ks[2], (E, H, D), jnp.float32) * s(H, D), 'b1': jax.random.normal(ks[3], (E, H), jnp.float32) * 0.01, 'w2': jax.random.normal(ks[4], (E, D, H), jnp.float32) * s(D, H), 'b2': jax.random.normal(ks[5], (E, D), jnp.float32) * 0.01, 'w3': jax.random.normal(ks[6], (E, H, D), jnp.float32) * s(H, D), 'b3': jax.random.normal(ks[7], (E, H), jnp.float32) * 0.01, 'sw1': jax.random.normal(ks[8], (I, D), jnp.float32) * s(I, D), 'sw2': jax.random.normal(ks[9], (I, D), jnp.float32) * s(I, D), 'sw3': jax.random.normal(ks[10], (D, I), jnp.float32) * s(D, I)}
    _L0_ffn_all = _L0_ffn_setup()
    _L0_ffn_in = {k: v for k, v in _L0_ffn_all.items() if k in ('gate_w', 'w1', 'b1', 'w2', 'b2', 'w3', 'b3', 'sw1', 'sw2', 'sw3')}
    del _L0_ffn_all
    return {'x': x, 'ctx_768': ctx_768, 'L0_xattn_Wq': _L0_xattn_in['Wq'], 'L0_xattn_Wk': _L0_xattn_in['Wk'], 'L0_xattn_Wv': _L0_xattn_in['Wv'], 'L0_xattn_Wo': _L0_xattn_in['Wo'], 'L0_xattn_bo': _L0_xattn_in['bo'], 'L0_attn_q_w': _L0_attn_in['q_w'], 'L0_attn_k_w': _L0_attn_in['k_w'], 'L0_attn_v_w': _L0_attn_in['v_w'], 'L0_attn_Wq': _L0_attn_in['Wq'], 'L0_attn_Wk': _L0_attn_in['Wk'], 'L0_attn_g_w': _L0_attn_in['g_w'], 'L0_attn_g_b': _L0_attn_in['g_b'], 'L0_attn_base_decay_logits': _L0_attn_in['base_decay_logits'], 'L0_attn_out_w': _L0_attn_in['out_w'], 'L0_attn_out_b': _L0_attn_in['out_b'], 'L0_attn_ln_g': _L0_attn_in['ln_g'], 'L0_attn_ln_b': _L0_attn_in['ln_b'], 'L0_ffn_gate_w': _L0_ffn_in['gate_w'], 'L0_ffn_w1': _L0_ffn_in['w1'], 'L0_ffn_b1': _L0_ffn_in['b1'], 'L0_ffn_w2': _L0_ffn_in['w2'], 'L0_ffn_b2': _L0_ffn_in['b2'], 'L0_ffn_w3': _L0_ffn_in['w3'], 'L0_ffn_b3': _L0_ffn_in['b3'], 'L0_ffn_sw1': _L0_ffn_in['sw1'], 'L0_ffn_sw2': _L0_ffn_in['sw2'], 'L0_ffn_sw3': _L0_ffn_in['sw3']}

def reference(x, ctx_768, L0_xattn_Wq, L0_xattn_Wk, L0_xattn_Wv, L0_xattn_Wo, L0_xattn_bo, L0_attn_q_w, L0_attn_k_w, L0_attn_v_w, L0_attn_Wq, L0_attn_Wk, L0_attn_g_w, L0_attn_g_b, L0_attn_base_decay_logits, L0_attn_out_w, L0_attn_out_b, L0_attn_ln_g, L0_attn_ln_b, L0_ffn_gate_w, L0_ffn_w1, L0_ffn_b1, L0_ffn_w2, L0_ffn_b2, L0_ffn_w3, L0_ffn_b3, L0_ffn_sw1, L0_ffn_sw2, L0_ffn_sw3):
    import jax
    import jax.numpy as jnp

    def _L0_xattn_ref(x, context, Wq, Wk, Wv, Wo, bo):
        import jax, jax.numpy as jnp
        import numpy as np
        HEADS = 16
        DIM_HEAD = 64
        b, n, _ = x.shape
        h, d = (HEADS, DIM_HEAD)
        scale = d ** (-0.5)
        q = (x @ Wq).reshape(b, n, h, d).transpose(0, 2, 1, 3)
        k = (context @ Wk).reshape(b, -1, h, d).transpose(0, 2, 1, 3)
        v = (context @ Wv).reshape(b, -1, h, d).transpose(0, 2, 1, 3)
        sim = jnp.einsum('bhid,bhjd->bhij', q, k) * scale
        attn = jax.nn.softmax(sim, axis=-1)
        out = jnp.einsum('bhij,bhjd->bhid', attn, v)
        out = out.transpose(0, 2, 1, 3).reshape(b, n, h * d)
        return out @ Wo + bo

    def _L0_attn_ref(x, q_w, k_w, v_w, Wq, Wk, g_w, g_b, base_decay_logits, out_w, out_b, ln_g, ln_b):
        import jax, jax.numpy as jnp
        import numpy as np
        B, T, HS, H, R = (4, 512, 256, 16, 16)
        D = HS // H
        LOGIT_01 = float(np.log(0.1 / 0.9))
        LOGIT_098 = float(np.log(0.98 / 0.02))

        def _rope_cos_sin(seq_len, dim, base=10000.0):
            half = dim // 2
            inv_freq = 1.0 / base ** (jnp.arange(half, dtype=jnp.float32) / half)
            freqs = jnp.arange(seq_len, dtype=jnp.float32)[:, None] * inv_freq[None, :]
            return (jnp.cos(freqs), jnp.sin(freqs))

        def _apply_rope(x, cos, sin):
            c = cos[None, :, None, :]
            s = sin[None, :, None, :]
            x1 = x[..., 0::2]
            x2 = x[..., 1::2]
            r1 = x1 * c - x2 * s
            r2 = x1 * s + x2 * c
            return jnp.stack((r1, r2), axis=-1).reshape(x.shape)
        b, t, hs = x.shape
        h, r, d = Wq.shape
        q = (x @ q_w.T).reshape(b, t, h, d)
        k = (x @ k_w.T).reshape(b, t, h, d)
        v = (x @ v_w.T).reshape(b, t, h, d)
        cos, sin = _rope_cos_sin(t, d)
        q = _apply_rope(q, cos, sin)
        k = _apply_rope(k, cos, sin)
        q_r = jnp.einsum('bthd,hrd->bthr', q, Wq)
        k_r = jnp.einsum('bthd,hrd->bthr', k, Wk)
        g = jax.nn.sigmoid((x @ g_w.T + g_b).reshape(b, t, h, r))
        decay = jax.nn.sigmoid(base_decay_logits)[None, :, :, None]
        scale = 1.0 / jnp.sqrt(jnp.asarray(d, dtype=x.dtype))

        def step(M, inp):
            q_t, k_t, v_t, g_t = inp
            M = M * decay + jnp.einsum('bhr,bhd->bhrd', g_t * k_t * scale, v_t)
            y = jnp.einsum('bhr,bhrd->bhd', q_t, M)
            return (M, y)
        xs = (q_r.transpose(1, 0, 2, 3), k_r.transpose(1, 0, 2, 3), v.transpose(1, 0, 2, 3), g.transpose(1, 0, 2, 3))
        M0 = jnp.zeros((b, h, r, d), dtype=x.dtype)
        _, Y = jax.lax.scan(step, M0, xs)
        Y = Y.transpose(1, 0, 2, 3).reshape(b, t, hs)
        out = Y @ out_w.T + out_b
        hres = x + out
        mu = jnp.mean(hres, axis=-1, keepdims=True)
        var = jnp.mean((hres - mu) ** 2, axis=-1, keepdims=True)
        return (hres - mu) / jnp.sqrt(var + 1e-05) * ln_g + ln_b

    def _L0_ffn_ref(x, gate_w, w1, b1, w2, b2, w3, b3, sw1, sw2, sw3):
        import jax, jax.numpy as jnp
        import numpy as np
        D = 256
        H = 256
        E = 8
        K = 2
        I = 2 * 256
        ROUTE_SCALE = 1.0
        B, S, _ = x.shape
        xt = x.reshape(-1, D)
        logits = xt @ gate_w.T
        scores = jax.nn.softmax(logits.astype(jnp.float32), axis=-1)
        top_vals, idx = jax.lax.top_k(scores, K)
        weights = jnp.take_along_axis(scores, idx, axis=1).astype(x.dtype) * ROUTE_SCALE
        xs = xt[:, None, :] * weights[:, :, None]
        y = jnp.zeros_like(xt)
        for e in range(E):
            mask = (idx == e).astype(x.dtype)
            h = jax.nn.silu(jnp.einsum('tkd,hd->tkh', xs, w1[e]) + b1[e])
            x2 = jnp.einsum('tkh,dh->tkd', h, w2[e]) + b2[e]
            x3 = jnp.einsum('tkd,hd->tkh', xs, w3[e]) + b3[e]
            y = y + jnp.sum(x2 * x3 * mask[:, :, None], axis=1)
        z = jax.nn.silu(xt @ sw1.T) * (xt @ sw2.T) @ sw3.T
        return (y + z).reshape(B, S, D)
    x = x + _L0_xattn_ref(_layernorm(x, axis=-1), ctx_768, L0_xattn_Wq, L0_xattn_Wk, L0_xattn_Wv, L0_xattn_Wo, L0_xattn_bo)
    x = x + _L0_attn_ref(_layernorm(x, axis=-1), L0_attn_q_w, L0_attn_k_w, L0_attn_v_w, L0_attn_Wq, L0_attn_Wk, L0_attn_g_w, L0_attn_g_b, L0_attn_base_decay_logits, L0_attn_out_w, L0_attn_out_b, L0_attn_ln_g, L0_attn_ln_b)
    x = x + _L0_ffn_ref(_layernorm(x, axis=-1), L0_ffn_gate_w, L0_ffn_w1, L0_ffn_b1, L0_ffn_w2, L0_ffn_b2, L0_ffn_w3, L0_ffn_b3, L0_ffn_sw1, L0_ffn_sw2, L0_ffn_sw3)
    return x

_drawn_inputs = setup_inputs


def setup_inputs(seed=0):
    import zlib

    import numpy as np

    out = dict(_drawn_inputs(seed))
    spreads = {'L0_attn_g_b': (-2.1972246170043945, 0.6),
     'L0_attn_base_decay_logits': (3.891820192337036, 0.6),
     'L0_attn_out_b': (0.0, 0.8),
     'L0_attn_ln_g': (1.0, 0.2),
     'L0_attn_ln_b': (0.0, 0.1)}
    factors = {'L0_xattn_bo': 5.811,
     'L0_attn_q_w': 8.0,
     'L0_attn_k_w': 8.0,
     'L0_attn_v_w': 8.0,
     'L0_attn_Wq': 8.0,
     'L0_attn_Wk': 8.0,
     'L0_attn_g_w': 8.0,
     'L0_attn_out_w': 8.0,
     'L0_ffn_b1': 39.162,
     'L0_ffn_b2': 8.0,
     'L0_ffn_b3': 35.411}
    for name, (base, spread) in spreads.items():
        noise = np.random.default_rng([zlib.crc32(name.encode()), seed]).standard_normal(out[name].shape)
        drawn = base * np.exp(spread * noise) if base else spread * noise
        out[name] = jnp.asarray(drawn.astype(out[name].dtype))
    for name, factor in factors.items():
        out[name] = (out[name] * factor).astype(out[name].dtype)
    return out
```

```python
import concourse.bass as bass
from concourse import mybir
from contextlib import ExitStack

F32 = mybir.dt.float32
F32R = mybir.dt.float32r
ALU = mybir.AluOpType
ACT = mybir.ActivationFunctionType
AX = mybir.AxisListType

P = 128
DM = 256
ROWS = 256
RT = ROWS // P
KEYS = 4096
CTX = 192
HEADS = 16
DH = 64
CH = 512
NC = KEYS // CH
KT = CH // P
QH = 4
NG = HEADS // QH
STEPS = QH * NC
SLOTS = 16
LEAD = 10
EPS = 1e-5
MROW = 64
M2 = 96


def cross_attention(nc, nb, top, d):
    ctx = ExitStack()
    with ctx:
        def sb(name, shape, dt=F32):
            return ctx.enter_context(nc.sbuf_tensor(name, shape, dt))

        def sem(name):
            return ctx.enter_context(nc.semaphore(name))

        x1, ident = top["x1"], top["ident"]
        C = sb("C", [P, 3, KEYS], F32R)
        craw = sb("craw", [P, 2, CH])
        KH = sb("KH", [P, SLOTS, CH], F32R)
        KL = sb("KL", [P, SLOTS, CH], F32R)
        V = sb("V", [P, NC * KT, QH * DH])
        PR = sb("PR", [P, 2, KT * ROWS])
        wk = sb("wk", [P, 2, 4, P], F32R)
        wv = sb("wv", [P, 4, QH * DH], F32R)
        wq = sb("wq", [P, 2, 2, P])
        wo = sb("wo", [P, 2, DM])
        Q1 = sb("Q1", [P, QH, ROWS], F32R)
        Q2 = sb("Q2", [P, QH, ROWS], F32R)
        qs = sb("qs", [P, ROWS])
        amx = sb("amx", [P, RT, NC])
        nmx = sb("nmx", [P, RT])
        acc = sb("acc", [P, KT * ROWS])
        accf = sb("accf", [P, 2, ROWS])
        Ot = sb("Ot", [P, 2, ROWS])
        rl = sb("rl", [P, RT])
        xnT = sb("xnT", [P, 2, nb * ROWS])

        ps = ctx.enter_context(nc.psum_tensor("ps1", [P, 8, 512], F32))
        psS, psK, psA, psO, psV, psM = ps[:, 0:2, :], ps[:, 2, :], ps[:, 3:5, :], ps[:, 5, :], ps[:, 6, :], ps[:, 7, :]

        xin = PR[:, :, :].rearrange("p a n -> p (a n)").rearrange("p (r n) -> p r n", n=DM)[:, 0:nb * RT, :]
        top["xin"][0] = xin

        x_in, xln_ready, wraw_in = sem("x_in"), sem("xln_ready"), sem("wraw_in")
        whi, wlo, wst = sem("whi"), sem("wlo"), sem("wst")
        xt_ps, xt_sb = sem("xt_ps"), sem("xt_sb")
        init = sem("init")
        craw_in, chi, cready = sem("craw_in"), sem("chi"), sem("cready")
        wk_in = [sem(f"wk_in{i}") for i in range(2)]
        wq_in = [sem(f"wq_in{i}") for i in range(2)]
        wo_in = [sem(f"wo_in{i}") for i in range(2)]
        wv_in = sem("wv_in")
        k_ps, k_hi, k_lo = sem("k_ps"), sem("k_hi"), sem("k_lo")
        a_ps, a_max = sem("a_ps"), sem("a_max")
        s_ps, p_ready, pv_done = sem("s_ps"), sem("p_ready"), sem("pv_done")
        acc_done, fold_done = sem("acc_done"), sem("fold_done")
        o_sb = sem("o_sb")
        l_ps, rl_ready, out_ps, x_added = sem("l_ps"), sem("rl_ready"), sem("out_ps"), sem("x_added")
        q_ps, q_sb, q_hi, q_ready = sem("q_ps"), sem("q_sb"), sem("q_hi"), sem("q_ready")
        m_ready, m_ps, m_row = sem("m_ready"), sem("m_ps"), sem("m_row")
        v_ps, v_sb = sem("v_ps"), sem("v_sb")
        ln = top["ln_sems"](sem)

        def vstep(u):
            return [25, 27, 29, 31, 32, 34, 36, 38][u // 2] + (u % 2)

        V_BEFORE = {}
        V_OWN = {}
        for u in range(2 * NC):
            s = vstep(u)
            (V_BEFORE if s < STEPS else V_OWN)[s % STEPS, u % 2] = u

        def loops(eng, quad):
            with eng.Fori(0, nb) as b:
                with eng.Fori(0, NG - 1) as g:
                    quad(b * NG + g, b, g)
                quad(b * NG + (NG - 1), b, NG - 1)

        block = ctx.enter_context(nc.Block())

        @block.sync
        def _(sp):
            sp.dma_start(x1[:, RT:, :], d["x"]).then_inc(x_in, 16)
            sp.dma_start(xin, d["x"]).then_inc(x_in, 16)
            sp.dma_start(top["bo"][:], d["bo"]).then_inc(x_in, 16)
            sp.dma_start(ident[:], d["ident"]).then_inc(x_in, 16)
            raw = V[:, :, :].rearrange("p t n -> p (t n)")
            sp.dma_start(raw[:, 0:4096], d["wk"]).then_inc(wraw_in, 16)
            sp.dma_start(raw[:, 4096:6144], d["wv"]).then_inc(wraw_in, 16)
            kh = KH[:, :, :].rearrange("p s n -> p (s n)").bitcast(F32).rearrange("p (t h m) -> p t h m", t=4, h=HEADS)
            kl = KL[:, :, :].rearrange("p s n -> p (s n)")[:, 0:4096].bitcast(F32).rearrange("p (t g m) -> p t g m", t=4, g=NG)
            sp.wait_ge(wlo, 2)
            for t in range(4):
                sp.dma_start(d["wk_split"][:, :, t, :].rearrange("h p m -> p h m"), kh[:, t, :, :]).then_inc(wst, 16)
                sp.dma_start(d["wv_split"][:, :, t, :].rearrange("g p m -> p g m"), kl[:, t, :, :]).then_inc(wst, 16)
            sp.wait_ge(wst, 128)

            def load_wk(n, h):
                sp.dma_start(wk[:, n % 2, :, :].bitcast(F32), d["wk_split"][bass.ds(h, 1)].rearrange("o p t m -> p (o t) m")).then_inc(wk_in[n % 2], 16)

            def load_wq(n, h):
                sp.dma_start(wq[:, n % 2, :, :], d["wq"][bass.ds(h, 1)].rearrange("o p t m -> p (o t) m")).then_inc(wq_in[n % 2], 16)

            def load_wo(n, h):
                sp.dma_start(wo[:, n % 2, :], d["wo"][bass.ds(h, 1)].rearrange("o p m -> p (o m)")).then_inc(wo_in[n % 2], 16)

            def load_wv(g):
                sp.dma_start(wv[:].bitcast(F32), d["wv_split"][bass.ds(g, 1)].rearrange("o p t m -> p (o t) m")).then_inc(wv_in, 16)

            def load_ctx(b, c):
                sp.dma_start(craw[:], d["ctx"][bass.ds(b, 1), c].rearrange("o p t n -> p (o t) n")).then_inc(craw_in, 16)

            load_wv(0)
            for n in range(2):
                load_wk(n, n)
                load_wq(n, n)
            load_wo(1, HEADS - 1)
            for c in range(NC):
                if c > 0:
                    sp.wait_ge(cready, c)
                load_ctx(0, c)
            sp.wait_ge(q_ps, 1)
            load_wq(2, 2)

            def quad(it, b, g):
                for hd in range(QH):
                    n = hd
                    h = g * QH + hd
                    sp.wait_ge(q_ps, it * QH + hd + 2)
                    load_wq(n + 3, (h + 3) % HEADS)
                    sp.wait_ge(k_ps, (it * QH + hd) * NC + NC)
                    load_wk(n, (h + 2) % HEADS)
                    if hd == 1:
                        sp.wait_ge(v_ps, it * 16 + 16)
                        load_wv((g + 1) % NG)
                    if type(g) is int and hd == 2:
                        for c in range(NC):
                            sp.wait_ge(cready, b * NC + NC + c)
                            load_ctx((b + 1) % nb, c)
                    sp.wait_ge(out_ps, it * QH + hd + 1)
                    load_wo(n + 1, (h + 1) % HEADS)
            load_wo(0, 0)
            loops(sp, quad)

        @block.tensor
        def _(pe):
            top["ln_transposes"](pe, ln, ps, nb)
            pe.wait_ge(init, 4)
            pe.sem_inc(pv_done, 1)
            for half in range(2):
                pe.matmul(psO[half * DH:half * DH + DH, 0:ROWS], V[:, 31, 3 * DH:4 * DH], PR[:, 1, 0:ROWS],
                          start=True, stop=False, skip_group_check=True)

            def split_product(out, stationary, moving):
                for i, (w, c) in enumerate([(0, 0), (0, 1), (2, 0), (1, 2), (3, 2)]):
                    mm = pe.matmul(out, stationary(w, c), moving(w, c), start=(i == 0), stop=(i == 4))
                return mm

            def project_q(n, row0):
                for t in range(2):
                    mm = pe.matmul(psM[:, 0:ROWS], wq[:, n % 2, t, :], xnT[:, t, bass.ds(row0, ROWS)],
                                   start=(t == 0), stop=(t == 1))
                mm.then_inc(q_ps, 1)

            def project_k(n, c):
                split_product(psK, lambda w, _: wk[:, n % 2, w, :], lambda _, k: C[:, k, c * CH:c * CH + CH]).then_inc(k_ps, 1)

            def guess(n, slot):
                for t in range(RT):
                    pe.matmul(psA[:, t, :], Q1[:, n % QH, t * P:t * P + P], KH[:, slot, :],
                              start=True, stop=True).then_inc(a_ps, 1)

            def project_v(u):
                for k in range(2):
                    t = 2 * u + k
                    mm = split_product(psV[:, k * 256:k * 256 + 256], lambda _, c: C[:, c, t * P:t * P + P],
                                       lambda w, _: wv[:, w, :])
                mm.then_inc(v_ps, 1)

            def scores(n, slot):
                for k in range(KT):
                    out = psS[:, k // 2, (k % 2) * ROWS:(k % 2) * ROWS + ROWS]
                    pe.matmul(out, KH[:, slot, k * P:k * P + P], Q1[:, n % QH, :], start=True, stop=False)
                    mm = pe.matmul(out, KL[0:M2, slot, k * P:k * P + P], Q2[0:M2, n % QH, :], start=False, stop=True)
                mm.then_inc(s_ps, 1)

            def weighted_sum(hd, c):
                for k in range(KT):
                    half = k % 2
                    mm = pe.matmul(psO[half * DH:half * DH + DH, 0:ROWS], V[:, c * KT + k, hd * DH:hd * DH + DH],
                                   PR[:, c % 2, k * ROWS:k * ROWS + ROWS],
                                   start=(c == 0 and k < 2), stop=(c == NC - 1 and k >= 2), skip_group_check=True)
                mm.then_inc(pv_done, 1)

            def row_sums(par):
                for t in range(RT):
                    mm = pe.matmul(psM[:, t:t + 1], accf[:, par, t * P:t * P + P], top["ones"][:, 0:1], start=True, stop=True)
                mm.then_inc(l_ps, 1)

            def project_out(par):
                for t in range(RT):
                    mm = pe.matmul(psM[:, t * DM:t * DM + DM], Ot[:, par, t * P:t * P + P], wo[:, par, :], start=True, stop=True)
                mm.then_inc(out_ps, 1)

            def max_rows():
                for t in range(RT):
                    mm = pe.matmul(psM[MROW:MROW + 1, t * P:t * P + P], nmx[:, t:t + 1], ident[:, :], start=True, stop=True)
                mm.then_inc(m_ps, 1)

            pe.wait_ge(cready, NC)
            pe.wait_ge(wv_in, 16)
            for u in range(7):
                if u > 0:
                    pe.wait_ge(v_sb, u)
                project_v(u)
            for n in range(2):
                pe.wait_ge(wq_in[n], 16)
                if n > 0:
                    pe.wait_ge(q_sb, n)
                project_q(n, 0)
            for j in range(LEAD):
                if j % NC == 0:
                    pe.wait_ge(wk_in[j // NC], 16)
                if j > 0:
                    pe.wait_ge(k_lo, j)
                project_k(j // NC, j % NC)
                if j > 0:
                    a = j - 1
                    pe.wait_ge(k_hi, a + 1)
                    if a == 0 or a == NC:
                        pe.wait_ge(q_ready, 1 + a // NC)
                    if a > 0:
                        pe.wait_ge(a_max, 2 * a)
                    guess(a // NC, a % SLOTS)
            pe.wait_ge(m_ready, 1)
            pe.wait_ge(q_sb, 2)
            max_rows()

            def quad(it, b, g):
                head0 = it * QH
                for s in range(STEPS):
                    hd, c = s // NC, s % NC
                    G = it * STEPS + s
                    pe.wait_ge(k_lo, G + 1)
                    pe.wait_ge(p_ready, G + 1)
                    if c == 0:
                        pe.wait_ge(m_row, head0 + hd + 1)
                    scores(hd, s % SLOTS)
                    for before, table in ((False, V_OWN), (True, V_BEFORE)):
                        if (s, 1) in table:
                            u = table[s, 1]
                            pe.wait_ge(v_sb, (it + before) * 16 + u)
                            project_v(u)
                    j = s + LEAD
                    if j % NC == 0:
                        pe.wait_ge(wk_in[(j // NC) % 2], (it * 2 + j // NC // 2) * 16 + 16)
                    if type(g) is int and STEPS <= j < STEPS + NC:
                        pe.wait_ge(cready, b * NC + NC + j - STEPS + 1)
                    pe.wait_ge(k_lo, G + LEAD)
                    project_k(j // NC, j % NC)
                    a = j - 1
                    pe.wait_ge(k_hi, G + LEAD)
                    if a % NC == 0:
                        pe.wait_ge(q_ready, head0 + a // NC + 1)
                    pe.wait_ge(a_max, 2 * (G + LEAD - 1))
                    guess(a // NC, a % SLOTS)
                    if c == NC - 1:
                        pe.wait_ge(m_ready, head0 + hd + 2)
                        pe.wait_ge(q_sb, head0 + hd + 3)
                        max_rows()
                    pe.wait_ge(p_ready, G + 1)
                    if c == 1:
                        pe.wait_ge(o_sb, head0 + hd + 1)
                    if 1 <= s <= NC:
                        pe.wait_ge(v_sb, it * 16 + 2 * s)
                    weighted_sum((s - 1) // NC % QH, (s - 1) % NC)
                    for before, table in ((False, V_OWN), (True, V_BEFORE)):
                        if (s, 0) in table:
                            u = table[s, 0]
                            if u == 0:
                                pe.wait_ge(wv_in, (it + 1) * 16 + 16)
                            pe.wait_ge(v_sb, (it + before) * 16 + u)
                            project_v(u)
                    if c == 2:
                        pe.wait_ge(fold_done, 2 * (head0 + hd) + 2)
                        pe.wait_ge(m_row, head0 + hd + 1)
                        row_sums((hd + 1) % 2)
                    if c == 3:
                        pe.wait_ge(rl_ready, head0 + hd + 1)
                        if hd % 2 == 0:
                            pe.wait_ge(wo_in[1], (it * 2 + hd // 2) * 16 + 16)
                        else:
                            pe.wait_ge(wo_in[0], (it * 2 + hd // 2) * 16 + 16)
                        project_out((hd + 1) % 2)
                    if c == 4:
                        n = hd + 2
                        pe.wait_ge(wq_in[n % 2], (it * 2 + n // 2) * 16 + 16)
                        pe.wait_ge(x_added, 2 * (head0 + hd) + 2)
                        nextb = (b + 1) % nb if type(g) is int and hd >= 2 else b
                        project_q(n, nextb * ROWS)

            loops(pe, quad)
            last = nb * NG * STEPS
            heads = nb * HEADS
            pe.wait_ge(p_ready, last + 1)
            weighted_sum(QH - 1, NC - 1)
            pe.wait_ge(fold_done, 2 * heads + 2)
            pe.wait_ge(m_row, heads + 1)
            row_sums(1)
            pe.wait_ge(rl_ready, heads + 1)
            pe.wait_ge(wo_in[1], (nb * NG * 2) * 16 + 16)
            pe.wait_ge(o_sb, heads + 1)
            project_out(1)

        @block.scalar
        def _(act):
            act.wait_ge(wraw_in, 32)
            raw = V[:, :, :].rearrange("p t n -> p (t n)")
            act.activation(KH[:, 0:8, :].rearrange("p s n -> p (s n)"), raw[:, 0:4096], ACT.Copy).then_inc(whi, 1)
            act.activation(KL[:, 0:4, :].rearrange("p s n -> p (s n)"), raw[:, 4096:6144], ACT.Copy).then_inc(whi, 1)
            top["ln_sqrt"](act, ln)
            top["ln_copies"](act, ln, ps, xnT, nb)

            def context_hi(c):
                act.activation(C[:, 0:3:2, c * CH:c * CH + CH], craw[:], ACT.Copy).then_inc(chi, 1)

            def keys_hi(slot):
                act.activation(KH[:, slot, :], psK, ACT.Copy).then_inc(k_hi, 1)

            def scale_q():
                act.activation(qs[:], psM[:, 0:ROWS], ACT.Copy, scale=float(DH) ** -0.5).then_inc(q_sb, 1)

            def max_row(n):
                act.activation(Q2[MROW:MROW + 1, n % QH, :], psM[MROW:MROW + 1, 0:ROWS], ACT.Copy).then_inc(m_row, 1)

            for c in range(NC):
                act.wait_ge(craw_in, 16 * c + 16)
                context_hi(c)
            act.wait_ge(q_ps, 1)
            scale_q()
            act.wait_ge(q_ps, 2)
            act.wait_ge(q_ready, 1)
            scale_q()
            for j in range(LEAD):
                act.wait_ge(k_ps, j + 1)
                keys_hi(j)
            act.wait_ge(m_ps, 1)
            max_row(0)
            act.wait_ge(init, 4)
            act.sem_inc(p_ready, 1)

            def quad(it, b, g):
                head0 = it * QH
                for s in range(STEPS):
                    hd, c = s // NC, s % NC
                    G = it * STEPS + s
                    act.wait_ge(s_ps, G + 1)
                    act.wait_ge(pv_done, G + 1)
                    pool = {0: 6, 1: 7, 2: 8, 3: 8}.get(c, 7 + c - 2)
                    act.wait_ge(acc_done, 7 * (head0 + hd) + pool)
                    act.activation(PR[:, s % 2, :], psS.rearrange("p a n -> p (a n)"), ACT.Exp).then_inc(p_ready, 1)
                    act.wait_ge(k_ps, G + LEAD + 1)
                    keys_hi((s + LEAD) % SLOTS)
                    if c == 0:
                        act.wait_ge(pv_done, G + 2)
                        act.wait_ge(out_ps, head0 + hd + 0) if hd else None
                        act.activation(Ot[:, (hd + 1) % 2, :], psO[:, 0:ROWS], ACT.Copy).then_inc(o_sb, 1)
                    if c == 4:
                        act.wait_ge(q_ps, head0 + hd + 3)
                        act.wait_ge(q_ready, head0 + hd + 2)
                        scale_q()
                    if c == NC - 1:
                        act.wait_ge(m_ps, head0 + hd + 2)
                        max_row(hd + 1)
                    if type(g) is int and 17 <= s < 17 + NC:
                        k = s - 17
                        act.wait_ge(craw_in, (b * NC + NC + k) * 16 + 16)
                        context_hi(k)

            loops(act, quad)
            act.wait_ge(pv_done, nb * NG * STEPS + 2)
            act.activation(Ot[:, 1, :], psO[:, 0:ROWS], ACT.Copy).then_inc(o_sb, 1)

        @block.vector
        def _(dve):
            dve.memset(top["ones"][:], 1.0)
            dve.memset(accf[:, 1, :], 1.0)
            dve.memset(Q2[MROW:M2, :, :].bitcast(F32), 0.0).then_inc(init, 1)
            raw = V[:, :, :].rearrange("p t n -> p (t n)")
            kh = KH[:, :, :].rearrange("p s n -> p (s n)")
            kl = KL[:, :, :].rearrange("p s n -> p (s n)")
            dve.wait_ge(whi, 1)
            dve.tensor_tensor(kh[:, 4096:8192], raw[:, 0:4096], kh[:, 0:4096].bitcast(F32), ALU.subtract).then_inc(wlo, 1)
            dve.wait_ge(whi, 2)
            dve.tensor_tensor(kl[:, 2048:4096], raw[:, 4096:6144], kl[:, 0:2048].bitcast(F32), ALU.subtract).then_inc(wlo, 1)
            dve.wait_ge(x_in, 64)
            top["ln_vector"](dve, ln, nb)
            dve.tensor_tensor(x1[:, RT:, :], xin, top["bo"][:, :].unsqueeze(1).to_broadcast([P, nb * RT, DM]), ALU.add).then_inc(init, 1)
            dve.memset(x1[:, 0:RT, :], 0.0)
            dve.wait_ge(init, 2)
            dve.memset(PR[:, 1, :], 0.0)
            dve.wait_ge(wlo, 2)
            dve.memset(V[:, 28:32, :], 0.0).then_inc(init, 1)
            dve.wait_ge(wst, 128)
            dve.memset(KL[MROW:M2, :, :].bitcast(F32), 0.0).then_inc(init, 1)
            dve.wait_ge(init, 4)
            dve.memset(KL[MROW:MROW + 1, :, :].bitcast(F32), 1.0).then_inc(init, 1)

            def context_lo(c):
                k = slice(c * CH, c * CH + CH)
                dve.tensor_tensor(C[:, 1, k], craw[:, 0, :], C[:, 0, k].bitcast(F32), ALU.subtract)
                dve.tensor_tensor(C[DH:, 2, k], craw[DH:, 1, :], C[DH:, 2, k].bitcast(F32), ALU.subtract).then_inc(cready, 1)

            def keys_lo(slot):
                dve.tensor_tensor(KL[0:DH, slot, :], psK[0:DH], KH[0:DH, slot, :].bitcast(F32), ALU.subtract).then_inc(k_lo, 1)

            def chunk_max(c, t):
                dve.tensor_reduce(amx[:, t, c:c + 1], psA[:, t, :], AX.X, ALU.max).then_inc(a_max, 1)

            def negate_max():
                dve.tensor_reduce(nmx[:, :], amx[:, :, :], AX.X, ALU.max, negate=True).then_inc(m_ready, 1)

            def copy_v(u):
                dve.tensor_copy(V[:, 2 * u:2 * u + 2, :].rearrange("p t n -> p (t n)"), psV).then_inc(v_sb, 1)

            def split_q(n, before):
                dve.tensor_copy(Q1[:, n % QH, :], qs[:]).then_inc(q_hi, 1)
                dve.tensor_copy(Q2[0:DH, n % QH, :], qs[0:DH, :])
                dve.wait_ge(q_hi, before + 1)
                dve.tensor_tensor(Q1[DH:, n % QH, :], qs[DH:, :], Q1[DH:, n % QH, :].bitcast(F32), ALU.subtract).then_inc(q_ready, 1)

            for c in range(NC):
                dve.wait_ge(chi, c + 1)
                context_lo(c)
            for u in range(7):
                dve.wait_ge(v_ps, u + 1)
                copy_v(u)
            for n in range(2):
                dve.wait_ge(q_sb, n + 1)
                split_q(n, n)
            for j in range(LEAD):
                dve.wait_ge(k_hi, j + 1)
                keys_lo(j)
                if j > 0:
                    for t in range(RT):
                        if j == LEAD - 1:
                            dve.wait_ge(m_ready, 1)
                        dve.wait_ge(a_ps, 2 * j - 1 + t)
                        chunk_max((j - 1) % NC, t)
                if j == NC:
                    dve.wait_ge(a_max, 2 * NC)
                    negate_max()

            def quad(it, b, g):
                head0 = it * QH
                for s in range(STEPS):
                    hd, c = s // NC, s % NC
                    G = it * STEPS + s
                    for before, table in ((False, V_OWN), (True, V_BEFORE)):
                        if (s, 1) in table:
                            u = table[s, 1]
                            dve.wait_ge(v_ps, (it + before) * 16 + u + 1)
                            copy_v(u)
                    dve.wait_ge(k_hi, G + LEAD + 1)
                    keys_lo((s + LEAD) % SLOTS)
                    a = (s + LEAD - 1) % NC
                    if a == 0:
                        dve.wait_ge(m_ready, head0 + (s + LEAD - 1) // NC)
                    for t in range(RT):
                        dve.wait_ge(a_ps, 2 * (G + LEAD - 1) + t + 1)
                        chunk_max(a, t)
                    if a == NC - 1:
                        dve.wait_ge(a_max, 2 * (G + LEAD))
                        dve.wait_ge(m_ps, head0 + hd + 1)
                        negate_max()
                    for before, table in ((False, V_OWN), (True, V_BEFORE)):
                        if (s, 0) in table:
                            u = table[s, 0]
                            dve.wait_ge(v_ps, (it + before) * 16 + u + 1)
                            copy_v(u)
                    if c == 2:
                        dve.wait_ge(l_ps, head0 + hd + 1)
                        dve.wait_ge(x_added, 2 * (head0 + hd)) if hd else None
                        dve.reciprocal(rl[:, :], psM[:, 0:RT]).then_inc(rl_ready, 1)
                    if c == 3:
                        dve.wait_ge(out_ps, head0 + hd + 1)
                        dve.wait_ge(rl_ready, head0 + hd + 1)
                        add_rows((head0 + hd + HEADS - 1) // HEADS)
                    if c == 4:
                        dve.wait_ge(q_sb, head0 + hd + 3)
                        split_q(hd + 2, head0 + hd + 2)
                    if type(g) is int and 17 <= s < 17 + NC:
                        k = s - 17
                        dve.wait_ge(chi, b * NC + NC + k + 1)
                        context_lo(k)

            def add_rows(slot):
                for t in range(RT):
                    row = x1[:, bass.ds(slot * RT + t, 1), :].rearrange("p o n -> p (o n)")
                    dve.scalar_tensor_tensor(out=row, in0=psM[:, t * DM:t * DM + DM], scalar=rl[:, t:t + 1], in1=row,
                                             op0=ALU.mult, op1=ALU.add).then_inc(x_added, 1)

            loops(dve, quad)
            heads = nb * HEADS
            dve.wait_ge(l_ps, heads + 1)
            dve.wait_ge(x_added, 2 * heads)
            dve.reciprocal(rl[:, :], psM[:, 0:RT]).then_inc(rl_ready, 1)
            dve.wait_ge(out_ps, heads + 1)
            dve.wait_ge(rl_ready, heads + 1)
            add_rows(nb)
            dve.wait_ge(x_added, 2 * heads + 2)

        @block.gpsimd
        def _(pool):
            pool.wait_ge(init, 4)
            pool.sem_inc(acc_done, 7)
            pool.sem_inc(fold_done, 2)

            def quad(it, b, g):
                head0 = it * QH
                for s in range(STEPS):
                    hd, c = s // NC, s % NC
                    G = it * STEPS + s
                    if c == 0:
                        continue
                    n = head0 + hd
                    pool.wait_ge(p_ready, G + 2)
                    if c == 1:
                        pool.wait_ge(fold_done, 2 * n + 2)
                        pool.tensor_tensor(acc[:], PR[:, 0, :], PR[:, 1, :], ALU.add).then_inc(acc_done, 1)
                    else:
                        pool.wait_ge(acc_done, 7 * n + 7 + c - 1)
                        pool.tensor_tensor(acc[:], acc[:], PR[:, c % 2, :], ALU.add).then_inc(acc_done, 1)
                    if c == NC - 1:
                        pool.wait_ge(acc_done, 7 * n + 14)
                        pool.tensor_tensor(acc[:, 0:512], acc[:, 0:512], acc[:, 512:1024], ALU.add).then_inc(fold_done, 1)
                        pool.wait_ge(fold_done, 2 * n + 3)
                        if hd:
                            pool.wait_ge(l_ps, n)
                        pool.tensor_tensor(accf[:, hd % 2, :], acc[:, 0:256], acc[:, 256:512], ALU.add).then_inc(fold_done, 1)

            loops(pool, quad)


def norm_sems(sem, name):
    return {k: sem(f"{name}_{k}") for k in ("stats", "mean", "var", "sqrt", "rstd", "normed", "t_ps", "t_sb")}


def norm_vector(dve, s, tiles, src, dst, st6, mv, rs, ready=None):
    for r in range(tiles):
        if ready:
            ready(r)
        dve.bn_stats(st6[:, r, :], src(r)).then_inc(s["stats"], 1)
    for r in range(tiles):
        dve.wait_ge(s["stats"], r + 1)
        dve.bn_aggr(mv[:, r, :], st6[:, r, :]).then_inc(s["mean"], 1)
    dve.wait_ge(s["mean"], tiles)
    dve.tensor_scalar(rs[:], mv[:, :, 1], EPS, None, ALU.add).then_inc(s["var"], 1)
    dve.wait_ge(s["sqrt"], 1)
    dve.reciprocal(rs[:], rs[:]).then_inc(s["rstd"], 1)
    dve.wait_ge(s["rstd"], 1)
    for r in range(tiles):
        dve.tensor_scalar(dst(r), src(r), mv[:, r, 0:1], rs[:, r:r + 1], ALU.subtract, ALU.mult).then_inc(s["normed"], 1)


def norm_sqrt(act, s, rs):
    act.wait_ge(s["var"], 1)
    act.activation(rs[:], rs[:], ACT.Sqrt).then_inc(s["sqrt"], 1)


def transpose_rows(pe, s, tiles, src, bank, ident):
    for r in range(tiles):
        pe.wait_ge(s["normed"], r + 1)
        if r >= 4:
            pe.wait_ge(s["t_sb"], r - 3)
        for t in range(2):
            mm = pe.transpose(bank(r)[:, t * P:t * P + P], src(r)[:, t * P:t * P + P], ident[:, :])
        mm.then_inc(s["t_ps"], 1)


def copy_rows(act, s, tiles, bank, dst):
    for r in range(tiles):
        act.wait_ge(s["t_ps"], r + 1)
        act.activation(dst[:, :, r * P:r * P + P], bank(r)[:, 0:2 * P].rearrange("p (t n) -> p t n", t=2), ACT.Copy).then_inc(s["t_sb"], 1)


def recurrence(nc, nb, top, d):
    x1, ident = top["x1"], top["ident"]
    NR = nb * RT
    N = nb * ROWS
    HALVES = max(1, N // 512)
    W = N // HALVES
    G = 2
    ctx = ExitStack()
    with ctx:
        def sb(name, shape, dt=F32):
            return ctx.enter_context(nc.sbuf_tensor(name, shape, dt))

        def sem(name):
            return ctx.enter_context(nc.semaphore(name))

        u = sb("u", [P, NR, DM])
        uT = sb("uT", [P, 2, N])
        w6 = sb("w6", [P, 6, 2, DM])
        bd = sb("bd", [P, 2, G, P])
        rope = sb("rope", [P, 2, W])
        gb = sb("gb", [P, G])
        dl = sb("dl", [P, G])
        dec = sb("dec", [P, G])
        seq = sb("seq", [P, N])
        dect = sb("dect", [P, G, N])
        selv = sb("selv", [P, 16, P])
        selvr = sb("selvr", [P, 16, P], F32R)
        sely = sb("sely", [P, 4, 32])
        ow = sb("ow", [P, G, DM])
        vecs = sb("vecs", [P, 3, DM])
        t1 = sb("t1", [P, 2, W])
        t2 = sb("t2", [P, 2, W])
        rot = sb("rot", [P, 2, W])
        qr = sb("qr", [P, G, N])
        gate = sb("gate", [P, 2, W])
        kk = sb("kk", [P, G, N])
        vh = sb("vh", [P, G, N], F32R)
        vl = sb("vl", [P, G, N], F32R)
        kv = sb("kv", [P, 2, N])
        M = sb("M", [P, 2, N])
        qm = sb("qm", [P, 2, N])
        yT = sb("yT", [P, G, N])
        st6, mv, rs = sb("st6b", [P, NR, 6]), sb("mvb", [P, NR, 2]), sb("rsb", [P, NR])
        st6c, mvc, rsc = sb("st6c", [P, NR, 6]), sb("mvc", [P, NR, 2]), sb("rsc", [P, NR])
        ps = ctx.enter_context(nc.psum_tensor("ps2", [P, 8, 512], F32))

        w_in = [sem(f"w6_in{i}") for i in range(4)]
        ln = norm_sems(sem, "n2")
        lo = norm_sems(sem, "n3")
        pr_ps = sem("pr_ps")
        ropes, rot_ready, r_ps, qr_ready, gate_ready, kk_ready = (sem(x) for x in ("ropes", "rot_ready", "r_ps", "qr_ready", "gate_ready", "kk_ready"))
        vhi, vlo, dec_ready, dect_ready, selr = sem("vhi"), sem("vlo"), sem("dec_ready"), sem("dect_ready"), sem("selr")
        v_ps, kv_ready, m_done, qm_ready, y_ps, y_sb = (sem(x) for x in ("vb_ps", "kv_ready", "m_done", "qm_ready", "y_ps", "y_sb"))
        o_ps, h_ready, scaled, fin = sem("o_ps"), sem("h_ready"), sem("scaled"), sem("fin2")
        ub = sem("ub")
        pairs = [(g, hf) for g in range(G) for hf in range(HALVES)]
        NJ = len(pairs)
        cols = lambda hf: slice(hf * W, hf * W + W)
        block = ctx.enter_context(nc.Block())

        @block.sync
        def _(sp):
            sp.dma_start(w6[:], d["w6"]).then_inc(w_in[0], 16)
            sp.dma_start(rope[:], d["rope"][:, :, 0:W]).then_inc(w_in[1], 16)
            sp.dma_start(gb[:], d["gb"]).then_inc(w_in[1], 16)
            sp.dma_start(dl[:], d["dl"]).then_inc(w_in[1], 16)
            sp.dma_start(seq[:], d["seq"][:, 0:N]).then_inc(w_in[1], 16)
            sp.dma_start(bd[:], d["bd"]).then_inc(w_in[1], 16)
            sp.dma_start(selv[:], d["selv"]).then_inc(w_in[2], 16)
            sp.dma_start(sely[:], d["sely"]).then_inc(w_in[2], 16)
            sp.dma_start(ow[:], d["ow"]).then_inc(w_in[3], 16)
            sp.dma_start(vecs[:], d["vecs"]).then_inc(w_in[3], 16)

        bank = lambda r: ps[:, 4 + r % 4, :]

        @block.tensor
        def _(pe):
            transpose_rows(pe, ln, NR, lambda r: u[:, r, :], bank, ident)
            pe.wait_ge(ln["t_sb"], NR)
            pe.wait_ge(w_in[0], 16)
            pe.wait_ge(w_in[1], 80)

            def project(i, g, hf, out):
                for t in range(2):
                    mm = pe.matmul(out, w6[:, i, t, g * P:g * P + P], uT[:, t, cols(hf)], start=(t == 0), stop=(t == 1))
                return mm
            for n, (g, hf) in enumerate(pairs):
                for i in range(2):
                    if n:
                        pe.wait_ge(ropes, 2 * (2 * (n - 1) + i) + 2)
                    project(2 * i, g, hf, ps[:, 2 * i, 0:W])
                    project(2 * i + 1, g, hf, ps[:, 2 * i + 1, 0:W]).then_inc(pr_ps, 1)
                if n:
                    pe.wait_ge(gate_ready, n)
                project(5, g, hf, ps[:, 5, 0:W]).then_inc(pr_ps, 1)
                if n:
                    pe.wait_ge(vlo, n)
                project(4, g, hf, ps[:, 4, 0:W]).then_inc(pr_ps, 1)
                for i in range(2):
                    pe.wait_ge(rot_ready, 2 * n + i + 1)
                    if n:
                        pe.wait_ge([qr_ready, kk_ready][i], n)
                    pe.matmul(ps[:, 6 + i, 0:W], bd[:, i, g, :], rot[:, i, :], start=True, stop=True).then_inc(r_ps, 1)
            pe.wait_ge(qr_ready, NJ)
            pe.wait_ge(kk_ready, NJ)
            pe.wait_ge(vlo, NJ)
            pe.wait_ge(selr, 1)

            def broadcast_v(j, g, dd):
                for hf in range(HALVES):
                    out = ps[:, 2 * (j % 2) + hf, 0:W]
                    pe.matmul(out, selvr[:, dd, :], vh[:, g, cols(hf)], start=True, stop=False)
                    mm = pe.matmul(out, selvr[:, dd, :], vl[:, g, cols(hf)], start=False, stop=True)
                mm.then_inc(v_ps, 1)

            def sum_r(j, g, dd):
                k, e = dd // 4, dd % 4
                for hf in range(HALVES):
                    mm = pe.matmul(ps[32 * k:32 * k + 32, 4 + 2 * g + hf, 0:W], sely[:, e, :], qm[:, j % 2, cols(hf)],
                                   start=(e == 0), stop=(e == 3), skip_group_check=True)
                mm.then_inc(y_ps, 1)

            steps = [(g, dd) for g in range(G) for dd in range(16)]
            for j, (g, dd) in enumerate(steps):
                if j >= 2:
                    pe.wait_ge(kv_ready, j - 1)
                broadcast_v(j, g, dd)
                if j >= 2:
                    pe.wait_ge(qm_ready, j - 1)
                    sum_r(j - 2, *steps[j - 2])
            for j in range(30, 32):
                pe.wait_ge(qm_ready, j + 1)
                sum_r(j, *steps[j])
            pe.wait_ge(y_sb, G)
            pe.wait_ge(w_in[3], 32)
            for r in range(NR):
                if r >= 4:
                    pe.wait_ge(h_ready, r - 3)
                for g in range(G):
                    mm = pe.matmul(ps[:, r % 4, 0:DM], yT[:, g, r * P:r * P + P], ow[:, g, :], start=(g == 0), stop=(g == 1))
                mm.then_inc(o_ps, 1)

        @block.scalar
        def _(act):
            norm_sqrt(act, ln, rs)
            copy_rows(act, ln, NR, bank, uT)
            act.wait_ge(w_in[1], 80)
            act.activation(dec[:], dl[:], ACT.Sigmoid).then_inc(dec_ready, 1)
            act.wait_ge(w_in[2], 32)
            act.activation(selvr[:, :, :], selv[:, :, :], ACT.Copy).then_inc(selr, 1)
            for n, (g, hf) in enumerate(pairs):
                act.wait_ge(pr_ps, 4 * n + 3)
                if n >= 2:
                    act.wait_ge(kk_ready, n - 1)
                act.activation(gate[:, n % 2, :], ps[:, 5, 0:W], ACT.Sigmoid, bias=gb[:, g:g + 1]).then_inc(gate_ready, 1)
                act.wait_ge(pr_ps, 4 * n + 4)
                act.activation(vh[:, g, cols(hf)], ps[:, 4, 0:W], ACT.Copy).then_inc(vhi, 1)
                act.wait_ge(r_ps, 2 * n + 1)
                act.activation(qr[:, g, cols(hf)], ps[:, 6, 0:W], ACT.Copy).then_inc(qr_ready, 1)
            for g in range(G):
                act.wait_ge(y_ps, 16 * g + 16)
                act.activation(yT[:, g, :].rearrange("p (a n) -> p a n", a=HALVES), ps[:, 4 + 2 * g:4 + 2 * g + HALVES, 0:W], ACT.Copy).then_inc(y_sb, 1)
            norm_sqrt(act, lo, rsc)

        @block.vector
        def _(dve):
            norm_vector(dve, ln, NR, lambda r: x1[:, RT + r, :], lambda r: u[:, r, :], st6, mv, rs)
            dve.wait_ge(w_in[1], 80)
            dve.wait_ge(dec_ready, 1)
            for g in range(G):
                dve.tensor_scalar(dect[:, g, :], seq[:, :], dec[:, g:g + 1], None, ALU.mult).then_inc(dect_ready, 1)
            for n, (g, hf) in enumerate(pairs):
                for i in range(2):
                    dve.wait_ge(pr_ps, 4 * n + i + 1)
                    if n:
                        dve.wait_ge(rot_ready, 2 * (n - 1) + i + 1)
                    dve.tensor_tensor(t1[:, i, :], ps[:, 2 * i, 0:W], rope[:, 0, :], ALU.mult).then_inc(ropes, 1)
                    dve.tensor_tensor(t2[:, i, :], ps[:, 2 * i + 1, 0:W], rope[:, 1, :], ALU.mult).then_inc(ropes, 1)
                dve.wait_ge(vhi, n + 1)
                dve.tensor_tensor(vl[:, g, cols(hf)], ps[:, 4, 0:W], vh[:, g, cols(hf)].bitcast(F32), ALU.subtract).then_inc(vlo, 1)
                dve.wait_ge(r_ps, 2 * n + 2)
                dve.wait_ge(gate_ready, n + 1)
                dve.scalar_tensor_tensor(out=kk[:, g, cols(hf)], in0=ps[:, 7, 0:W], scalar=0.25, in1=gate[:, n % 2, :],
                                         op0=ALU.mult, op1=ALU.mult).then_inc(kk_ready, 1)
            dve.wait_ge(kk_ready, NJ)
            dve.wait_ge(dect_ready, G)
            for j in range(32):
                g = j // 16
                if j >= 2:
                    dve.wait_ge(m_done, j - 1)
                dve.wait_ge(v_ps, j + 1)
                dve.tensor_tensor(kv[:, j % 2, :].rearrange("p (a n) -> p a n", a=HALVES), ps[:, 2 * (j % 2):2 * (j % 2) + HALVES, 0:W],
                                  kk[:, g, :].rearrange("p (a n) -> p a n", a=HALVES), ALU.mult).then_inc(kv_ready, 1)
                dve.wait_ge(kv_ready, j + 1)
                if j >= 2:
                    dve.wait_ge(qm_ready, j - 1)
                dve.tensor_tensor_scan(M[:, j % 2, :], dect[:, g, :], kv[:, j % 2, :], 0.0, ALU.mult, ALU.add).then_inc(m_done, 1)
            dve.wait_ge(ub, 1)
            for r in range(NR):
                dve.wait_ge(o_ps, r + 1)
                dve.tensor_tensor(u[:, r, :], ps[:, r % 4, 0:DM], u[:, r, :], ALU.add).then_inc(h_ready, 1)
            norm_vector(dve, lo, NR, lambda r: u[:, r, :], lambda r: u[:, r, :], st6c, mvc, rsc, ready=lambda r: dve.wait_ge(h_ready, r + 1))
            dve.wait_ge(lo["normed"], NR)
            dve.tensor_tensor(u[:, :, :], u[:, :, :], vecs[:, 1, :].unsqueeze(1).to_broadcast([P, NR, DM]), ALU.mult).then_inc(scaled, 1)
            dve.wait_ge(scaled, 1)
            dve.wait_ge(fin, 1)
            dve.tensor_tensor(x1[:, RT:, :], u[:, :, :], x1[:, RT:, :], ALU.add).then_inc(fin, 1)
            dve.wait_ge(fin, 2)

        @block.gpsimd
        def _(pool):
            for j in range(2 * NJ):
                pool.wait_ge(ropes, 2 * j + 2)
                if j >= 2:
                    pool.wait_ge(r_ps, j - 1)
                pool.tensor_tensor(rot[:, j % 2, :], t1[:, j % 2, :], t2[:, j % 2, :], ALU.add).then_inc(rot_ready, 1)
            pool.wait_ge(qr_ready, NJ)
            for j in range(32):
                pool.wait_ge(m_done, j + 1)
                if j >= 2:
                    pool.wait_ge(y_ps, j - 1)
                pool.tensor_tensor(qm[:, j % 2, :], M[:, j % 2, :], qr[:, j // 16, :], ALU.mult).then_inc(qm_ready, 1)
            pool.wait_ge(w_in[3], 32)
            pool.tensor_tensor(u[:, :, :], u[:, :, :], vecs[:, 0, :].unsqueeze(1).to_broadcast([P, NR, DM]), ALU.add).then_inc(ub, 1)
            pool.tensor_tensor(x1[:, RT:, :], x1[:, RT:, :], vecs[:, 2, :].unsqueeze(1).to_broadcast([P, NR, DM]), ALU.add).then_inc(fin, 1)


def experts(nc, nb, top, d, out):
    x2, ident = top["x1"], top["ident"]
    NR = nb * RT
    N = nb * ROWS
    HALVES = max(1, N // 512)
    W = N // HALVES
    E = 8
    ctx = ExitStack()
    with ctx:
        def sb(name, shape, dt=F32):
            return ctx.enter_context(nc.sbuf_tensor(name, shape, dt))

        def sem(name):
            return ctx.enter_context(nc.semaphore(name))

        w = sb("w", [P, NR, DM])
        wT = sb("wT", [P, 2, N])
        gw = sb("gw", [P, 2, E])
        sw12 = sb("sw12", [P, 2, 2, 512])
        sw3 = sb("sw3", [P, 4, DM])
        we = sb("we", [P, 2, 3, 2, DM])
        be = sb("be", [P, 2, 3, 2])
        lg = sb("lg", [P, NR, E])
        mx = sb("mx", [P, NR])
        sm = sb("sm", [P, NR])
        iota = sb("iota", [P, E])
        cand = sb("cand", [P, NR, E])
        sc2 = sb("sc2", [P, NR, E])
        hot = sb("hot", [P, NR, E])
        wm = sb("wm", [P, NR, 2 * E])
        wmT = sb("wmT", [2 * E, N])
        bc = sb("bc", [P, 2, 2, N])
        t1 = sb("e_t1", [P, 2, N])
        hT = sb("hT", [P, 2, N])
        t3 = sb("e_t3", [P, 2, N])
        t3m = sb("e_t3m", [P, 2, N])
        yT = sb("y_T", [P, 2, N])
        zs = sb("zs", [P, 2, N])
        zT = sb("zT", [P, 4, N])
        st6, mv, rs = sb("st6d", [P, NR, 6]), sb("mvd", [P, NR, 2]), sb("rsd", [P, NR])
        ps = ctx.enter_context(nc.psum_tensor("ps3", [P, 8, 512], F32))
        g_in, s_in = sem("g_in"), sem("s_in")
        e_in = [sem(f"e_in{i}") for i in range(2)]
        bc_in = [sem(f"bc_in{i}") for i in range(2)]
        ln = norm_sems(sem, "n4")
        lg_ps, chain, ex, wm_ready, wm_ps, wm_sb, wm_out = (sem(x) for x in ("lg_ps", "chain", "ex", "wm_ready", "wm_ps", "wm_sb", "wm_out"))
        z_ps, z_silu, z_ready = sem("z_ps"), sem("z_silu"), sem("z_ready")
        h_ps, t1_ready, h_ready, x3_ps, t3_ready, t3m_ready, x2_ps, xy_ready, y_ready = (sem("e_" + x) for x in (
            "h_ps", "t1_ready", "h_ready", "x3_ps", "t3_ready", "t3m_ready", "x2_ps", "xy_ready", "y_ready"))
        f_ps, added, f_ready, done = sem("f_ps"), sem("x_z_added"), sem("f_ready"), sem("done3")
        bank = lambda r: ps[:, 4 + r % 4, :]
        jobs = [(m, hf) for m in range(2) for hf in range(HALVES)]
        NJ = len(jobs)
        cols = lambda hf: slice(hf * W, hf * W + W)
        block = ctx.enter_context(nc.Block())

        @block.sync
        def _(sp):
            sp.dma_start(gw[:], d["gw"]).then_inc(g_in, 16)
            sp.dma_start(iota[:], d["iota"]).then_inc(g_in, 16)
            sp.dma_start(sw12[:], d["sw12"]).then_inc(s_in, 16)
            sp.dma_start(sw3[:], d["sw3"]).then_inc(s_in, 16)
            for e in range(2):
                sp.dma_start(we[:, e, :, :, :], d["we"][e]).then_inc(e_in[e], 16)
                sp.dma_start(be[:, e, :, :], d["be"][e]).then_inc(e_in[e], 16)
            sp.wait_ge(wm_sb, NR)
            sp.dma_start(d["wm_rows"][:, 0:N], wmT[:, :]).then_inc(wm_out, 16)
            sp.wait_ge(wm_out, 16)

            def load_bc(slot, e):
                for k in range(2):
                    sp.dma_start(bc[:, slot, k, :], d["wm_rows"][bass.ds(e + k * E, 1), 0:N].to_broadcast([P, N])).then_inc(bc_in[slot], 16)

            for e in range(2):
                load_bc(e, e)
            with sp.Fori(0, E // 2 - 1) as i:
                for k in range(2):
                    sp.wait_ge(xy_ready, (i * 2 + k) * NJ + 2 * NJ)
                    sp.dma_start(we[:, k, :, :, :], d["we"][bass.ds(i * 2 + 2 + k, 1)].rearrange("o p a t n -> p (o a) t n")).then_inc(e_in[k], 16)
                    sp.dma_start(be[:, k, :, :], d["be"][bass.ds(i * 2 + 2 + k, 1)].rearrange("o p a m -> p (o a) m")).then_inc(e_in[k], 16)
                    load_bc(k, i * 2 + 2 + k)
            sp.wait_ge(f_ready, NR)
            sp.dma_start(out, w[:, :, :]).then_inc(done, 16)
            sp.wait_ge(done, 16)

        @block.tensor
        def _(pe):
            transpose_rows(pe, ln, NR, lambda r: w[:, r, :], bank, ident)
            pe.wait_ge(ln["t_sb"], NR)
            pe.wait_ge(g_in, 32)
            for r in range(NR):
                for t in range(2):
                    mm = pe.matmul(ps[:, 0, r * E:r * E + E], wT[:, t, r * P:r * P + P], gw[:, t, :], start=(t == 0), stop=(t == 1))
            mm.then_inc(lg_ps, 1)
            pe.wait_ge(s_in, 32)
            n = 0
            for m in range(4):
                for hf in range(HALVES):
                    if n >= 2:
                        pe.wait_ge(z_ready, n - 1)
                    for a in range(2):
                        for t in range(2):
                            mm = pe.matmul(ps[:, 1 + 2 * (n % 2) + a, 0:W], sw12[:, t, a, m * P:m * P + P], wT[:, t, cols(hf)],
                                           start=(t == 0), stop=(t == 1))
                    mm.then_inc(z_ps, 1)
                    n += 1
            pe.wait_ge(wm_ready, 1)
            for r in range(NR):
                if r >= 2:
                    pe.wait_ge(wm_sb, r - 1)
                pe.transpose(ps[0:2 * E, 6 + r % 2, 0:P], wm[:, r, :], ident[:, :]).then_inc(wm_ps, 1)
            pe.wait_ge(z_ready, 4 * HALVES)
            pe.wait_ge(wm_sb, NR)

            def layer(slot, a, src, m, hf, out):
                for t in range(2):
                    mm = pe.matmul(out, we[:, slot, a, t, m * P:m * P + P], src[:, t, cols(hf)], start=(t == 0), stop=(t == 1))
                return mm

            def expert(e, slot, first):
                pe.wait_ge(e_in[slot], first)
                base = e * NJ
                for n, (m, hf) in enumerate(jobs):
                    pe.wait_ge(t1_ready, base + n + 1)
                    layer(slot, 0, wT, m, hf, ps[:, n % 2, 0:W]).then_inc(h_ps, 1)
                    pe.wait_ge(t3_ready, base + n + 1)
                    layer(slot, 2, wT, m, hf, ps[:, 2 + n % 2, 0:W]).then_inc(x3_ps, 1)
                pe.wait_ge(h_ready, base + 2 * NJ)
                for n, (m, hf) in enumerate(jobs):
                    pe.wait_ge(xy_ready, base + n + 1)
                    layer(slot, 1, hT, m, hf, ps[:, 4 + n, 0:W]).then_inc(x2_ps, 1)

            pe.sem_inc(x2_ps, 1)
            with pe.Fori(0, E // 2) as i:
                for k in range(2):
                    expert(i * 2 + k, k, i * 32 + 32)
            pe.wait_ge(y_ready, NJ * E + NJ)
            for r in range(NR):
                if r >= 4:
                    pe.wait_ge(f_ready, r - 3)
                for t in range(4):
                    pe.matmul(ps[:, r % 4, 0:DM], zT[:, t, r * P:r * P + P], sw3[:, t, :], start=(t == 0), stop=(t == 3))
                for t in range(2):
                    mm = pe.transpose(ps[:, 4 + r % 4, t * P:t * P + P], yT[:, t, r * P:r * P + P], ident[:, :])
                mm.then_inc(f_ps, 1)

        @block.scalar
        def _(act):
            norm_sqrt(act, ln, rs)
            copy_rows(act, ln, NR, bank, wT)
            act.wait_ge(chain, 2)
            act.activation(lg[:, :, :], lg[:, :, :], ACT.Exp).then_inc(ex, 1)
            n = 0
            for m in range(4):
                for hf in range(HALVES):
                    act.wait_ge(z_ps, n + 1)
                    if n >= 2:
                        act.wait_ge(z_ready, n - 1)
                    act.activation(zs[:, n % 2, 0:W], ps[:, 1 + 2 * (n % 2), 0:W], ACT.Silu).then_inc(z_silu, 1)
                    n += 1
            for r in range(NR):
                act.wait_ge(wm_ps, r + 1)
                act.activation(wmT[:, r * P:r * P + P], ps[0:2 * E, 6 + r % 2, 0:P], ACT.Copy).then_inc(wm_sb, 1)
            act.sem_inc(h_ready, NJ)

            def expert(e, k, loads):
                act.wait_ge(e_in[k], loads)
                for n, (m, hf) in enumerate(jobs):
                    act.wait_ge(t1_ready, e * NJ + n + 3)
                    act.wait_ge(x2_ps, e * NJ + 1)
                    act.activation(hT[:, m, cols(hf)], t1[:, m, cols(hf)], ACT.Silu, bias=be[:, k, 0, m:m + 1]).then_inc(h_ready, 1)

            with act.Fori(0, E // 2) as i:
                for k in range(2):
                    expert(i * 2 + k, k, i * 32 + 32)

        @block.vector
        def _(dve):
            norm_vector(dve, ln, NR, lambda r: x2[:, RT + r, :], lambda r: w[:, r, :], st6, mv, rs)
            count = [0]

            def link(ins):
                count[0] += 1
                ins.then_inc(chain, 1)
                dve.wait_ge(chain, count[0])

            rows = lambda t: t[:, :].unsqueeze(2).to_broadcast([P, NR, E])
            dve.wait_ge(lg_ps, 1)
            logits = ps[:, 0, 0:NR * E].rearrange("p (r e) -> p r e", e=E)
            link(dve.tensor_reduce(mx[:, :], logits, AX.X, ALU.max))
            link(dve.tensor_tensor(lg[:, :, :], logits, rows(mx), ALU.subtract))
            dve.wait_ge(ex, 1)
            link(dve.tensor_reduce(sm[:, :], lg[:, :, :], AX.X, ALU.add))
            link(dve.reciprocal(sm[:, :], sm[:, :]))
            link(dve.tensor_tensor(lg[:, :, :], lg[:, :, :], rows(sm), ALU.mult))
            order = iota[:, :].unsqueeze(1).to_broadcast([P, NR, E])
            score = lg
            for k in range(2):
                link(dve.tensor_reduce(mx[:, :], score[:, :, :], AX.X, ALU.max))
                link(dve.tensor_tensor(hot[:, :, :], score[:, :, :], rows(mx), ALU.is_ge))
                link(dve.scalar_tensor_tensor(out=cand[:, :, :], in0=hot[:, :, :], scalar=-float(E), in1=order, op0=ALU.mult, op1=ALU.add))
                link(dve.tensor_reduce(mx[:, :], cand[:, :, :], AX.X, ALU.min))
                one = wm[:, :, E:2 * E] if k == 0 else hot[:, :, :]
                link(dve.tensor_tensor(one, cand[:, :, :], rows(mx), ALU.is_equal))
                if k == 0:
                    link(dve.scalar_tensor_tensor(out=sc2[:, :, :], in0=one, scalar=-4.0, in1=lg[:, :, :], op0=ALU.mult, op1=ALU.add))
                    score = sc2
            link(dve.tensor_tensor(wm[:, :, E:2 * E], wm[:, :, E:2 * E], hot[:, :, :], ALU.add))
            dve.tensor_tensor(wm[:, :, 0:E], wm[:, :, E:2 * E], lg[:, :, :], ALU.mult).then_inc(wm_ready, 1)
            n = 0
            for m in range(4):
                for hf in range(HALVES):
                    dve.wait_ge(z_silu, n + 1)
                    dve.tensor_tensor(zT[:, m, cols(hf)], ps[:, 2 + 2 * (n % 2), 0:W], zs[:, n % 2, 0:W], ALU.mult).then_inc(z_ready, 1)
                    n += 1
            dve.memset(yT[:, :, :], 0.0).then_inc(t1_ready, 2)
            dve.sem_inc(t3_ready, 2)
            dve.sem_inc(t3m_ready, NJ)
            dve.sem_inc(xy_ready, NJ)

            def expert(e, k, loads):
                base = e * NJ
                dve.wait_ge(bc_in[k], loads)
                dve.wait_ge(e_in[k], loads)
                for n, (m, hf) in enumerate(jobs):
                    dve.wait_ge(h_ps, base + n + 1)
                    dve.wait_ge(h_ready, base + n + 1)
                    dve.tensor_tensor(t1[:, m, cols(hf)], ps[:, n % 2, 0:W], bc[:, k, 0, cols(hf)], ALU.mult).then_inc(t1_ready, 1)
                    dve.wait_ge(x3_ps, base + n + 1)
                    dve.wait_ge(t3m_ready, base + n + 1)
                    dve.tensor_tensor(t3[:, m, cols(hf)], ps[:, 2 + n % 2, 0:W], bc[:, k, 0, cols(hf)], ALU.mult).then_inc(t3_ready, 1)
                    dve.wait_ge(t3_ready, base + n + 3)
                    dve.wait_ge(y_ready, base + n + 1)
                    dve.scalar_tensor_tensor(out=t3m[:, m, cols(hf)], in0=t3[:, m, cols(hf)], scalar=be[:, k, 2, m:m + 1],
                                             in1=bc[:, k, 1, cols(hf)], op0=ALU.add, op1=ALU.mult).then_inc(t3m_ready, 1)
                for n, (m, hf) in enumerate(jobs):
                    dve.wait_ge(x2_ps, base + n + 2)
                    dve.wait_ge(t3m_ready, base + NJ + n + 1)
                    dve.scalar_tensor_tensor(out=t3m[:, m, cols(hf)], in0=ps[:, 4 + n, 0:W], scalar=be[:, k, 1, m:m + 1],
                                             in1=t3m[:, m, cols(hf)], op0=ALU.add, op1=ALU.mult).then_inc(xy_ready, 1)

            with dve.Fori(0, E // 2) as i:
                for k in range(2):
                    expert(i * 2 + k, k, i * 32 + 32)
            for r in range(NR):
                dve.wait_ge(f_ps, r + 1)
                dve.tensor_tensor(w[:, r, :], ps[:, r % 4, 0:DM], x2[:, RT + r, :], ALU.add).then_inc(added, 1)
                dve.wait_ge(added, r + 1)
                dve.tensor_tensor(w[:, r, :], w[:, r, :], ps[:, 4 + r % 4, 0:DM], ALU.add).then_inc(f_ready, 1)

        @block.gpsimd
        def _(pool):
            pool.wait_ge(t1_ready, 1)
            pool.sem_inc(y_ready, NJ)
            with pool.Fori(0, E) as e:
                for n, (m, hf) in enumerate(jobs):
                    pool.wait_ge(xy_ready, e * NJ + NJ + n + 1)
                    pool.wait_ge(y_ready, e * NJ + n + 1)
                    pool.tensor_tensor(yT[:, m, cols(hf)], yT[:, m, cols(hf)], t3m[:, m, cols(hf)], ALU.add).then_inc(y_ready, 1)


def build(nc, nb, d, x1_out):
    top_ctx = ExitStack()
    with top_ctx:
        def sb(name, shape, dt=F32):
            return top_ctx.enter_context(nc.sbuf_tensor(name, shape, dt))
        NR = nb * RT
        x1 = sb("x1", [P, (nb + 1) * RT, DM])
        ident = sb("ident_sb", [P, P])
        ones = sb("ones_sb", [P, 1])
        with ExitStack() as c1:
            xin = [None]
            bo = c1.enter_context(nc.sbuf_tensor("bo_sb", [P, DM], F32))
            mv = c1.enter_context(nc.sbuf_tensor("mv", [P, NR, 2], F32))
            st6 = c1.enter_context(nc.sbuf_tensor("st6", [P, NR, 6], F32))
            rs = c1.enter_context(nc.sbuf_tensor("rs", [P, NR], F32))

            def ln_sems(sem):
                return {k: sem("ln_" + k) for k in ("stats", "mean", "var", "sqrt", "rstd", "norm", "tps", "tsb")}

            def ln_vector(dve, ln, nb):
                for r in range(NR):
                    dve.bn_stats(st6[:, r, :], xin[0][:, r, :]).then_inc(ln["stats"], 1)
                dve.wait_ge(ln["stats"], NR)
                for r in range(NR):
                    dve.bn_aggr(mv[:, r, :], st6[:, r, :]).then_inc(ln["mean"], 1)
                dve.wait_ge(ln["mean"], NR)
                dve.tensor_scalar(rs[:], mv[:, :, 1], EPS, None, ALU.add).then_inc(ln["var"], 1)
                dve.wait_ge(ln["sqrt"], 1)
                dve.reciprocal(rs[:], rs[:]).then_inc(ln["rstd"], 1)
                dve.wait_ge(ln["rstd"], 1)
                for r in range(NR):
                    dve.tensor_scalar(x1[:, RT + r, :], xin[0][:, r, :], mv[:, r, 0:1], rs[:, r:r + 1], ALU.subtract, ALU.mult).then_inc(ln["norm"], 1)
                dve.wait_ge(ln["tps"], 2 * NR)

            def ln_sqrt(act, ln):
                act.wait_ge(ln["var"], 1)
                act.activation(rs[:], rs[:], ACT.Sqrt).then_inc(ln["sqrt"], 1)

            def ln_transposes(pe, ln, ps, nb):
                for r in range(NR):
                    pe.wait_ge(ln["norm"], r + 1)
                    for t in range(2):
                        j = 2 * r + t
                        if j >= 8:
                            pe.wait_ge(ln["tsb"], j - 7)
                        pe.transpose(ps[:, j % 8, 0:P], x1[:, RT + r, t * P:t * P + P], ident[:, :]).then_inc(ln["tps"], 1)
                pe.wait_ge(ln["tsb"], 2 * NR)

            def ln_copies(act, ln, ps, xnT, nb):
                for j in range(2 * NR):
                    act.wait_ge(ln["tps"], j + 1)
                    act.activation(xnT[:, j % 2, (j // 2) * P:(j // 2) * P + P], ps[:, j % 8, 0:P], ACT.Copy).then_inc(ln["tsb"], 1)

            top = dict(x1=x1, ident=ident, ones=ones, xin=xin, bo=bo, ln_sems=ln_sems, ln_vector=ln_vector,
                       ln_sqrt=ln_sqrt, ln_transposes=ln_transposes, ln_copies=ln_copies)
            cross_attention(nc, nb, top, d)
        recurrence(nc, nb, top, d)
        experts(nc, nb, top, d, x1_out)


NB = 4
SCRATCH = {"wk_split": (HEADS, P, 4, P), "wv_split": (NG, P, 4, QH * DH), "wm_rows": (16, NB * ROWS)}


def layout(I, nb):
    import numpy as np

    A = {}
    rep = lambda a, shape: np.broadcast_to(a, shape)
    fold = lambda a: a.reshape(2, P, -1).transpose(1, 0, 2)
    x, ctx = I["x"][:nb], I["ctx_768"][:nb]
    A["x"] = x.reshape(nb * RT, P, DM).transpose(1, 0, 2)
    t = ctx.transpose(0, 2, 1)
    c = np.stack([t[:, :P], np.concatenate([t[:, P:], t[:, P:]], 1)], 2)
    A["ctx"] = c.reshape(nb, P, 2, NC, CH).transpose(0, 3, 1, 2, 4)
    rows = lambda W: np.stack([W[:P], np.concatenate([W[P:], W[P:]], 0)], 1)
    A["wk"] = rep(rows(I["L0_xattn_Wk"]).reshape(P, 2, HEADS, 1, DH), (P, 2, HEADS, 2, DH)).reshape(P, 4096)
    A["wv"] = rows(I["L0_xattn_Wv"]).reshape(P, 2048)
    wq = I["L0_xattn_Wq"].reshape(2, P, HEADS, 1, DH).transpose(2, 1, 0, 3, 4)
    A["wq"] = rep(wq, (HEADS, P, 2, 2, DH)).reshape(HEADS, P, 2, P)
    A["wo"] = rep(I["L0_xattn_Wo"].reshape(HEADS, 1, DH, DM), (HEADS, 2, DH, DM)).reshape(HEADS, P, DM)
    A["bo"] = rep(I["L0_xattn_bo"], (P, DM))
    A["ident"] = np.eye(P, dtype=np.float32)
    sw = np.arange(DM) ^ 1
    q, k, v, g = (I["L0_attn_" + n] for n in ("q_w", "k_w", "v_w", "g_w"))
    A["w6"] = np.stack([fold(m.T) for m in (q, q[sw], k, k[sw], v, g)], 1)
    f = np.float32
    inv = (f(1.0) / f(10000.0) ** (np.arange(8, dtype=f) / f(8))).astype(f)
    ang = np.arange(ROWS, dtype=f)[:, None] * inv[None, :]
    cos, sin = np.cos(ang).astype(f).T, np.sin(ang).astype(f).T
    dd = np.arange(P) % 16
    A["rope"] = np.stack([np.tile(cos[dd // 2], (1, 2)), np.tile(sin[dd // 2], (1, 2)) * np.where(dd % 2, 1, -1).astype(f)[:, None]], 1)
    bd = np.zeros((P, 2, 2, P), f)
    for i, n in enumerate(("Wq", "Wk")):
        for h in range(16):
            s = slice(16 * (h % 8), 16 * (h % 8) + 16)
            bd[s, i, h // 8, s] = I["L0_attn_" + n][h].T
    A["bd"] = bd
    A["gb"] = I["L0_attn_g_b"].reshape(2, P).T
    A["dl"] = I["L0_attn_base_decay_logits"].reshape(2, P).T
    A["seq"] = rep((np.arange(NB * ROWS) % ROWS != 0).astype(f), (P, NB * ROWS))
    p = np.arange(P)
    same = (p[:, None] // 16 == p[None, :] // 16)
    A["selv"] = np.stack([(same & (p[:, None] % 16 == e)).astype(f) for e in range(16)], 1)
    j = np.arange(32)
    A["sely"] = np.stack([((p[:, None] // 16 == j[None, :] // 4) & (j[None, :] % 4 == e)).astype(f) for e in range(4)], 1)
    order = 16 * (p % 32 // 4) + 4 * (p // 32) + p % 4
    A["ow"] = np.stack([I["L0_attn_out_w"].T[P * g + order] for g in range(2)], 1)
    A["vecs"] = np.stack([rep(I["L0_attn_" + n], (P, DM)) for n in ("out_b", "ln_g", "ln_b")], 1)
    A["gw"] = fold(I["L0_ffn_gate_w"].T)
    A["iota"] = rep(np.arange(8, dtype=f), (P, 8))
    A["we"] = np.stack([np.stack([fold(I["L0_ffn_" + n][e].T) for n in ("w1", "w2", "w3")], 1) for e in range(8)], 0)
    A["be"] = np.stack([I["L0_ffn_" + n].reshape(8, 2, P).transpose(0, 2, 1) for n in ("b1", "b2", "b3")], 2)
    A["sw12"] = np.stack([fold(I["L0_ffn_" + n].T) for n in ("sw1", "sw2")], 2)
    A["sw3"] = I["L0_ffn_sw3"].T.reshape(4, P, DM).transpose(1, 0, 2)
    return {n: np.ascontiguousarray(a, dtype=f) for n, a in A.items()}


def kernel(**inputs):
    import numpy as np
    from concourse import bacc
    from concourse.bass_utils import run_bass_kernel_spmd

    arrays = layout({n: np.asarray(a) for n, a in inputs.items()}, NB)
    nc = bacc.Bacc("TRN2", target_bir_lowering=False, num_devices=1)
    d = {n: nc.dram_tensor("in_" + n, a.shape, F32, kind="ExternalInput").ap() for n, a in arrays.items()}
    d |= {n: nc.dram_tensor(n, shape, F32).ap() for n, shape in SCRATCH.items()}
    out = nc.dram_tensor("out_0", (P, NB * RT, DM), F32, kind="ExternalOutput").ap()
    build(nc, NB, d, out)
    r = run_bass_kernel_spmd(nc, [{"in_" + n: a for n, a in arrays.items()}], core_ids=[0])
    return np.ascontiguousarray(r.results[0]["out_0"].transpose(1, 0, 2).reshape(NB, ROWS, DM))
```

```python
import concourse.bass as bass
from concourse import mybir
from contextlib import ExitStack

F32 = mybir.dt.float32
F32R = mybir.dt.float32r
ALU = mybir.AluOpType
ACT = mybir.ActivationFunctionType
AX = mybir.AxisListType

P = 128
DM = 256
ROWS = 256
RT = ROWS // P
KEYS = 4096
CTX = 192
HEADS = 16
DH = 64
CH = 512
NC = KEYS // CH
KT = CH // P
QH = 4
NG = HEADS // QH
EPS = 1e-5
MROW = 64
M2 = 96


def cross_attention(nc, nb, top, d):
    ctx = ExitStack()
    with ctx:
        def sb(name, shape, dt=F32):
            return ctx.enter_context(nc.sbuf_tensor(name, shape, dt))

        def sem(name):
            return ctx.enter_context(nc.semaphore(name))

        x1, ident, ones = top["x1"], top["ident"], top["ones"]
        NR = nb * RT
        C = sb("C", [P, 3, KEYS], F32R)
        craw = sb("craw", [P, 2, CH])
        KH = sb("KH", [P, 2, NC, CH], F32R)
        KL = sb("KL", [P, 2, NC, CH], F32R)
        V = sb("V", [P, NC * KT, QH * DH])
        PR = sb("PR", [P, 2, KT * ROWS])
        acc = sb("acc", [P, 2, KT * ROWS])
        wk = sb("wk", [P, 2, 4, P], F32R)
        wv = sb("wv", [P, 4, QH * DH], F32R)
        wq = sb("wq", [P, 2, 2, P])
        wo = sb("wo", [P, 2, 2, DM])
        Q1 = sb("Q1", [P, 2, 2, ROWS], F32R)
        Q2 = sb("Q2", [P, 2, 2, ROWS], F32R)
        qs = sb("qs", [P, ROWS])
        qh = sb("qh", [P, ROWS], F32R)
        amx = sb("amx", [P, 2, RT, NC])
        nmx = sb("nmx", [P, 2, RT])
        accf = sb("accf", [P, 2, ROWS])
        Ot = sb("Ot", [P, 2, ROWS])
        rl = sb("rl", [P, 2 * RT])
        zero = sb("zero", [P, 1])
        warm = sb("warm", [P, 1])
        xnT = sb("xnT_sb", [P, 2, ROWS])
        bo = sb("bo_sb", [P, DM])
        st6, mv, rs = sb("st6", [P, NR, 6]), sb("mv", [P, NR, 2]), sb("rs", [P, NR])

        flat = lambda t: t.rearrange("p a n -> p (a n)")
        xin = flat(PR[:, :, :]).rearrange("p (r n) -> p r n", n=DM)[:, 0:NR, :]
        raw = flat(V[:, :, :])
        rawk, rawv = raw[:, 0:2048], raw[:, 2048:4096]
        xnT_all = raw[:, 6144:6144 + 2 * nb * ROWS].rearrange("p (t n) -> p t n", t=2)
        khf = KH[:, :, :, :].rearrange("p h c n -> p (h c n)")
        klf = KL[:, :, :, :].rearrange("p h c n -> p (h c n)")
        crawb = [craw[:, :, :]] + [acc[:, h, :].rearrange("p (a n) -> p a n", a=2) for h in range(2)]
        BUFS = len(crawb)

        ps = ctx.enter_context(nc.psum_tensor("ps1", [P, 8, 512], F32))
        psS, psK, psA, psO, psV, psM = ps[:, 0:2, :], ps[:, 2, :], ps[:, 3:5, :], ps[:, 5, :], ps[:, 6, :], ps[:, 7, :]

        x_in, c_in = sem("x_in"), sem("c_in")
        wkraw_in, wvraw_in, wk_st, wv_st = sem("wkraw_in"), sem("wvraw_in"), sem("wk_st"), sem("wv_st")
        whi, wlo, xst, xn_in = sem("whi"), sem("wlo"), sem("xst"), sem("xn_in")
        init, filled = sem("init"), sem("filled")
        craw_in = [sem(f"craw_in{i}") for i in range(BUFS)]
        chi, cready = sem("chi"), sem("cready")
        wk_in = [sem(f"wk_in{i}") for i in range(2)]
        wq_in = [sem(f"wq_in{i}") for i in range(2)]
        wo_in = [sem(f"wo_in{i}") for i in range(2)]
        wv_in = sem("wv_in")
        k_ps, k_hi, k_lo = sem("k_ps"), sem("k_hi"), sem("k_lo")
        a_ps, a_max = sem("a_ps"), sem("a_max")
        s_ps, p_ready, pv_done = sem("s_ps"), sem("p_ready"), sem("pv_done")
        acc_done, fold_done = sem("acc_done"), sem("fold_done")
        o_sb = sem("o_sb")
        l_ps, rl_ready, out_ps, x_added = sem("l_ps"), sem("rl_ready"), sem("out_ps"), sem("x_added")
        q_ps, q_sb, q_hi, q_ready = sem("q_ps"), sem("q_sb"), sem("q_hi"), sem("q_ready")
        m_ready, m_ps, m_row = sem("m_ready"), sem("m_ps"), sem("m_row")
        v_ps, v_sb = sem("v_ps"), sem("v_sb")
        ln = norm_sems(sem, "n1")

        HS = 2 * 2 * NC
        V_JOB = {}
        for u in range(2 * NC):
            t = 18 + 9 * u // 5
            V_JOB[t % HS] = (u, t < HS)
        V_FIRST = sum(late for _, late in V_JOB.values())

        def loops(eng, quad):
            with eng.Fori(0, nb) as b:
                with eng.Fori(0, NG - 1) as g:
                    quad(b * NG + g, b, g, False)
                quad(b * NG + (NG - 1), b, NG - 1, True)

        block = ctx.enter_context(nc.Block())

        @block.sync
        def _(sp):
            def load_ctx(b, c, buf):
                sp.dma_start(crawb[buf], d["ctx"][bass.ds(b, 1), c].rearrange("o p t n -> p (o t) n")).then_inc(craw_in[buf], 16)

            def load_wk(p, slot):
                sp.dma_start(wk[:, slot, :, :].bitcast(F32), d["wk_split"][bass.ds(p, 1)].rearrange("o p t m -> p (o t) m")).then_inc(wk_in[slot], 16)

            def load_wq(p, slot):
                sp.dma_start(wq[:, slot, :, :], d["wq"][bass.ds(p, 1)].rearrange("o p t m -> p (o t) m")).then_inc(wq_in[slot], 16)

            def load_wo(p, slot):
                sp.dma_start(wo[:, slot, :, :], d["wo"][bass.ds(p, 1)].rearrange("o p h m -> p (o h) m")).then_inc(wo_in[slot], 16)

            def load_wv(g):
                sp.dma_start(wv[:].bitcast(F32), d["wv_split"][bass.ds(g, 1)].rearrange("o p t m -> p (o t) m")).then_inc(wv_in, 16)

            def load_xnT(b):
                sp.dma_start(xnT[:], d["xnT"][bass.ds(b, 1)].rearrange("o p t n -> p (o t) n")).then_inc(xn_in, 16)

            sp.dma_start(xin, d["x"]).then_inc(x_in, 16)
            sp.dma_start(rawk, d["wk"]).then_inc(wkraw_in, 16)
            load_ctx(0, 0, 0)
            sp.dma_start(ident[:], d["ident"]).then_inc(c_in, 16)
            sp.dma_start(rawv, d["wv"]).then_inc(wvraw_in, 16)
            load_ctx(0, 1, 1)
            load_ctx(0, 2, 2)
            sp.dma_start(bo[:], d["bo"]).then_inc(c_in, 16)
            for p in range(2):
                load_wq(p, p)
            kh = khf[:, 0:4096].bitcast(F32).rearrange("p (t h m) -> p t h m", t=4, h=HEADS // 2)
            kl = klf[:, 0:4096].bitcast(F32).rearrange("p (t g m) -> p t g m", t=4, g=NG)
            sp.wait_ge(wlo, 1)
            for p in range(2):
                sp.dma_start(wk[:, p, :, :].bitcast(F32), kh[:, :, p, :]).then_inc(wk_in[p], 16)
            for t in range(4):
                sp.dma_start(d["wk_split"][:, :, t, :].rearrange("h p m -> p h m"), kh[:, t, :, :]).then_inc(wk_st, 16)
            sp.wait_ge(ln["t_sb"], NR)
            sp.dma_start(xnT[:], xnT_all[:, :, 0:ROWS]).then_inc(xn_in, 16)
            sp.wait_ge(wlo, 2)
            sp.dma_start(wv[:].bitcast(F32), kl[:, :, 0, :]).then_inc(wv_in, 16)
            for t in range(4):
                sp.dma_start(d["wv_split"][:, :, t, :].rearrange("g p m -> p g m"), kl[:, t, :, :]).then_inc(wv_st, 16)
            for b in range(nb):
                sp.dma_start(d["xnT"][b], xnT_all[:, :, b * ROWS:b * ROWS + ROWS]).then_inc(xst, 16)
            load_wo(NC - 1, 1)
            load_wo(0, 0)
            for c in range(BUFS, NC):
                sp.wait_ge(cready, c - BUFS + 1)
                load_ctx(0, c, c % BUFS)
            sp.wait_ge(wk_st, 64)
            sp.wait_ge(wv_st, 64)
            sp.wait_ge(xst, 16 * nb)

            def quad(it, b, g, last):
                for pi in range(2):
                    p = it * 2 + pi
                    of_next = lambda k: (g * 2 + pi + k) % (HEADS // 2)
                    sp.wait_ge(k_ps, NC * p + NC)
                    load_wk(of_next(2), pi)
                    sp.wait_ge(q_ps, p + 1)
                    load_wq(of_next(2), pi)
                    if pi == 1:
                        sp.wait_ge(v_ps, it * 16 + 16)
                        load_wv((g + 1) % NG)
                    if last and pi == 0:
                        sp.wait_ge(q_ps, p + 2)
                        load_xnT((b + 1) % nb)
                        for c in range(NC):
                            sp.wait_ge(cready, b * NC + NC + c)
                            load_ctx((b + 1) % nb, c, 0)
                    sp.wait_ge(out_ps, 2 * p + 3)
                    load_wo(of_next(1), (pi + 1) % 2)

            loops(sp, quad)

        @block.tensor
        def _(pe):
            bank = lambda r: ps[:, r % 4, :]
            pe.wait_ge(c_in, 32)
            transpose_rows(pe, ln, NR, lambda r: x1[:, RT + r, :], bank, ident)
            pe.wait_ge(ln["t_sb"], NR)

            def split_product(out, stationary, moving):
                for i, (w, c) in enumerate([(0, 0), (0, 1), (2, 0), (1, 2), (3, 2)]):
                    mm = pe.matmul(out, stationary(w, c), moving(w, c), start=(i == 0), stop=(i == 4))
                return mm

            def project_q(slot):
                for t in range(2):
                    mm = pe.matmul(psM[:, 0:ROWS], wq[:, slot, t, :], xnT[:, t, :], start=(t == 0), stop=(t == 1))
                mm.then_inc(q_ps, 1)

            def project_k(slot, c):
                split_product(psK, lambda w, _: wk[:, slot, w, :], lambda _, k: C[:, k, c * CH:c * CH + CH]).then_inc(k_ps, 1)

            def guess(slot, h, c, before):
                for t in range(RT):
                    if before is not None:
                        pe.wait_ge(a_max, before + t - 1)
                    pe.matmul(psA[:, t, :], Q1[:, slot, h, t * P:t * P + P], KH[:, h, c, :],
                              start=True, stop=True).then_inc(a_ps, 1)

            def project_v(u):
                for k in range(2):
                    t = 2 * u + k
                    mm = split_product(psV[:, k * 256:k * 256 + 256], lambda _, c: C[:, c, t * P:t * P + P],
                                       lambda w, _: wv[:, w, :])
                mm.then_inc(v_ps, 1)

            def scores_part(part, slot, h, c, k, start=True):
                out = psS[:, k // 2, (k % 2) * ROWS:(k % 2) * ROWS + ROWS]
                if part == 0:
                    return pe.matmul(out, KH[:, h, c, k * P:k * P + P], Q1[:, slot, h, :], start=start, stop=False, skip_group_check=True)
                return pe.matmul(out, KL[0:M2, h, c, k * P:k * P + P], Q2[0:M2, slot, h, :], start=False, stop=True, skip_group_check=True)

            def scores(slot, h, c):
                for k in range(KT):
                    scores_part(0, slot, h, c, k)
                    mm = scores_part(1, slot, h, c, k)
                mm.then_inc(s_ps, 1)

            def scores_without_max(slot, h):
                for k in range(KT):
                    scores_part(0, slot, h, 0, k, start=(k % 2 == 0))

            def scores_with_max(slot, h):
                for k in range(KT):
                    mm = scores_part(1, slot, h, 0, k)
                mm.then_inc(s_ps, 1)

            def weighted_sum(hd, h, c):
                for k in range(KT):
                    half = k % 2
                    mm = pe.matmul(psO[half * DH:half * DH + DH, h * ROWS:h * ROWS + ROWS], V[:, c * KT + k, hd * DH:hd * DH + DH],
                                   PR[:, h, k * ROWS:k * ROWS + ROWS],
                                   start=(c == 0 and k < 2 and h == 0), stop=(c == NC - 1 and k >= 2), skip_group_check=True)
                mm.then_inc(pv_done, 1)

            def row_sums():
                for h in range(2):
                    for t in range(RT):
                        mm = pe.matmul(psM[:, 2 * h + t:2 * h + t + 1], accf[:, h, t * P:t * P + P], ones[:, 0:1], start=True, stop=True)
                mm.then_inc(l_ps, 1)

            def project_out(slot, h):
                for t in range(RT):
                    mm = pe.matmul(psM[:, t * DM:t * DM + DM], Ot[:, h, t * P:t * P + P], wo[:, slot, h, :], start=True, stop=True)
                mm.then_inc(out_ps, 1)

            def max_row(h):
                for t in range(RT):
                    mm = pe.matmul(psM[MROW:MROW + 1, ROWS + t * P:ROWS + t * P + P], nmx[:, h, t:t + 1], ident[:, :],
                                   start=True, stop=True)
                mm.then_inc(m_ps, 1)

            pe.wait_ge(xn_in, 16)
            pe.wait_ge(wq_in[0], 16)
            project_q(0)
            pe.wait_ge(wk_in[0], 16)
            for c in range(NC):
                pe.wait_ge(cready, c + 1)
                if c > 0:
                    pe.wait_ge(k_lo, 2 * c)
                    pe.wait_ge(k_hi, 4 * c)
                project_k(0, c)
                for u in range(2 * c, min(2 * c + 2, V_FIRST)):
                    if u == 0:
                        pe.wait_ge(wv_in, 16)
                        pe.wait_ge(wlo, 2)
                    else:
                        pe.wait_ge(v_sb, u)
                    project_v(u)
                if c > 0:
                    if c == 1:
                        pe.wait_ge(q_ready, 1)
                    for h in range(2):
                        pe.wait_ge(k_hi, 4 * (c - 1) + h + 3)
                        guess(0, h, c - 1, 4 * (c - 1) + 2 * h if 2 * (c - 1) + h > 0 else None)
            pe.wait_ge(filled, 6)
            pe.sem_inc(pv_done, 1)
            pe.sem_inc(out_ps, 1)
            pe.sem_inc(m_ps, 1)
            for half in range(2):
                pe.matmul(psO[half * DH:half * DH + DH, :], V[:, 31, DH:2 * DH], PR[:, 1, 0:2 * ROWS],
                          start=True, stop=False, skip_group_check=True)

            def quad(it, b, g, last):
                for t in range(HS):
                    pi, c, h = t // (2 * NC), t % (2 * NC) // 2, t % 2
                    p, T = it * 2 + pi, it * HS + t
                    nslot = (pi + 1) % 2
                    chunk = NC * p + c
                    nchunk = chunk + NC

                    def sum_before():
                        pe.wait_ge(p_ready, T + 1)
                        u = (t - 1) % HS
                        if t > 0 and pi == 0:
                            pe.wait_ge(v_sb, it * 16 + 2 * (u % (2 * NC) // 2) + 2)
                        if t % (2 * NC) == 1:
                            pe.wait_ge(o_sb, p + 1)
                        weighted_sum(u // (2 * NC) * 2 + u % 2, u % 2, u % (2 * NC) // 2)

                    def next_keys():
                        if c == 0:
                            pe.wait_ge(wk_in[nslot], (it + 1 + pi) * 16)
                        if last and pi == 1:
                            pe.wait_ge(cready, b * NC + NC + c + 1)
                        pe.wait_ge(k_lo, 2 * nchunk)
                        project_k(nslot, c)

                    def next_guess(slot, k, n, c):
                        pe.wait_ge(k_hi, 4 * n + k + 3)
                        guess(slot, k, c, 4 * n + 2 * k)

                    def v_job():
                        u, ahead = V_JOB[t]
                        if u == 0:
                            pe.wait_ge(wv_in, (it + 1) * 16 + 16)
                        pe.wait_ge(v_sb, (it + ahead) * 16 + u)
                        project_v(u)

                    if c == 0 and h == 0:
                        pe.wait_ge(wq_in[nslot], (it + 1 + pi) * 16)
                        if last and pi == 1:
                            pe.wait_ge(xn_in, (b + 2) * 16)
                        pe.wait_ge(x_added, 4 * p + 4)
                        project_q(nslot)
                        next_guess(pi, 0, nchunk - 1, NC - 1)
                        sum_before()
                        next_guess(pi, 1, nchunk - 1, NC - 1)
                        pe.wait_ge(p_ready, T + 1)
                        scores_without_max(pi, 0)
                        pe.wait_ge(m_ready, 2 * p + 1)
                        pe.wait_ge(q_sb, p + 2)
                        max_row(0)
                        if t in V_JOB:
                            v_job()
                        pe.wait_ge(m_row, 2 * p + 1)
                        scores_with_max(pi, 0)
                    elif c == 0:
                        next_keys()
                        pe.wait_ge(m_ready, 2 * p + 2)
                        max_row(1)
                        pe.wait_ge(p_ready, T + 1)
                        scores_without_max(pi, 1)
                        pe.wait_ge(m_row, 2 * p + 2)
                        scores_with_max(pi, 1)
                        sum_before()
                    else:
                        pe.wait_ge(k_lo, 2 * chunk + h + 1)
                        pe.wait_ge(p_ready, T + 1)
                        scores(pi, h, c)
                        if h == 0:
                            if c == 1:
                                pe.wait_ge(q_ready, p + 2)
                            next_guess(nslot, 0, nchunk - 1, c - 1)
                            sum_before()
                            next_guess(nslot, 1, nchunk - 1, c - 1)
                        else:
                            next_keys()
                            sum_before()
                    if t in V_JOB and not (c == 0 and h == 0):
                        v_job()
                    if c == 2 and h == 0:
                        pe.wait_ge(fold_done, 4 * p + 4)
                        row_sums()
                    if c in (3, 4) and h == 0:
                        pe.wait_ge(rl_ready, p + 1)
                        pe.wait_ge(x_added, 4 * p + 2 * (c - 3) + 4)
                        pe.wait_ge(wo_in[nslot], (it + 1) * 16)
                        project_out(nslot, c - 3)

            loops(pe, quad)
            pairs = nb * HEADS // 2
            pe.wait_ge(p_ready, pairs * 2 * NC + 1)
            weighted_sum(QH - 1, 1, NC - 1)
            pe.wait_ge(fold_done, 4 * pairs + 4)
            pe.wait_ge(q_sb, pairs + 1)
            row_sums()
            pe.wait_ge(rl_ready, pairs + 1)
            pe.wait_ge(wo_in[1], (nb * NG + 1) * 16)
            pe.wait_ge(o_sb, pairs + 1)
            for h in range(2):
                pe.wait_ge(x_added, 4 * pairs + 2 * h + 4)
                project_out(1, h)

        @block.scalar
        def _(act):
            norm_sqrt(act, ln, rs)
            act.wait_ge(wkraw_in, 16)
            act.activation(khf[:, 0:2048], rawk, ACT.Copy).then_inc(whi, 1)
            copy_rows(act, ln, NR, lambda r: ps[:, r % 4, :], xnT_all)

            def context_hi(c, buf):
                act.activation(C[:, 0:3:2, c * CH:c * CH + CH], crawb[buf], ACT.Copy).then_inc(chi, 1)

            def keys_hi(c, h):
                own = slice(h * DH, h * DH + DH)
                act.activation(KH[own, h, c, :], psK[own], ACT.Copy).then_inc(k_hi, 1)

            def keys_hi_twice(c, before):
                for h in range(2):
                    own, other = slice(h * DH, h * DH + DH), slice((1 - h) * DH, (1 - h) * DH + DH)
                    act.wait_ge(k_hi, before + h + 1)
                    act.activation(KH[other, h, c, :], KH[own, h, c, :].bitcast(F32), ACT.Copy).then_inc(k_hi, 1)

            def scale_q():
                act.activation(qs[:], psM[:, 0:ROWS], ACT.Copy, scale=float(DH) ** -0.5).then_inc(q_sb, 1)

            def copy_max(slot, h):
                act.activation(Q2[MROW:MROW + 1, slot, h, :], psM[MROW:MROW + 1, ROWS:2 * ROWS], ACT.Copy).then_inc(m_row, 1)

            def first_context_hi(c):
                act.wait_ge(craw_in[c % BUFS], 16 * (c // BUFS) + 16)
                context_hi(c, c % BUFS)

            first_context_hi(0)
            act.wait_ge(wvraw_in, 16)
            act.activation(klf[:, 0:2048], rawv, ACT.Copy).then_inc(whi, 1)
            for c in range(1, BUFS):
                first_context_hi(c)
            act.wait_ge(q_ps, 1)
            scale_q()
            act.wait_ge(wk_st, 64)
            act.wait_ge(wk_in[0], 16)
            act.wait_ge(wk_in[1], 16)
            for c in range(NC):
                if c + BUFS < NC:
                    first_context_hi(c + BUFS)
                act.wait_ge(k_ps, c + 1)
                keys_hi(c, 0)
                keys_hi(c, 1)
                keys_hi_twice(c, 4 * c)
            act.wait_ge(filled, 6)
            act.sem_inc(p_ready, 1)

            def quad(it, b, g, last):
                for t in range(HS):
                    pi, c, h = t // (2 * NC), t % (2 * NC) // 2, t % 2
                    p, T = it * 2 + pi, it * HS + t
                    nchunk = NC * (p + 1) + c
                    if t == 0:
                        act.activation(warm[:], zero[:], ACT.Exp)
                    if c == 0 and h == 0:
                        act.wait_ge(q_ps, p + 2)
                        act.wait_ge(q_ready, p + 1)
                        scale_q()
                        act.wait_ge(m_ps, 2 * p + 2)
                        copy_max(pi, 0)
                        act.wait_ge(pv_done, T + 2)
                        act.wait_ge(out_ps, 2 * p + 1)
                        act.activation(flat(Ot[:, :, :]), psO, ACT.Copy).then_inc(o_sb, 1)
                    if c == 0 and h == 1:
                        act.wait_ge(k_ps, nchunk + 1)
                        keys_hi(c, 0)
                    act.wait_ge(s_ps, T + 1)
                    act.wait_ge(pv_done, T + 1)
                    act.wait_ge(acc_done, T + 1)
                    act.activation(PR[:, h, :], flat(psS), ACT.Exp).then_inc(p_ready, 1)
                    if c == 0 and h == 0:
                        act.wait_ge(m_ps, 2 * p + 3)
                        copy_max(pi, 1)
                    if h == 1:
                        if c > 0:
                            act.wait_ge(k_ps, nchunk + 1)
                            keys_hi(c, 0)
                        keys_hi(c, 1)
                        keys_hi_twice(c, 4 * nchunk)
                    if last and 4 <= t < 4 + 2 * NC and h == 0:
                        k = (t - 4) // 2
                        act.wait_ge(craw_in[0], 16 * -(-NC // BUFS) + (b * NC + k + 1) * 16)
                        act.wait_ge(k_ps, NC * (it * 2 + 1) + k + 1)
                        context_hi(k, 0)

            loops(act, quad)
            pairs = nb * HEADS // 2
            act.wait_ge(pv_done, pairs * 2 * NC + 2)
            act.wait_ge(out_ps, 2 * pairs + 1)
            act.activation(flat(Ot[:, :, :]), psO, ACT.Copy).then_inc(o_sb, 1)

        @block.vector
        def _(dve):
            def context_lo(c, buf):
                k = slice(c * CH, c * CH + CH)
                dve.tensor_tensor(C[:, 1, k], crawb[buf][:, 0, :], C[:, 0, k].bitcast(F32), ALU.subtract)
                dve.tensor_tensor(C[DH:, 2, k], crawb[buf][DH:, 1, :], C[DH:, 2, k].bitcast(F32), ALU.subtract).then_inc(cready, 1)

            def keys_lo(c, h):
                dve.tensor_tensor(KL[0:DH, h, c, :], psK[h * DH:h * DH + DH], KH[h * DH:h * DH + DH, h, c, :].bitcast(F32), ALU.subtract).then_inc(k_lo, 1)

            def chunk_max(h, c, t):
                dve.tensor_reduce(amx[:, h, t, c:c + 1], psA[:, t, :], AX.X, ALU.max).then_inc(a_max, 1)

            def negate_max(h):
                dve.tensor_reduce(nmx[:, h, :], amx[:, h, :, :], AX.X, ALU.max, negate=True).then_inc(m_ready, 1)

            def copy_v(u):
                dve.tensor_copy(flat(V[:, 2 * u:2 * u + 2, :]), psV).then_inc(v_sb, 1)

            def split_q(slot, before):
                dve.tensor_copy(qh[:], qs[:]).then_inc(q_hi, 1)
                dve.wait_ge(q_hi, before + 1)
                for h in range(2):
                    own = slice(h * DH, h * DH + DH)
                    dve.tensor_copy(Q1[0:DH, slot, h, :], qh[own, :].bitcast(F32))
                    dve.tensor_copy(Q2[0:DH, slot, h, :], qh[own, :].bitcast(F32))
                    ins = dve.tensor_tensor(Q1[DH:, slot, h, :], qs[own, :], qh[own, :].bitcast(F32), ALU.subtract)
                ins.then_inc(q_ready, 1)

            dve.wait_ge(x_in, 16)
            norm_vector(dve, ln, NR, lambda r: xin[:, r, :], lambda r: x1[:, RT + r, :], st6, mv, rs)
            dve.wait_ge(whi, 1)
            dve.tensor_tensor(khf[:, 2048:4096], rawk, khf[:, 0:2048].bitcast(F32), ALU.subtract).then_inc(wlo, 1)
            def first_context_lo(c):
                dve.wait_ge(chi, c + 1)
                context_lo(c, c % BUFS)

            first_context_lo(0)
            dve.wait_ge(whi, 2)
            dve.tensor_tensor(klf[:, 2048:4096], rawv, klf[:, 0:2048].bitcast(F32), ALU.subtract).then_inc(wlo, 1)
            for c in range(1, BUFS):
                first_context_lo(c)
            dve.wait_ge(q_sb, 1)
            split_q(0, 0)
            dve.wait_ge(ln["t_ps"], NR)
            dve.wait_ge(c_in, 32)
            dve.tensor_tensor(x1[:, RT:, :], xin, bo[:, :].unsqueeze(1).to_broadcast([P, NR, DM]), ALU.add).then_inc(init, 1)
            dve.wait_ge(wv_st, 64)
            dve.wait_ge(wv_in, 16)
            for c in range(NC):
                if c + BUFS < NC:
                    first_context_lo(c + BUFS)
                for u in range(2 * c, min(2 * c + 2, V_FIRST)):
                    dve.wait_ge(v_ps, u + 1)
                    copy_v(u)
                for h in range(2):
                    if c > 0:
                        for t in range(RT):
                            dve.wait_ge(a_ps, 4 * (c - 1) + 2 * h + t + 1)
                            chunk_max(h, c - 1, t)
                    if c < NC - 1:
                        dve.wait_ge(k_hi, 4 * c + h + 1)
                        keys_lo(c, h)

            def quad(it, b, g, last):
                for t in range(HS):
                    pi, c, h = t // (2 * NC), t % (2 * NC) // 2, t % 2
                    p = it * 2 + pi
                    nchunk = NC * (p + 1) + c
                    if h == 0:
                        n = nchunk - 1
                        for k in range(2):
                            if c == 1:
                                dve.wait_ge(m_ready, 2 * p + 2)
                            for r in range(RT):
                                dve.wait_ge(a_ps, 4 * n + 2 * k + r + 1)
                                chunk_max(k, (c - 1) % NC, r)
                            if c == 0:
                                dve.wait_ge(a_max, 4 * n + 2 * k + 2)
                                dve.wait_ge(m_ps, 2 * p + 1)
                                negate_max(k)
                                if k == 0:
                                    for j in range(2):
                                        dve.wait_ge(k_hi, 4 * n + j + 1)
                                        keys_lo(NC - 1, j)
                    else:
                        if c == 0:
                            dve.wait_ge(q_sb, p + 2)
                            split_q((pi + 1) % 2, p + 1)
                        if c < NC - 1:
                            for j in range(2):
                                dve.wait_ge(k_hi, 4 * nchunk + j + 1)
                                keys_lo(c, j)
                    if t in V_JOB:
                        u, ahead = V_JOB[t]
                        dve.wait_ge(v_ps, (it + ahead) * 16 + u + 1)
                        copy_v(u)
                    if c == 2 and h == 0:
                        dve.wait_ge(l_ps, p + 1)
                        dve.wait_ge(x_added, 4 * p + 4)
                        dve.reciprocal(rl[:, :], psM[:, 0:2 * RT]).then_inc(rl_ready, 1)
                    if c in (3, 4) and h == 0:
                        k = c - 3
                        dve.wait_ge(rl_ready, p + 1)
                        dve.wait_ge(out_ps, 2 * p + k + 2)
                        dve.wait_ge(x_added, 4 * p + 2 * k + 4)
                        add_rows((p + NC - 1) // NC, k)
                    if last and 4 <= t < 4 + 2 * NC and h == 0:
                        k = (t - 4) // 2
                        dve.wait_ge(chi, b * NC + NC + k + 1)
                        context_lo(k, 0)

            def add_rows(slot, h):
                for t in range(RT):
                    row = x1[:, bass.ds(slot * RT + t, 1), :].rearrange("p o n -> p (o n)")
                    dve.scalar_tensor_tensor(out=row, in0=psM[:, t * DM:t * DM + DM], scalar=rl[:, 2 * h + t:2 * h + t + 1], in1=row,
                                             op0=ALU.mult, op1=ALU.add).then_inc(x_added, 1)

            dve.wait_ge(filled, 6)
            dve.sem_inc(x_added, 4)
            loops(dve, quad)
            pairs = nb * HEADS // 2
            dve.wait_ge(l_ps, pairs + 1)
            dve.wait_ge(x_added, 4 * pairs + 4)
            dve.reciprocal(rl[:, :], psM[:, 0:2 * RT]).then_inc(rl_ready, 1)
            dve.wait_ge(rl_ready, pairs + 1)
            for h in range(2):
                dve.wait_ge(out_ps, 2 * pairs + h + 2)
                dve.wait_ge(x_added, 4 * pairs + 2 * h + 4)
                add_rows(nb, h)
            dve.wait_ge(x_added, 4 * pairs + 8)

        @block.gpsimd
        def _(pool):
            pool.memset(ones[:], 1.0)
            pool.memset(zero[:], 0.0)
            pool.memset(accf[:, :, :], 1.0)
            pool.memset(x1[:, 0:RT, :], 0.0).then_inc(filled, 1)
            pool.wait_ge(filled, 1)
            pool.memset(Q2[MROW:M2].bitcast(F32), 0.0).then_inc(filled, 1)
            pool.wait_ge(filled, 2)
            pool.wait_ge(wv_st, 64)
            pool.wait_ge(wv_in, 16)
            pool.memset(KL[MROW:M2].bitcast(F32), 0.0).then_inc(filled, 1)
            pool.wait_ge(filled, 3)
            pool.memset(KL[MROW:MROW + 1].bitcast(F32), 1.0).then_inc(filled, 1)
            pool.wait_ge(filled, 4)
            pool.wait_ge(init, 1)
            pool.memset(PR[:, 1, :], 0.0).then_inc(filled, 1)
            pool.wait_ge(xst, 16 * nb)
            pool.wait_ge(xn_in, 16)
            pool.memset(V[:, 28:32, :], 0.0).then_inc(filled, 1)
            pool.wait_ge(cready, NC)
            pool.wait_ge(filled, 6)
            pool.sem_inc(acc_done, 2)
            pool.sem_inc(fold_done, 4)

            def quad(it, b, g, last):
                for t in range(HS):
                    pi, c, h = t // (2 * NC), t % (2 * NC) // 2, t % 2
                    p, T = it * 2 + pi, it * HS + t
                    pool.wait_ge(p_ready, T + 2)
                    if c == 0:
                        pool.wait_ge(fold_done, 4 * p + 2 * h + 2)
                        pool.tensor_tensor(acc[:, h, :], PR[:, h, :], zero[:, 0:1].to_broadcast([P, KT * ROWS]), ALU.add).then_inc(acc_done, 1)
                    else:
                        pool.wait_ge(acc_done, T + 1)
                        pool.tensor_tensor(acc[:, h, :], acc[:, h, :], PR[:, h, :], ALU.add).then_inc(acc_done, 1)
                    if c == NC - 1:
                        pool.wait_ge(acc_done, T + 3)
                        pool.tensor_tensor(acc[:, h, 0:512], acc[:, h, 0:512], acc[:, h, 512:1024], ALU.add).then_inc(fold_done, 1)
                        pool.wait_ge(fold_done, 4 * p + 2 * h + 5)
                        pool.wait_ge(l_ps, p + 1)
                        pool.tensor_tensor(accf[:, h, :], acc[:, h, 0:256], acc[:, h, 256:512], ALU.add).then_inc(fold_done, 1)

            loops(pool, quad)


def norm_sems(sem, name):
    return {k: sem(f"{name}_{k}") for k in ("stats", "mean", "var", "sqrt", "rstd", "normed", "t_ps", "t_sb")}


def norm_vector(dve, s, tiles, src, dst, st6, mv, rs, ready=None):
    for r in range(tiles):
        if ready:
            ready(r)
        dve.bn_stats(st6[:, r, :], src(r)).then_inc(s["stats"], 1)
    for r in range(tiles):
        dve.wait_ge(s["stats"], r + 1)
        dve.bn_aggr(mv[:, r, :], st6[:, r, :]).then_inc(s["mean"], 1)
    dve.wait_ge(s["mean"], tiles)
    dve.tensor_scalar(rs[:], mv[:, :, 1], EPS, None, ALU.add).then_inc(s["var"], 1)
    dve.wait_ge(s["sqrt"], 1)
    dve.reciprocal(rs[:], rs[:]).then_inc(s["rstd"], 1)
    dve.wait_ge(s["rstd"], 1)
    for r in range(tiles):
        dve.tensor_scalar(dst(r), src(r), mv[:, r, 0:1], rs[:, r:r + 1], ALU.subtract, ALU.mult).then_inc(s["normed"], 1)


def norm_sqrt(act, s, rs):
    act.wait_ge(s["var"], 1)
    act.activation(rs[:], rs[:], ACT.Sqrt).then_inc(s["sqrt"], 1)


def transpose_rows(pe, s, tiles, src, bank, ident):
    for r in range(tiles):
        pe.wait_ge(s["normed"], r + 1)
        if r >= 4:
            pe.wait_ge(s["t_sb"], r - 3)
        for t in range(2):
            mm = pe.transpose(bank(r)[:, t * P:t * P + P], src(r)[:, t * P:t * P + P], ident[:, :])
        mm.then_inc(s["t_ps"], 1)


def copy_rows(act, s, tiles, bank, dst):
    for r in range(tiles):
        act.wait_ge(s["t_ps"], r + 1)
        act.activation(dst[:, :, r * P:r * P + P], bank(r)[:, 0:2 * P].rearrange("p (t n) -> p t n", t=2), ACT.Copy).then_inc(s["t_sb"], 1)


def recurrence(nc, nb, top, d):
    x1, ident = top["x1"], top["ident"]
    NR = nb * RT
    N = nb * ROWS
    HALVES = max(1, N // 512)
    W = N // HALVES
    G = 2
    ctx = ExitStack()
    with ctx:
        def sb(name, shape, dt=F32):
            return ctx.enter_context(nc.sbuf_tensor(name, shape, dt))

        def sem(name):
            return ctx.enter_context(nc.semaphore(name))

        u = sb("u", [P, NR, DM])
        uT = sb("uT", [P, 2, N])
        w6 = sb("w6", [P, 6, 2, DM])
        bd = sb("bd", [P, 2, G, P])
        rope = sb("rope", [P, 2, W])
        gb = sb("gb", [P, G])
        dl = sb("dl", [P, G])
        dec = sb("dec", [P, G])
        seq = sb("seq", [P, N])
        dect = sb("dect", [P, G, N])
        selv = sb("selv", [P, 16, P])
        selvr = sb("selvr", [P, 16, P], F32R)
        sely = sb("sely", [P, 4, 32])
        ow = sb("ow", [P, G, DM])
        vecs = sb("vecs", [P, 3, DM])
        t1 = sb("t1", [P, 2, W])
        t2 = sb("t2", [P, 2, W])
        rot = sb("rot", [P, 2, W])
        qr = sb("qr", [P, G, N])
        gate = sb("gate", [P, 2, W])
        kk = sb("kk", [P, G, N])
        vh = sb("vh", [P, G, N], F32R)
        vl = sb("vl", [P, G, N], F32R)
        kv = sb("kv", [P, 2, N])
        M = sb("M", [P, 2, N])
        qm = sb("qm", [P, 2, N])
        yT = sb("yT", [P, G, N])
        st6, mv, rs = sb("st6b", [P, NR, 6]), sb("mvb", [P, NR, 2]), sb("rsb", [P, NR])
        st6c, mvc, rsc = sb("st6c", [P, NR, 6]), sb("mvc", [P, NR, 2]), sb("rsc", [P, NR])
        ps = ctx.enter_context(nc.psum_tensor("ps2", [P, 8, 512], F32))

        w_in = [sem(f"w6_in{i}") for i in range(4)]
        ln = norm_sems(sem, "n2")
        lo = norm_sems(sem, "n3")
        pr_ps = sem("pr_ps")
        ropes, rot_ready, r_ps, qr_ready, gate_ready, kk_ready = (sem(x) for x in ("ropes", "rot_ready", "r_ps", "qr_ready", "gate_ready", "kk_ready"))
        vhi, vlo, dec_ready, dect_ready, selr = sem("vhi"), sem("vlo"), sem("dec_ready"), sem("dect_ready"), sem("selr")
        v_ps, kv_ready, m_done, qm_ready, y_ps, y_sb = (sem(x) for x in ("vb_ps", "kv_ready", "m_done", "qm_ready", "y_ps", "y_sb"))
        o_ps, h_ready, scaled, fin = sem("o_ps"), sem("h_ready"), sem("scaled"), sem("fin2")
        ub = sem("ub")
        pairs = [(g, hf) for g in range(G) for hf in range(HALVES)]
        NJ = len(pairs)
        cols = lambda hf: slice(hf * W, hf * W + W)
        block = ctx.enter_context(nc.Block())

        @block.sync
        def _(sp):
            sp.dma_start(w6[:], d["w6"]).then_inc(w_in[0], 16)
            sp.dma_start(rope[:], d["rope"][:, :, 0:W]).then_inc(w_in[1], 16)
            sp.dma_start(gb[:], d["gb"]).then_inc(w_in[1], 16)
            sp.dma_start(dl[:], d["dl"]).then_inc(w_in[1], 16)
            sp.dma_start(seq[:], d["seq"][:, 0:N]).then_inc(w_in[1], 16)
            sp.dma_start(bd[:], d["bd"]).then_inc(w_in[1], 16)
            sp.dma_start(selv[:], d["selv"]).then_inc(w_in[2], 16)
            sp.dma_start(sely[:], d["sely"]).then_inc(w_in[2], 16)
            sp.dma_start(ow[:], d["ow"]).then_inc(w_in[3], 16)
            sp.dma_start(vecs[:], d["vecs"]).then_inc(w_in[3], 16)

        bank = lambda r: ps[:, 4 + r % 4, :]

        @block.tensor
        def _(pe):
            transpose_rows(pe, ln, NR, lambda r: u[:, r, :], bank, ident)
            pe.wait_ge(ln["t_sb"], NR)
            pe.wait_ge(w_in[0], 16)
            pe.wait_ge(w_in[1], 80)

            def project(i, g, hf, out):
                for t in range(2):
                    mm = pe.matmul(out, w6[:, i, t, g * P:g * P + P], uT[:, t, cols(hf)], start=(t == 0), stop=(t == 1))
                return mm
            for n, (g, hf) in enumerate(pairs):
                for i in range(2):
                    if n:
                        pe.wait_ge(ropes, 2 * (2 * (n - 1) + i) + 2)
                    project(2 * i, g, hf, ps[:, 2 * i, 0:W])
                    project(2 * i + 1, g, hf, ps[:, 2 * i + 1, 0:W]).then_inc(pr_ps, 1)
                if n:
                    pe.wait_ge(gate_ready, n)
                project(5, g, hf, ps[:, 5, 0:W]).then_inc(pr_ps, 1)
                if n:
                    pe.wait_ge(vlo, n)
                project(4, g, hf, ps[:, 4, 0:W]).then_inc(pr_ps, 1)
                for i in range(2):
                    pe.wait_ge(rot_ready, 2 * n + i + 1)
                    if n:
                        pe.wait_ge([qr_ready, kk_ready][i], n)
                    pe.matmul(ps[:, 6 + i, 0:W], bd[:, i, g, :], rot[:, i, :], start=True, stop=True).then_inc(r_ps, 1)
            pe.wait_ge(qr_ready, NJ)
            pe.wait_ge(kk_ready, NJ)
            pe.wait_ge(vlo, NJ)
            pe.wait_ge(selr, 1)

            def broadcast_v(j, g, dd):
                for hf in range(HALVES):
                    out = ps[:, 2 * (j % 2) + hf, 0:W]
                    pe.matmul(out, selvr[:, dd, :], vh[:, g, cols(hf)], start=True, stop=False)
                    mm = pe.matmul(out, selvr[:, dd, :], vl[:, g, cols(hf)], start=False, stop=True)
                mm.then_inc(v_ps, 1)

            def sum_r(j, g, dd):
                k, e = dd // 4, dd % 4
                for hf in range(HALVES):
                    mm = pe.matmul(ps[32 * k:32 * k + 32, 4 + 2 * g + hf, 0:W], sely[:, e, :], qm[:, j % 2, cols(hf)],
                                   start=(e == 0), stop=(e == 3), skip_group_check=True)
                mm.then_inc(y_ps, 1)

            steps = [(g, dd) for g in range(G) for dd in range(16)]
            for j, (g, dd) in enumerate(steps):
                if j >= 2:
                    pe.wait_ge(kv_ready, j - 1)
                broadcast_v(j, g, dd)
                if j >= 2:
                    pe.wait_ge(qm_ready, j - 1)
                    sum_r(j - 2, *steps[j - 2])
            for j in range(30, 32):
                pe.wait_ge(qm_ready, j + 1)
                sum_r(j, *steps[j])
            pe.wait_ge(y_sb, G)
            pe.wait_ge(w_in[3], 32)
            for r in range(NR):
                if r >= 4:
                    pe.wait_ge(h_ready, r - 3)
                for g in range(G):
                    mm = pe.matmul(ps[:, r % 4, 0:DM], yT[:, g, r * P:r * P + P], ow[:, g, :], start=(g == 0), stop=(g == 1))
                mm.then_inc(o_ps, 1)

        @block.scalar
        def _(act):
            norm_sqrt(act, ln, rs)
            copy_rows(act, ln, NR, bank, uT)
            act.wait_ge(w_in[1], 80)
            act.activation(dec[:], dl[:], ACT.Sigmoid).then_inc(dec_ready, 1)
            act.wait_ge(w_in[2], 32)
            act.activation(selvr[:, :, :], selv[:, :, :], ACT.Copy).then_inc(selr, 1)
            for n, (g, hf) in enumerate(pairs):
                act.wait_ge(pr_ps, 4 * n + 3)
                if n >= 2:
                    act.wait_ge(kk_ready, n - 1)
                act.activation(gate[:, n % 2, :], ps[:, 5, 0:W], ACT.Sigmoid, bias=gb[:, g:g + 1]).then_inc(gate_ready, 1)
                act.wait_ge(pr_ps, 4 * n + 4)
                act.activation(vh[:, g, cols(hf)], ps[:, 4, 0:W], ACT.Copy).then_inc(vhi, 1)
                act.wait_ge(r_ps, 2 * n + 1)
                act.activation(qr[:, g, cols(hf)], ps[:, 6, 0:W], ACT.Copy).then_inc(qr_ready, 1)
            for g in range(G):
                act.wait_ge(y_ps, 16 * g + 16)
                act.activation(yT[:, g, :].rearrange("p (a n) -> p a n", a=HALVES), ps[:, 4 + 2 * g:4 + 2 * g + HALVES, 0:W], ACT.Copy).then_inc(y_sb, 1)
            norm_sqrt(act, lo, rsc)

        @block.vector
        def _(dve):
            norm_vector(dve, ln, NR, lambda r: x1[:, RT + r, :], lambda r: u[:, r, :], st6, mv, rs)
            dve.wait_ge(w_in[1], 80)
            dve.wait_ge(dec_ready, 1)
            for g in range(G):
                dve.tensor_scalar(dect[:, g, :], seq[:, :], dec[:, g:g + 1], None, ALU.mult).then_inc(dect_ready, 1)
            for n, (g, hf) in enumerate(pairs):
                for i in range(2):
                    dve.wait_ge(pr_ps, 4 * n + i + 1)
                    if n:
                        dve.wait_ge(rot_ready, 2 * (n - 1) + i + 1)
                    dve.tensor_tensor(t1[:, i, :], ps[:, 2 * i, 0:W], rope[:, 0, :], ALU.mult).then_inc(ropes, 1)
                    dve.tensor_tensor(t2[:, i, :], ps[:, 2 * i + 1, 0:W], rope[:, 1, :], ALU.mult).then_inc(ropes, 1)
                dve.wait_ge(vhi, n + 1)
                dve.tensor_tensor(vl[:, g, cols(hf)], ps[:, 4, 0:W], vh[:, g, cols(hf)].bitcast(F32), ALU.subtract).then_inc(vlo, 1)
                dve.wait_ge(r_ps, 2 * n + 2)
                dve.wait_ge(gate_ready, n + 1)
                dve.scalar_tensor_tensor(out=kk[:, g, cols(hf)], in0=ps[:, 7, 0:W], scalar=0.25, in1=gate[:, n % 2, :],
                                         op0=ALU.mult, op1=ALU.mult).then_inc(kk_ready, 1)
            dve.wait_ge(kk_ready, NJ)
            dve.wait_ge(dect_ready, G)
            for j in range(32):
                g = j // 16
                if j >= 2:
                    dve.wait_ge(m_done, j - 1)
                dve.wait_ge(v_ps, j + 1)
                dve.tensor_tensor(kv[:, j % 2, :].rearrange("p (a n) -> p a n", a=HALVES), ps[:, 2 * (j % 2):2 * (j % 2) + HALVES, 0:W],
                                  kk[:, g, :].rearrange("p (a n) -> p a n", a=HALVES), ALU.mult).then_inc(kv_ready, 1)
                dve.wait_ge(kv_ready, j + 1)
                if j >= 2:
                    dve.wait_ge(qm_ready, j - 1)
                dve.tensor_tensor_scan(M[:, j % 2, :], dect[:, g, :], kv[:, j % 2, :], 0.0, ALU.mult, ALU.add).then_inc(m_done, 1)
            dve.wait_ge(ub, 1)
            for r in range(NR):
                dve.wait_ge(o_ps, r + 1)
                dve.tensor_tensor(u[:, r, :], ps[:, r % 4, 0:DM], u[:, r, :], ALU.add).then_inc(h_ready, 1)
            norm_vector(dve, lo, NR, lambda r: u[:, r, :], lambda r: u[:, r, :], st6c, mvc, rsc, ready=lambda r: dve.wait_ge(h_ready, r + 1))
            dve.wait_ge(lo["normed"], NR)
            dve.tensor_tensor(u[:, :, :], u[:, :, :], vecs[:, 1, :].unsqueeze(1).to_broadcast([P, NR, DM]), ALU.mult).then_inc(scaled, 1)
            dve.wait_ge(scaled, 1)
            dve.wait_ge(fin, 1)
            dve.tensor_tensor(x1[:, RT:, :], u[:, :, :], x1[:, RT:, :], ALU.add).then_inc(fin, 1)
            dve.wait_ge(fin, 2)

        @block.gpsimd
        def _(pool):
            for j in range(2 * NJ):
                pool.wait_ge(ropes, 2 * j + 2)
                if j >= 2:
                    pool.wait_ge(r_ps, j - 1)
                pool.tensor_tensor(rot[:, j % 2, :], t1[:, j % 2, :], t2[:, j % 2, :], ALU.add).then_inc(rot_ready, 1)
            pool.wait_ge(qr_ready, NJ)
            for j in range(32):
                pool.wait_ge(m_done, j + 1)
                if j >= 2:
                    pool.wait_ge(y_ps, j - 1)
                pool.tensor_tensor(qm[:, j % 2, :], M[:, j % 2, :], qr[:, j // 16, :], ALU.mult).then_inc(qm_ready, 1)
            pool.wait_ge(w_in[3], 32)
            pool.tensor_tensor(u[:, :, :], u[:, :, :], vecs[:, 0, :].unsqueeze(1).to_broadcast([P, NR, DM]), ALU.add).then_inc(ub, 1)
            pool.tensor_tensor(x1[:, RT:, :], x1[:, RT:, :], vecs[:, 2, :].unsqueeze(1).to_broadcast([P, NR, DM]), ALU.add).then_inc(fin, 1)


def experts(nc, nb, top, d, out):
    x2, ident = top["x1"], top["ident"]
    NR = nb * RT
    N = nb * ROWS
    HALVES = max(1, N // 512)
    W = N // HALVES
    E = 8
    ctx = ExitStack()
    with ctx:
        def sb(name, shape, dt=F32):
            return ctx.enter_context(nc.sbuf_tensor(name, shape, dt))

        def sem(name):
            return ctx.enter_context(nc.semaphore(name))

        w = sb("w", [P, NR, DM])
        wT = sb("wT", [P, 2, N])
        gw = sb("gw", [P, 2, E])
        sw12 = sb("sw12", [P, 2, 2, 512])
        sw3 = sb("sw3", [P, 4, DM])
        we = sb("we", [P, 2, 3, 2, DM])
        be = sb("be", [P, 2, 3, 2])
        lg = sb("lg", [P, NR, E])
        mx = sb("mx", [P, NR])
        sm = sb("sm", [P, NR])
        iota = sb("iota", [P, E])
        cand = sb("cand", [P, NR, E])
        sc2 = sb("sc2", [P, NR, E])
        hot = sb("hot", [P, NR, E])
        wm = sb("wm", [P, NR, 2 * E])
        wmT = sb("wmT", [2 * E, N])
        bc = sb("bc", [P, 2, 2, N])
        t1 = sb("e_t1", [P, 2, N])
        hT = sb("hT", [P, 2, N])
        t3 = sb("e_t3", [P, 2, N])
        t3m = sb("e_t3m", [P, 2, N])
        yT = sb("y_T", [P, 2, N])
        zs = sb("zs", [P, 2, N])
        zT = sb("zT", [P, 4, N])
        st6, mv, rs = sb("st6d", [P, NR, 6]), sb("mvd", [P, NR, 2]), sb("rsd", [P, NR])
        ps = ctx.enter_context(nc.psum_tensor("ps3", [P, 8, 512], F32))
        g_in, s_in = sem("g_in"), sem("s_in")
        e_in = [sem(f"e_in{i}") for i in range(2)]
        bc_in = [sem(f"bc_in{i}") for i in range(2)]
        ln = norm_sems(sem, "n4")
        lg_ps, chain, ex, wm_ready, wm_ps, wm_sb, wm_out = (sem(x) for x in ("lg_ps", "chain", "ex", "wm_ready", "wm_ps", "wm_sb", "wm_out"))
        z_ps, z_silu, z_ready = sem("z_ps"), sem("z_silu"), sem("z_ready")
        h_ps, t1_ready, h_ready, x3_ps, t3_ready, t3m_ready, x2_ps, xy_ready, y_ready = (sem("e_" + x) for x in (
            "h_ps", "t1_ready", "h_ready", "x3_ps", "t3_ready", "t3m_ready", "x2_ps", "xy_ready", "y_ready"))
        f_ps, added, f_ready, done = sem("f_ps"), sem("x_z_added"), sem("f_ready"), sem("done3")
        bank = lambda r: ps[:, 4 + r % 4, :]
        jobs = [(m, hf) for m in range(2) for hf in range(HALVES)]
        NJ = len(jobs)
        cols = lambda hf: slice(hf * W, hf * W + W)
        block = ctx.enter_context(nc.Block())

        @block.sync
        def _(sp):
            sp.dma_start(gw[:], d["gw"]).then_inc(g_in, 16)
            sp.dma_start(iota[:], d["iota"]).then_inc(g_in, 16)
            sp.dma_start(sw12[:], d["sw12"]).then_inc(s_in, 16)
            sp.dma_start(sw3[:], d["sw3"]).then_inc(s_in, 16)
            for e in range(2):
                sp.dma_start(we[:, e, :, :, :], d["we"][e]).then_inc(e_in[e], 16)
                sp.dma_start(be[:, e, :, :], d["be"][e]).then_inc(e_in[e], 16)
            sp.wait_ge(wm_sb, NR)
            sp.dma_start(d["wm_rows"][:, 0:N], wmT[:, :]).then_inc(wm_out, 16)
            sp.wait_ge(wm_out, 16)

            def load_bc(slot, e):
                for k in range(2):
                    sp.dma_start(bc[:, slot, k, :], d["wm_rows"][bass.ds(e + k * E, 1), 0:N].to_broadcast([P, N])).then_inc(bc_in[slot], 16)

            for e in range(2):
                load_bc(e, e)
            with sp.Fori(0, E // 2 - 1) as i:
                for k in range(2):
                    sp.wait_ge(xy_ready, (i * 2 + k) * NJ + 2 * NJ)
                    sp.dma_start(we[:, k, :, :, :], d["we"][bass.ds(i * 2 + 2 + k, 1)].rearrange("o p a t n -> p (o a) t n")).then_inc(e_in[k], 16)
                    sp.dma_start(be[:, k, :, :], d["be"][bass.ds(i * 2 + 2 + k, 1)].rearrange("o p a m -> p (o a) m")).then_inc(e_in[k], 16)
                    load_bc(k, i * 2 + 2 + k)
            sp.wait_ge(f_ready, NR)
            sp.dma_start(out, w[:, :, :]).then_inc(done, 16)
            sp.wait_ge(done, 16)

        @block.tensor
        def _(pe):
            transpose_rows(pe, ln, NR, lambda r: w[:, r, :], bank, ident)
            pe.wait_ge(ln["t_sb"], NR)
            pe.wait_ge(g_in, 32)
            for r in range(NR):
                for t in range(2):
                    mm = pe.matmul(ps[:, 0, r * E:r * E + E], wT[:, t, r * P:r * P + P], gw[:, t, :], start=(t == 0), stop=(t == 1))
            mm.then_inc(lg_ps, 1)
            pe.wait_ge(s_in, 32)
            n = 0
            for m in range(4):
                for hf in range(HALVES):
                    if n >= 2:
                        pe.wait_ge(z_ready, n - 1)
                    for a in range(2):
                        for t in range(2):
                            mm = pe.matmul(ps[:, 1 + 2 * (n % 2) + a, 0:W], sw12[:, t, a, m * P:m * P + P], wT[:, t, cols(hf)],
                                           start=(t == 0), stop=(t == 1))
                    mm.then_inc(z_ps, 1)
                    n += 1
            pe.wait_ge(wm_ready, 1)
            for r in range(NR):
                if r >= 2:
                    pe.wait_ge(wm_sb, r - 1)
                pe.transpose(ps[0:2 * E, 6 + r % 2, 0:P], wm[:, r, :], ident[:, :]).then_inc(wm_ps, 1)
            pe.wait_ge(z_ready, 4 * HALVES)
            pe.wait_ge(wm_sb, NR)

            def layer(slot, a, src, m, hf, out):
                for t in range(2):
                    mm = pe.matmul(out, we[:, slot, a, t, m * P:m * P + P], src[:, t, cols(hf)], start=(t == 0), stop=(t == 1))
                return mm

            def expert(e, slot, first):
                pe.wait_ge(e_in[slot], first)
                base = e * NJ
                for n, (m, hf) in enumerate(jobs):
                    pe.wait_ge(t1_ready, base + n + 1)
                    layer(slot, 0, wT, m, hf, ps[:, n % 2, 0:W]).then_inc(h_ps, 1)
                    pe.wait_ge(t3_ready, base + n + 1)
                    layer(slot, 2, wT, m, hf, ps[:, 2 + n % 2, 0:W]).then_inc(x3_ps, 1)
                pe.wait_ge(h_ready, base + 2 * NJ)
                for n, (m, hf) in enumerate(jobs):
                    pe.wait_ge(xy_ready, base + n + 1)
                    layer(slot, 1, hT, m, hf, ps[:, 4 + n, 0:W]).then_inc(x2_ps, 1)

            pe.sem_inc(x2_ps, 1)
            with pe.Fori(0, E // 2) as i:
                for k in range(2):
                    expert(i * 2 + k, k, i * 32 + 32)
            pe.wait_ge(y_ready, NJ * E + NJ)
            for r in range(NR):
                if r >= 4:
                    pe.wait_ge(f_ready, r - 3)
                for t in range(4):
                    pe.matmul(ps[:, r % 4, 0:DM], zT[:, t, r * P:r * P + P], sw3[:, t, :], start=(t == 0), stop=(t == 3))
                for t in range(2):
                    mm = pe.transpose(ps[:, 4 + r % 4, t * P:t * P + P], yT[:, t, r * P:r * P + P], ident[:, :])
                mm.then_inc(f_ps, 1)

        @block.scalar
        def _(act):
            norm_sqrt(act, ln, rs)
            copy_rows(act, ln, NR, bank, wT)
            act.wait_ge(chain, 2)
            act.activation(lg[:, :, :], lg[:, :, :], ACT.Exp).then_inc(ex, 1)
            n = 0
            for m in range(4):
                for hf in range(HALVES):
                    act.wait_ge(z_ps, n + 1)
                    if n >= 2:
                        act.wait_ge(z_ready, n - 1)
                    act.activation(zs[:, n % 2, 0:W], ps[:, 1 + 2 * (n % 2), 0:W], ACT.Silu).then_inc(z_silu, 1)
                    n += 1
            for r in range(NR):
                act.wait_ge(wm_ps, r + 1)
                act.activation(wmT[:, r * P:r * P + P], ps[0:2 * E, 6 + r % 2, 0:P], ACT.Copy).then_inc(wm_sb, 1)
            act.sem_inc(h_ready, NJ)

            def expert(e, k, loads):
                act.wait_ge(e_in[k], loads)
                for n, (m, hf) in enumerate(jobs):
                    act.wait_ge(t1_ready, e * NJ + n + 3)
                    act.wait_ge(x2_ps, e * NJ + 1)
                    act.activation(hT[:, m, cols(hf)], t1[:, m, cols(hf)], ACT.Silu, bias=be[:, k, 0, m:m + 1]).then_inc(h_ready, 1)

            with act.Fori(0, E // 2) as i:
                for k in range(2):
                    expert(i * 2 + k, k, i * 32 + 32)

        @block.vector
        def _(dve):
            norm_vector(dve, ln, NR, lambda r: x2[:, RT + r, :], lambda r: w[:, r, :], st6, mv, rs)
            count = [0]

            def link(ins):
                count[0] += 1
                ins.then_inc(chain, 1)
                dve.wait_ge(chain, count[0])

            rows = lambda t: t[:, :].unsqueeze(2).to_broadcast([P, NR, E])
            dve.wait_ge(lg_ps, 1)
            logits = ps[:, 0, 0:NR * E].rearrange("p (r e) -> p r e", e=E)
            link(dve.tensor_reduce(mx[:, :], logits, AX.X, ALU.max))
            link(dve.tensor_tensor(lg[:, :, :], logits, rows(mx), ALU.subtract))
            dve.wait_ge(ex, 1)
            link(dve.tensor_reduce(sm[:, :], lg[:, :, :], AX.X, ALU.add))
            link(dve.reciprocal(sm[:, :], sm[:, :]))
            link(dve.tensor_tensor(lg[:, :, :], lg[:, :, :], rows(sm), ALU.mult))
            order = iota[:, :].unsqueeze(1).to_broadcast([P, NR, E])
            score = lg
            for k in range(2):
                link(dve.tensor_reduce(mx[:, :], score[:, :, :], AX.X, ALU.max))
                link(dve.tensor_tensor(hot[:, :, :], score[:, :, :], rows(mx), ALU.is_ge))
                link(dve.scalar_tensor_tensor(out=cand[:, :, :], in0=hot[:, :, :], scalar=-float(E), in1=order, op0=ALU.mult, op1=ALU.add))
                link(dve.tensor_reduce(mx[:, :], cand[:, :, :], AX.X, ALU.min))
                one = wm[:, :, E:2 * E] if k == 0 else hot[:, :, :]
                link(dve.tensor_tensor(one, cand[:, :, :], rows(mx), ALU.is_equal))
                if k == 0:
                    link(dve.scalar_tensor_tensor(out=sc2[:, :, :], in0=one, scalar=-4.0, in1=lg[:, :, :], op0=ALU.mult, op1=ALU.add))
                    score = sc2
            link(dve.tensor_tensor(wm[:, :, E:2 * E], wm[:, :, E:2 * E], hot[:, :, :], ALU.add))
            dve.tensor_tensor(wm[:, :, 0:E], wm[:, :, E:2 * E], lg[:, :, :], ALU.mult).then_inc(wm_ready, 1)
            n = 0
            for m in range(4):
                for hf in range(HALVES):
                    dve.wait_ge(z_silu, n + 1)
                    dve.tensor_tensor(zT[:, m, cols(hf)], ps[:, 2 + 2 * (n % 2), 0:W], zs[:, n % 2, 0:W], ALU.mult).then_inc(z_ready, 1)
                    n += 1
            dve.memset(yT[:, :, :], 0.0).then_inc(t1_ready, 2)
            dve.sem_inc(t3_ready, 2)
            dve.sem_inc(t3m_ready, NJ)
            dve.sem_inc(xy_ready, NJ)

            def expert(e, k, loads):
                base = e * NJ
                dve.wait_ge(bc_in[k], loads)
                dve.wait_ge(e_in[k], loads)
                for n, (m, hf) in enumerate(jobs):
                    dve.wait_ge(h_ps, base + n + 1)
                    dve.wait_ge(h_ready, base + n + 1)
                    dve.tensor_tensor(t1[:, m, cols(hf)], ps[:, n % 2, 0:W], bc[:, k, 0, cols(hf)], ALU.mult).then_inc(t1_ready, 1)
                    dve.wait_ge(x3_ps, base + n + 1)
                    dve.wait_ge(t3m_ready, base + n + 1)
                    dve.tensor_tensor(t3[:, m, cols(hf)], ps[:, 2 + n % 2, 0:W], bc[:, k, 0, cols(hf)], ALU.mult).then_inc(t3_ready, 1)
                    dve.wait_ge(t3_ready, base + n + 3)
                    dve.wait_ge(y_ready, base + n + 1)
                    dve.scalar_tensor_tensor(out=t3m[:, m, cols(hf)], in0=t3[:, m, cols(hf)], scalar=be[:, k, 2, m:m + 1],
                                             in1=bc[:, k, 1, cols(hf)], op0=ALU.add, op1=ALU.mult).then_inc(t3m_ready, 1)
                for n, (m, hf) in enumerate(jobs):
                    dve.wait_ge(x2_ps, base + n + 2)
                    dve.wait_ge(t3m_ready, base + NJ + n + 1)
                    dve.scalar_tensor_tensor(out=t3m[:, m, cols(hf)], in0=ps[:, 4 + n, 0:W], scalar=be[:, k, 1, m:m + 1],
                                             in1=t3m[:, m, cols(hf)], op0=ALU.add, op1=ALU.mult).then_inc(xy_ready, 1)

            with dve.Fori(0, E // 2) as i:
                for k in range(2):
                    expert(i * 2 + k, k, i * 32 + 32)
            for r in range(NR):
                dve.wait_ge(f_ps, r + 1)
                dve.tensor_tensor(w[:, r, :], ps[:, r % 4, 0:DM], x2[:, RT + r, :], ALU.add).then_inc(added, 1)
                dve.wait_ge(added, r + 1)
                dve.tensor_tensor(w[:, r, :], w[:, r, :], ps[:, 4 + r % 4, 0:DM], ALU.add).then_inc(f_ready, 1)

        @block.gpsimd
        def _(pool):
            pool.wait_ge(t1_ready, 1)
            pool.sem_inc(y_ready, NJ)
            with pool.Fori(0, E) as e:
                for n, (m, hf) in enumerate(jobs):
                    pool.wait_ge(xy_ready, e * NJ + NJ + n + 1)
                    pool.wait_ge(y_ready, e * NJ + n + 1)
                    pool.tensor_tensor(yT[:, m, cols(hf)], yT[:, m, cols(hf)], t3m[:, m, cols(hf)], ALU.add).then_inc(y_ready, 1)


def build(nc, nb, d, x1_out):
    top_ctx = ExitStack()
    with top_ctx:
        def sb(name, shape, dt=F32):
            return top_ctx.enter_context(nc.sbuf_tensor(name, shape, dt))
        x1 = sb("x1", [P, (nb + 1) * RT, DM])
        top = dict(x1=x1, ident=sb("ident_sb", [P, P]), ones=sb("ones_sb", [P, 1]))
        cross_attention(nc, nb, top, d)
        recurrence(nc, nb, top, d)
        experts(nc, nb, top, d, x1_out)


NB = 4
SCRATCH = {"xnT": (NB, P, 2, ROWS), "wk_split": (HEADS // 2, P, 4, P), "wv_split": (NG, P, 4, QH * DH), "wm_rows": (16, NB * ROWS)}


def layout(I, nb):
    import numpy as np

    A = {}
    rep = lambda a, shape: np.broadcast_to(a, shape)
    fold = lambda a: a.reshape(2, P, -1).transpose(1, 0, 2)
    x, ctx = I["x"][:nb], I["ctx_768"][:nb]
    A["x"] = x.reshape(nb * RT, P, DM).transpose(1, 0, 2)
    t = ctx.transpose(0, 2, 1)
    c = np.stack([t[:, :P], np.concatenate([t[:, P:], t[:, P:]], 1)], 2)
    A["ctx"] = c.reshape(nb, P, 2, NC, CH).transpose(0, 3, 1, 2, 4)
    rows = lambda W: np.stack([W[:P], np.concatenate([W[P:], W[P:]], 0)], 1)
    A["wk"] = rows(I["L0_xattn_Wk"]).reshape(P, 2048)
    A["wv"] = rows(I["L0_xattn_Wv"]).reshape(P, 2048)
    A["wq"] = I["L0_xattn_Wq"].reshape(2, P, HEADS // 2, P).transpose(2, 1, 0, 3)
    wo = I["L0_xattn_Wo"].reshape(HEADS // 2, 2, 1, DH, DM)
    A["wo"] = rep(wo, (HEADS // 2, 2, 2, DH, DM)).reshape(HEADS // 2, 2, P, DM).transpose(0, 2, 1, 3)
    A["bo"] = rep(I["L0_xattn_bo"], (P, DM))
    A["ident"] = np.eye(P, dtype=np.float32)
    sw = np.arange(DM) ^ 1
    q, k, v, g = (I["L0_attn_" + n] for n in ("q_w", "k_w", "v_w", "g_w"))
    A["w6"] = np.stack([fold(m.T) for m in (q, q[sw], k, k[sw], v, g)], 1)
    f = np.float32
    inv = (f(1.0) / f(10000.0) ** (np.arange(8, dtype=f) / f(8))).astype(f)
    ang = np.arange(ROWS, dtype=f)[:, None] * inv[None, :]
    cos, sin = np.cos(ang).astype(f).T, np.sin(ang).astype(f).T
    dd = np.arange(P) % 16
    A["rope"] = np.stack([np.tile(cos[dd // 2], (1, 2)), np.tile(sin[dd // 2], (1, 2)) * np.where(dd % 2, 1, -1).astype(f)[:, None]], 1)
    bd = np.zeros((P, 2, 2, P), f)
    for i, n in enumerate(("Wq", "Wk")):
        for h in range(16):
            s = slice(16 * (h % 8), 16 * (h % 8) + 16)
            bd[s, i, h // 8, s] = I["L0_attn_" + n][h].T
    A["bd"] = bd
    A["gb"] = I["L0_attn_g_b"].reshape(2, P).T
    A["dl"] = I["L0_attn_base_decay_logits"].reshape(2, P).T
    A["seq"] = rep((np.arange(NB * ROWS) % ROWS != 0).astype(f), (P, NB * ROWS))
    p = np.arange(P)
    same = (p[:, None] // 16 == p[None, :] // 16)
    A["selv"] = np.stack([(same & (p[:, None] % 16 == e)).astype(f) for e in range(16)], 1)
    j = np.arange(32)
    A["sely"] = np.stack([((p[:, None] // 16 == j[None, :] // 4) & (j[None, :] % 4 == e)).astype(f) for e in range(4)], 1)
    order = 16 * (p % 32 // 4) + 4 * (p // 32) + p % 4
    A["ow"] = np.stack([I["L0_attn_out_w"].T[P * g + order] for g in range(2)], 1)
    A["vecs"] = np.stack([rep(I["L0_attn_" + n], (P, DM)) for n in ("out_b", "ln_g", "ln_b")], 1)
    A["gw"] = fold(I["L0_ffn_gate_w"].T)
    A["iota"] = rep(np.arange(8, dtype=f), (P, 8))
    A["we"] = np.stack([np.stack([fold(I["L0_ffn_" + n][e].T) for n in ("w1", "w2", "w3")], 1) for e in range(8)], 0)
    A["be"] = np.stack([I["L0_ffn_" + n].reshape(8, 2, P).transpose(0, 2, 1) for n in ("b1", "b2", "b3")], 2)
    A["sw12"] = np.stack([fold(I["L0_ffn_" + n].T) for n in ("sw1", "sw2")], 2)
    A["sw3"] = I["L0_ffn_sw3"].T.reshape(4, P, DM).transpose(1, 0, 2)
    return {n: np.ascontiguousarray(a, dtype=f) for n, a in A.items()}


def kernel(**inputs):
    import numpy as np
    from concourse import bacc
    from concourse.bass_utils import run_bass_kernel_spmd

    arrays = layout({n: np.asarray(a) for n, a in inputs.items()}, NB)
    nc = bacc.Bacc("TRN2", target_bir_lowering=False, num_devices=1)
    d = {n: nc.dram_tensor("in_" + n, a.shape, F32, kind="ExternalInput").ap() for n, a in arrays.items()}
    d |= {n: nc.dram_tensor(n, shape, F32).ap() for n, shape in SCRATCH.items()}
    out = nc.dram_tensor("out_0", (P, NB * RT, DM), F32, kind="ExternalOutput").ap()
    build(nc, NB, d, out)
    r = run_bass_kernel_spmd(nc, [{"in_" + n: a for n, a in arrays.items()}], core_ids=[0])
    return np.ascontiguousarray(r.results[0]["out_0"].transpose(1, 0, 2).reshape(NB, ROWS, DM))
```

```python
import concourse.bass as bass
from concourse import mybir
from contextlib import ExitStack

F32 = mybir.dt.float32
F32R = mybir.dt.float32r
ALU = mybir.AluOpType
ACT = mybir.ActivationFunctionType
AX = mybir.AxisListType

P = 128
DM = 256
ROWS = 256
RT = ROWS // P
KEYS = 4096
CTX = 192
HEADS = 16
DH = 64
CH = 512
NC = KEYS // CH
KT = CH // P
QH = 4
NG = HEADS // QH
EPS = 1e-5
MROW = 64
M2 = 96


def cross_attention(nc, nb, top, d):
    ctx = ExitStack()
    with ctx:
        def sb(name, shape, dt=F32):
            return ctx.enter_context(nc.sbuf_tensor(name, shape, dt))

        def sem(name):
            return ctx.enter_context(nc.semaphore(name))

        x1, ident, ones = top["x1"], top["ident"], top["ones"]
        NR = nb * RT
        C = sb("C", [P, 3, KEYS], F32R)
        craw = sb("craw", [P, 2, CH])
        KH = sb("KH", [P, 2, NC, CH], F32R)
        KL = sb("KL", [P, 2, NC, CH], F32R)
        V = sb("V", [P, NC * KT, QH * DH])
        PR = sb("PR", [P, 2, KT * ROWS])
        acc = sb("acc", [P, 2, KT * ROWS])
        wk = sb("wk", [P, 2, 4, P], F32R)
        wv = sb("wv", [P, 4, QH * DH], F32R)
        wq = sb("wq", [P, 2, 2, P])
        wo = sb("wo", [P, 2, 2, DM])
        Q1 = sb("Q1", [P, 2, 2, ROWS], F32R)
        Q2 = sb("Q2", [P, 2, 2, ROWS], F32R)
        qs = sb("qs", [P, ROWS])
        qh = sb("qh", [P, ROWS], F32R)
        amx = sb("amx", [P, 2, RT, NC])
        nmx = sb("nmx", [P, 2, RT])
        accf = sb("accf", [P, 2, ROWS])
        Ot = sb("Ot", [P, 2, ROWS])
        rl = sb("rl", [P, 2 * RT])
        zero = sb("zero", [P, 1])
        warm = sb("warm", [P, 1])
        xnT = sb("xnT_sb", [P, 2, ROWS])
        bo = sb("bo_sb", [P, DM])
        st6, mv, rs = sb("st6", [P, NR, 6]), sb("mv", [P, NR, 2]), sb("rs", [P, NR])

        flat = lambda t: t.rearrange("p a n -> p (a n)")
        xin = flat(PR[:, :, :]).rearrange("p (r n) -> p r n", n=DM)[:, 0:NR, :]
        raw = flat(V[:, :, :])
        rawk, rawv = raw[:, 0:2048], raw[:, 2048:4096]
        xnT_all = raw[:, 6144:6144 + 2 * nb * ROWS].rearrange("p (t n) -> p t n", t=2)
        kh = KH[:, :, NC // 2:, :].rearrange("p s c n -> p s (c n)")
        kl = KL[:, :, NC // 2:, :].rearrange("p s c n -> p s (c n)")
        crawb = [craw[:, :, :]] + [acc[:, h, :].rearrange("p (a n) -> p a n", a=2) for h in range(2)]
        BUFS = len(crawb)

        ps = ctx.enter_context(nc.psum_tensor("ps1", [P, 8, 512], F32))
        psS, psK, psA, psO, psV, psM = ps[:, 0:2, :], ps[:, 2, :], ps[:, 3:5, :], ps[:, 5, :], ps[:, 6, :], ps[:, 7, :]

        x_in, c_in = sem("x_in"), sem("c_in")
        wkraw_in, wvraw_in, wk_st, wv_st = sem("wkraw_in"), sem("wvraw_in"), sem("wk_st"), sem("wv_st")
        whi, wlo, xst, xn_in = sem("whi"), sem("wlo"), sem("xst"), sem("xn_in")
        init, filled = sem("init"), sem("filled")
        craw_in = [sem(f"craw_in{i}") for i in range(BUFS)]
        chi, cready = sem("chi"), sem("cready")
        wk_in = [sem(f"wk_in{i}") for i in range(2)]
        wq_in = [sem(f"wq_in{i}") for i in range(2)]
        wo_in = [sem(f"wo_in{i}") for i in range(2)]
        wv_in = sem("wv_in")
        k_ps, k_hi, k_lo = sem("k_ps"), sem("k_hi"), sem("k_lo")
        a_ps, a_max = sem("a_ps"), sem("a_max")
        s_ps, p_ready, pv_done = sem("s_ps"), sem("p_ready"), sem("pv_done")
        acc_done, fold_done = sem("acc_done"), sem("fold_done")
        o_sb = sem("o_sb")
        l_ps, rl_ready, out_ps, x_added = sem("l_ps"), sem("rl_ready"), sem("out_ps"), sem("x_added")
        q_ps, q_sb, q_hi, q_ready = sem("q_ps"), sem("q_sb"), sem("q_hi"), sem("q_ready")
        m_ready, m_ps, m_row = sem("m_ready"), sem("m_ps"), sem("m_row")
        v_ps, v_sb = sem("v_ps"), sem("v_sb")
        ln = norm_sems(sem, "n1")

        HS = 2 * 2 * NC
        V_JOB = {}
        for u in range(2 * NC):
            t = max(18 + u, 16 + 2 * u)
            V_JOB[t % HS] = (u, t < HS)
        V_FIRST = sum(late for _, late in V_JOB.values())

        REFRESH = {(4 if k < 5 else 8) + 2 * k: k for k in range(NC)}

        def loops(eng, quad):
            if nb > 1:
                with eng.Fori(0, nb - 1) as b:
                    with eng.Fori(0, NG - 1) as g:
                        quad(b * NG + g, b, g, False, False)
                    quad(b * NG + (NG - 1), b, NG - 1, True, False)
            with eng.Fori(0, NG - 1) as g:
                quad(g + (nb - 1) * NG, nb - 1, g, False, False)
            quad(nb * NG - 1, nb - 1, NG - 1, False, True)

        tail_bank = lambda h: [psK, psV][h]

        def banks_of(h, more):
            return psA if h == 1 and not more else psS

        block = ctx.enter_context(nc.Block())

        @block.sync
        def _(sp):
            def load_ctx(b, c, buf):
                sp.dma_start(crawb[buf], d["ctx"][bass.ds(b, 1), c].rearrange("o p t n -> p (o t) n")).then_inc(craw_in[buf], 16)

            def load_wk(p, slot):
                sp.dma_start(wk[:, slot, :, :].bitcast(F32), d["wk_split"][bass.ds(p, 1)].rearrange("o p t m -> p (o t) m")).then_inc(wk_in[slot], 16)

            def load_wq(p, slot):
                sp.dma_start(wq[:, slot, :, :], d["wq"][bass.ds(p, 1)].rearrange("o p t m -> p (o t) m")).then_inc(wq_in[slot], 16)

            def load_wo(p, slot):
                sp.dma_start(wo[:, slot, :, :], d["wo"][bass.ds(p, 1)].rearrange("o p h m -> p (o h) m")).then_inc(wo_in[slot], 16)

            def load_wv(g):
                sp.dma_start(wv[:].bitcast(F32), d["wv_split"][bass.ds(g, 1)].rearrange("o p t m -> p (o t) m")).then_inc(wv_in, 16)

            def load_xnT(b):
                sp.dma_start(xnT[:], d["xnT"][bass.ds(b, 1)].rearrange("o p t n -> p (o t) n")).then_inc(xn_in, 16)

            sp.dma_start(xin, d["x"]).then_inc(x_in, 16)
            sp.dma_start(rawk, d["wk"]).then_inc(wkraw_in, 16)
            load_ctx(0, 0, 0)
            sp.dma_start(ident[:], d["ident"]).then_inc(c_in, 16)
            sp.dma_start(rawv, d["wv"]).then_inc(wvraw_in, 16)
            load_ctx(0, 1, 1)
            load_ctx(0, 2, 2)
            sp.dma_start(bo[:], d["bo"]).then_inc(c_in, 16)
            for p in range(2):
                load_wq(p, p)
            wks = kh.bitcast(F32).rearrange("p s (t h m) -> p s t h m", t=2, h=HEADS // 2)
            wvs = kl.bitcast(F32).rearrange("p s (t g m) -> p s t g m", t=2, g=NG)
            sp.wait_ge(wlo, 1)
            for p in range(2):
                for k in range(2):
                    sp.dma_start(wk[:, p, 2 * k:2 * k + 2, :].bitcast(F32), wks[:, k, :, p, :]).then_inc(wk_in[p], 16)
            for t in range(4):
                sp.dma_start(d["wk_split"][:, :, t, :].rearrange("h p m -> p h m"), wks[:, t // 2, t % 2, :, :]).then_inc(wk_st, 16)
            def load_first_ctx(c):
                sp.wait_ge(cready, c - BUFS + 1)
                load_ctx(0, c, c % BUFS)

            load_first_ctx(BUFS)
            sp.wait_ge(ln["t_sb"], NR)
            sp.dma_start(xnT[:], xnT_all[:, :, 0:ROWS]).then_inc(xn_in, 16)
            sp.wait_ge(wlo, 2)
            for k in range(2):
                sp.dma_start(wv[:, 2 * k:2 * k + 2, :].bitcast(F32), wvs[:, k, :, 0, :]).then_inc(wv_in, 16)
            load_first_ctx(BUFS + 1)
            load_first_ctx(BUFS + 2)
            for t in range(4):
                sp.dma_start(d["wv_split"][:, :, t, :].rearrange("g p m -> p g m"), wvs[:, t // 2, t % 2, :, :]).then_inc(wv_st, 16)
            for b in range(nb):
                sp.dma_start(d["xnT"][b], xnT_all[:, :, b * ROWS:b * ROWS + ROWS]).then_inc(xst, 16)
            load_wo(NC - 1, 1)
            load_wo(0, 0)
            for c in range(BUFS + 3, NC):
                load_first_ctx(c)
            sp.wait_ge(wk_st, 64)
            sp.wait_ge(wv_st, 64)
            sp.wait_ge(xst, 16 * nb)

            def quad(it, b, g, last, final):
                for pi in range(2):
                    p = it * 2 + pi
                    of_next = lambda k: (g * 2 + pi + k) % (HEADS // 2)
                    if not final:
                        sp.wait_ge(k_ps, NC * p + NC)
                        load_wk(of_next(2), pi)
                        sp.wait_ge(q_ps, p + 1)
                        load_wq(of_next(2), pi)
                    if pi == 1 and not final:
                        sp.wait_ge(v_ps, it * 16 + 16)
                        load_wv((g + 1) % NG)
                    if last and pi == 0:
                        sp.wait_ge(q_ps, p + 2)
                        load_xnT(b + 1)
                    if last:
                        for c in (range(0, 6) if pi == 0 else range(6, NC)):
                            sp.wait_ge(cready, b * NC + NC + c)
                            load_ctx(b + 1, c, 0)
                    if not (final and pi == 1):
                        sp.wait_ge(out_ps, 2 * p + 3)
                        load_wo(of_next(1), (pi + 1) % 2)

            loops(sp, quad)

        @block.tensor
        def _(pe):
            bank = lambda r: ps[:, r % 4, :]
            pe.wait_ge(c_in, 32)
            transpose_rows(pe, ln, NR, lambda r: x1[:, RT + r, :], bank, ident)
            pe.wait_ge(ln["t_sb"], NR)

            def split_product(out, stationary, moving):
                for i, (w, c) in enumerate([(0, 0), (0, 1), (2, 0), (1, 2), (3, 2)]):
                    mm = pe.matmul(out, stationary(w, c), moving(w, c), start=(i == 0), stop=(i == 4))
                return mm

            def project_q(slot):
                for t in range(2):
                    mm = pe.matmul(psM[:, 0:ROWS], wq[:, slot, t, :], xnT[:, t, :], start=(t == 0), stop=(t == 1))
                mm.then_inc(q_ps, 1)

            def project_k(slot, c):
                split_product(psK, lambda w, _: wk[:, slot, w, :], lambda _, k: C[:, k, c * CH:c * CH + CH]).then_inc(k_ps, 1)

            def guess(slot, h, c, before):
                for t in range(RT):
                    if before is not None:
                        pe.wait_ge(a_max, before + t - 1)
                    pe.matmul(psA[:, t, :], Q1[:, slot, h, t * P:t * P + P], KH[:, h, c, :],
                              start=True, stop=True).then_inc(a_ps, 1)

            def project_v(u):
                for k in range(2):
                    t = 2 * u + k
                    mm = split_product(psV[:, k * 256:k * 256 + 256], lambda _, c: C[:, c, t * P:t * P + P],
                                       lambda w, _: wv[:, w, :])
                mm.then_inc(v_ps, 1)

            def scores_part(part, slot, h, c, k, start=True, banks=psS):
                out = banks[:, k // 2, (k % 2) * ROWS:(k % 2) * ROWS + ROWS]
                if part == 0:
                    return pe.matmul(out, KH[:, h, c, k * P:k * P + P], Q1[:, slot, h, :], start=start, stop=False, skip_group_check=True)
                return pe.matmul(out, KL[0:M2, h, c, k * P:k * P + P], Q2[0:M2, slot, h, :], start=False, stop=True, skip_group_check=True)

            def scores(slot, h, c, banks):
                for k in range(KT):
                    scores_part(0, slot, h, c, k, banks=banks)
                    mm = scores_part(1, slot, h, c, k, banks=banks)
                mm.then_inc(s_ps, 1)

            def scores_without_max(slot, h):
                for k in range(KT):
                    scores_part(0, slot, h, 0, k, start=(k % 2 == 0))

            def scores_with_max(slot, h):
                for k in range(KT):
                    mm = scores_part(1, slot, h, 0, k)
                mm.then_inc(s_ps, 1)

            def weighted_sum(hd, h, c):
                for k in range(KT):
                    half = k % 2
                    mm = pe.matmul(psO[half * DH:half * DH + DH, h * ROWS:h * ROWS + ROWS], V[:, c * KT + k, hd * DH:hd * DH + DH],
                                   PR[:, h, k * ROWS:k * ROWS + ROWS],
                                   start=(c == 0 and k < 2 and h == 0), stop=(c == NC - 1 and k >= 2), skip_group_check=True)
                mm.then_inc(pv_done, 1)

            def row_sums():
                for h in range(2):
                    for t in range(RT):
                        mm = pe.matmul(psM[:, 2 * h + t:2 * h + t + 1], accf[:, h, t * P:t * P + P], ones[:, 0:1], start=True, stop=True)
                mm.then_inc(l_ps, 1)

            def project_out(slot, h, bank=psM):
                for t in range(RT):
                    mm = pe.matmul(bank[:, t * DM:t * DM + DM], Ot[:, h, t * P:t * P + P], wo[:, slot, h, :], start=True, stop=True)
                mm.then_inc(out_ps, 1)

            def max_row(h):
                for t in range(RT):
                    mm = pe.matmul(psM[MROW:MROW + 1, ROWS + t * P:ROWS + t * P + P], nmx[:, h, t:t + 1], ident[:, :],
                                   start=True, stop=True)
                mm.then_inc(m_ps, 1)

            pe.wait_ge(xn_in, 16)
            pe.wait_ge(wq_in[0], 16)
            project_q(0)
            pe.wait_ge(wk_in[0], 32)
            for c in range(NC):
                pe.wait_ge(cready, c + 1)
                if c > 0:
                    pe.wait_ge(k_lo, 2 * c)
                    pe.wait_ge(k_hi, 4 * c)
                project_k(0, c)
                if c > 0:
                    if c == 1:
                        pe.wait_ge(q_ready, 1)
                    pe.wait_ge(k_hi, 4 * (c - 1) + 3)
                    guess(0, 0, c - 1, 4 * (c - 1) if c > 1 else None)
                if c < V_FIRST:
                    if c == 0:
                        pe.wait_ge(wv_in, 32)
                        pe.wait_ge(wlo, 2)
                    else:
                        pe.wait_ge(v_sb, c)
                    project_v(c)
                if c > 0:
                    pe.wait_ge(k_hi, 4 * (c - 1) + 4)
                    guess(0, 1, c - 1, 4 * (c - 1) + 2)
            pe.wait_ge(filled, 6)
            pe.sem_inc(pv_done, 1)
            pe.sem_inc(out_ps, 1)
            pe.sem_inc(m_ps, 1)
            for half in range(2):
                pe.matmul(psO[half * DH:half * DH + DH, :], V[:, 31, DH:2 * DH], PR[:, 1, 0:2 * ROWS],
                          start=True, stop=False, skip_group_check=True)

            def quad(it, b, g, last, final):
                for t in range(HS):
                    pi, c, h = t // (2 * NC), t % (2 * NC) // 2, t % 2
                    p, T = it * 2 + pi, it * HS + t
                    nslot = (pi + 1) % 2
                    chunk = NC * p + c
                    nchunk = chunk + NC
                    more = not (final and pi == 1)

                    def sum_before():
                        pe.wait_ge(p_ready, T + 1)
                        u = (t - 1) % HS
                        if t > 0 and pi == 0:
                            pe.wait_ge(v_sb, it * 16 + 2 * (u % (2 * NC) // 2) + 2)
                        if t % (2 * NC) == 1:
                            pe.wait_ge(o_sb, p + 1)
                        weighted_sum(u // (2 * NC) * 2 + u % 2, u % 2, u % (2 * NC) // 2)

                    def next_keys():
                        if c == 0:
                            pe.wait_ge(wk_in[nslot], (it + 2 + pi) * 16)
                        if last and pi == 1:
                            pe.wait_ge(cready, b * NC + NC + c + 1)
                        pe.wait_ge(k_lo, 2 * nchunk)
                        project_k(nslot, c)

                    def next_guess(slot, k, n, c):
                        pe.wait_ge(k_hi, 4 * n + k + 3)
                        guess(slot, k, c, 4 * n + 2 * k)

                    def v_job():
                        u, ahead = V_JOB[t]
                        if u == 0:
                            pe.wait_ge(wv_in, (it + 3) * 16)
                        pe.wait_ge(v_sb, (it + ahead) * 16 + u)
                        project_v(u)

                    v_now = t in V_JOB and not (final and V_JOB[t][1])

                    if c == 0 and h == 0:
                        pe.wait_ge(x_added, 4 * p + 4)
                        if more:
                            pe.wait_ge(wq_in[nslot], (it + 1 + pi) * 16)
                            if last and pi == 1:
                                pe.wait_ge(xn_in, (b + 2) * 16)
                            project_q(nslot)
                        next_guess(pi, 0, nchunk - 1, NC - 1)
                        sum_before()
                        next_guess(pi, 1, nchunk - 1, NC - 1)
                        pe.wait_ge(m_ready, 2 * p + 1)
                        if more:
                            pe.wait_ge(q_sb, p + 2)
                        max_row(0)
                        pe.wait_ge(p_ready, T + 1)
                        scores_without_max(pi, 0)
                        if v_now:
                            v_job()
                        pe.wait_ge(m_row, 2 * p + 1)
                        scores_with_max(pi, 0)
                    elif c == 0:
                        if more:
                            next_keys()
                        pe.wait_ge(m_ready, 2 * p + 2)
                        max_row(1)
                        pe.wait_ge(p_ready, T + 1)
                        scores_without_max(pi, 1)
                        pe.wait_ge(m_row, 2 * p + 2)
                        scores_with_max(pi, 1)
                        sum_before()
                    else:
                        pe.wait_ge(k_lo, 2 * chunk + h + 1)
                        pe.wait_ge(p_ready, T + 1 if more or t % (2 * NC) == 2 else T)
                        scores(pi, h, c, banks_of(h, more))
                        if not more:
                            sum_before()
                        elif h == 0:
                            if c == 1:
                                pe.wait_ge(q_ready, p + 2)
                            next_guess(nslot, 0, nchunk - 1, c - 1)
                            sum_before()
                            if v_now:
                                v_job()
                            next_guess(nslot, 1, nchunk - 1, c - 1)
                        else:
                            next_keys()
                            sum_before()
                    if v_now and h == 1:
                        v_job()
                    if c == 2 and h == 0:
                        pe.wait_ge(fold_done, 4 * p + 4)
                        row_sums()
                    if c in (3, 4) and h == 0:
                        pe.wait_ge(rl_ready, p + 1)
                        pe.wait_ge(x_added, 4 * p + 2 * (c - 3) + 4)
                        pe.wait_ge(wo_in[nslot], (it + 1) * 16)
                        project_out(nslot, c - 3)

            loops(pe, quad)
            pairs = nb * HEADS // 2
            pe.wait_ge(p_ready, pairs * 2 * NC + 1)
            weighted_sum(QH - 1, 1, NC - 1)
            pe.wait_ge(wo_in[1], (nb * NG + 1) * 16)
            pe.wait_ge(o_sb, pairs + 1)
            for h in range(2):
                project_out(1, h, tail_bank(h))
            pe.wait_ge(fold_done, 4 * pairs + 4)
            pe.wait_ge(x_added, 4 * pairs + 4)
            row_sums()

        @block.scalar
        def _(act):
            norm_sqrt(act, ln, rs)
            act.wait_ge(wkraw_in, 16)
            act.activation(kh[:, 0, :], rawk, ACT.Copy).then_inc(whi, 1)
            copy_rows(act, ln, NR, lambda r: ps[:, r % 4, :], xnT_all)

            def context_hi(c, buf):
                act.activation(C[:, 0:3:2, c * CH:c * CH + CH], crawb[buf], ACT.Copy).then_inc(chi, 1)

            def keys_hi(c, h):
                own = slice(h * DH, h * DH + DH)
                act.activation(KH[own, h, c, :], psK[own], ACT.Copy).then_inc(k_hi, 1)

            def keys_hi_twice(c, before):
                for h in range(2):
                    own, other = slice(h * DH, h * DH + DH), slice((1 - h) * DH, (1 - h) * DH + DH)
                    act.wait_ge(k_hi, before + h + 1)
                    act.activation(KH[other, h, c, :], KH[own, h, c, :].bitcast(F32), ACT.Copy).then_inc(k_hi, 1)

            def scale_q():
                act.activation(qs[:], psM[:, 0:ROWS], ACT.Copy, scale=float(DH) ** -0.5).then_inc(q_sb, 1)

            def copy_max(slot, h):
                act.activation(Q2[MROW:MROW + 1, slot, h, :], psM[MROW:MROW + 1, ROWS:2 * ROWS], ACT.Copy).then_inc(m_row, 1)

            def first_context_hi(c):
                act.wait_ge(craw_in[c % BUFS], 16 * (c // BUFS) + 16)
                context_hi(c, c % BUFS)

            first_context_hi(0)
            act.wait_ge(wvraw_in, 16)
            act.activation(kl[:, 0, :], rawv, ACT.Copy).then_inc(whi, 1)
            for c in range(1, BUFS):
                first_context_hi(c)
            act.wait_ge(q_ps, 1)
            scale_q()
            for c in range(NC):
                if c == NC // 2:
                    act.wait_ge(wk_st, 64)
                    act.wait_ge(wk_in[0], 32)
                    act.wait_ge(wk_in[1], 32)
                act.wait_ge(k_ps, c + 1)
                keys_hi(c, 0)
                keys_hi(c, 1)
                keys_hi_twice(c, 4 * c)
                if c + BUFS < NC:
                    first_context_hi(c + BUFS)
            act.wait_ge(filled, 6)
            act.sem_inc(p_ready, 1)

            def quad(it, b, g, last, final):
                for t in range(HS):
                    pi, c, h = t // (2 * NC), t % (2 * NC) // 2, t % 2
                    p, T = it * 2 + pi, it * HS + t
                    nchunk = NC * (p + 1) + c
                    more = not (final and pi == 1)
                    if t == 0:
                        act.activation(warm[:], zero[:], ACT.Exp)
                    if c == 0 and h == 0:
                        if more:
                            act.wait_ge(q_ps, p + 2)
                            act.wait_ge(q_ready, p + 1)
                            scale_q()
                        act.wait_ge(m_ps, 2 * p + 2)
                        copy_max(pi, 0)
                        act.wait_ge(pv_done, T + 2)
                        act.wait_ge(out_ps, 2 * p + 1)
                        act.activation(flat(Ot[:, :, :]), psO, ACT.Copy).then_inc(o_sb, 1)
                    if c == 0 and h == 1 and more:
                        act.wait_ge(k_ps, nchunk + 1)
                        keys_hi(c, 0)
                    act.wait_ge(s_ps, T + 1)
                    act.wait_ge(pv_done, T + 1)
                    act.wait_ge(acc_done, T + 1)
                    act.activation(PR[:, h, :], flat(psS if c == 0 else banks_of(h, more)), ACT.Exp).then_inc(p_ready, 1)
                    if c == 0 and h == 0:
                        act.wait_ge(m_ps, 2 * p + 3)
                        copy_max(pi, 1)
                    if h == 1 and more:
                        if c > 0:
                            act.wait_ge(k_ps, nchunk + 1)
                            keys_hi(c, 0)
                        keys_hi(c, 1)
                        keys_hi_twice(c, 4 * nchunk)
                    if last and t in REFRESH:
                        k = REFRESH[t]
                        act.wait_ge(craw_in[0], 16 * -(-NC // BUFS) + (b * NC + k + 1) * 16)
                        act.wait_ge(k_ps, NC * (it * 2 + 1) + k + 1)
                        context_hi(k, 0)

            loops(act, quad)
            pairs = nb * HEADS // 2
            act.wait_ge(pv_done, pairs * 2 * NC + 2)
            act.wait_ge(out_ps, 2 * pairs + 1)
            act.activation(flat(Ot[:, :, :]), psO, ACT.Copy).then_inc(o_sb, 1)

        @block.vector
        def _(dve):
            def context_lo(c, buf):
                k = slice(c * CH, c * CH + CH)
                dve.tensor_tensor(C[:, 1, k], crawb[buf][:, 0, :], C[:, 0, k].bitcast(F32), ALU.subtract)
                dve.tensor_tensor(C[DH:, 2, k], crawb[buf][DH:, 1, :], C[DH:, 2, k].bitcast(F32), ALU.subtract).then_inc(cready, 1)

            def keys_lo(c, h):
                dve.tensor_tensor(KL[0:DH, h, c, :], psK[h * DH:h * DH + DH], KH[h * DH:h * DH + DH, h, c, :].bitcast(F32), ALU.subtract).then_inc(k_lo, 1)

            def chunk_max(h, c, t):
                dve.tensor_reduce(amx[:, h, t, c:c + 1], psA[:, t, :], AX.X, ALU.max).then_inc(a_max, 1)

            def negate_max(h):
                dve.tensor_reduce(nmx[:, h, :], amx[:, h, :, :], AX.X, ALU.max, negate=True).then_inc(m_ready, 1)

            def copy_v(u):
                dve.tensor_copy(flat(V[:, 2 * u:2 * u + 2, :]), psV).then_inc(v_sb, 1)

            def split_q(slot, before):
                dve.tensor_copy(qh[:], qs[:]).then_inc(q_hi, 1)
                dve.wait_ge(q_hi, before + 1)
                for h in range(2):
                    own = slice(h * DH, h * DH + DH)
                    dve.tensor_copy(Q1[0:DH, slot, h, :], qh[own, :].bitcast(F32))
                    dve.tensor_copy(Q2[0:DH, slot, h, :], qh[own, :].bitcast(F32))
                    ins = dve.tensor_tensor(Q1[DH:, slot, h, :], qs[own, :], qh[own, :].bitcast(F32), ALU.subtract)
                ins.then_inc(q_ready, 1)

            dve.wait_ge(x_in, 16)
            norm_vector(dve, ln, NR, lambda r: xin[:, r, :], lambda r: x1[:, RT + r, :], st6, mv, rs)
            dve.wait_ge(whi, 1)
            dve.tensor_tensor(kh[:, 1, :], rawk, kh[:, 0, :].bitcast(F32), ALU.subtract).then_inc(wlo, 1)

            def first_context_lo(c):
                dve.wait_ge(chi, c + 1)
                context_lo(c, c % BUFS)

            first_context_lo(0)
            dve.wait_ge(whi, 2)
            dve.tensor_tensor(kl[:, 1, :], rawv, kl[:, 0, :].bitcast(F32), ALU.subtract).then_inc(wlo, 1)
            for c in range(1, BUFS):
                first_context_lo(c)
            dve.wait_ge(q_sb, 1)
            split_q(0, 0)
            dve.wait_ge(ln["t_ps"], NR)
            dve.wait_ge(c_in, 32)
            dve.tensor_tensor(x1[:, RT:, :], xin, bo[:, :].unsqueeze(1).to_broadcast([P, NR, DM]), ALU.add).then_inc(init, 1)
            for c in range(NC):
                if c == NC // 2:
                    dve.wait_ge(wv_st, 64)
                    dve.wait_ge(wv_in, 32)
                if c < NC - 1:
                    for h in range(2):
                        dve.wait_ge(k_hi, 4 * c + h + 1)
                        keys_lo(c, h)
                for h in range(2):
                    if c > 0:
                        for t in range(RT):
                            dve.wait_ge(a_ps, 4 * (c - 1) + 2 * h + t + 1)
                            chunk_max(h, c - 1, t)
                    if h == 0 and c < V_FIRST:
                        dve.wait_ge(v_ps, c + 1)
                        copy_v(c)
                if c + BUFS < NC:
                    first_context_lo(c + BUFS)

            def quad(it, b, g, last, final):
                for t in range(HS):
                    pi, c, h = t // (2 * NC), t % (2 * NC) // 2, t % 2
                    p = it * 2 + pi
                    nchunk = NC * (p + 1) + c
                    more = not (final and pi == 1)

                    def copy_v_of_step():
                        if t in V_JOB and not (final and V_JOB[t][1]):
                            u, ahead = V_JOB[t]
                            dve.wait_ge(v_ps, (it + ahead) * 16 + u + 1)
                            copy_v(u)

                    if h == 0 and (more or c == 0):
                        n = nchunk - 1
                        for k in range(2):
                            if c == 1:
                                dve.wait_ge(m_ready, 2 * p + 2)
                            for r in range(RT):
                                dve.wait_ge(a_ps, 4 * n + 2 * k + r + 1)
                                chunk_max(k, (c - 1) % NC, r)
                            if c > 0 and k == 0:
                                copy_v_of_step()
                            if c == 0:
                                dve.wait_ge(a_max, 4 * n + 2 * k + 2)
                                dve.wait_ge(m_ps, 2 * p + 1)
                                negate_max(k)
                                if k == 0:
                                    for j in range(2):
                                        dve.wait_ge(k_hi, 4 * n + j + 1)
                                        keys_lo(NC - 1, j)
                    elif h == 1 and more:
                        if c == 0:
                            dve.wait_ge(q_sb, p + 2)
                            split_q((pi + 1) % 2, p + 1)
                        if c < NC - 1:
                            for j in range(2):
                                dve.wait_ge(k_hi, 4 * nchunk + j + 1)
                                keys_lo(c, j)
                    if c == 0 or h == 1:
                        copy_v_of_step()
                    if c == 2 and h == 0:
                        dve.wait_ge(l_ps, p + 1)
                        dve.wait_ge(x_added, 4 * p + 4)
                        dve.reciprocal(rl[:, :], psM[:, 0:2 * RT]).then_inc(rl_ready, 1)
                    if c in (3, 4) and h == 0:
                        k = c - 3
                        dve.wait_ge(rl_ready, p + 1)
                        dve.wait_ge(out_ps, 2 * p + k + 2)
                        dve.wait_ge(x_added, 4 * p + 2 * k + 4)
                        add_rows((p + NC - 1) // NC, k)
                    if last and t in REFRESH:
                        k = REFRESH[t]
                        dve.wait_ge(chi, b * NC + NC + k + 1)
                        context_lo(k, 0)

            def add_rows(slot, h, bank=psM):
                for t in range(RT):
                    row = x1[:, bass.ds(slot * RT + t, 1), :].rearrange("p o n -> p (o n)")
                    dve.scalar_tensor_tensor(out=row, in0=bank[:, t * DM:t * DM + DM], scalar=rl[:, 2 * h + t:2 * h + t + 1], in1=row,
                                             op0=ALU.mult, op1=ALU.add).then_inc(x_added, 1)

            dve.wait_ge(filled, 6)
            dve.sem_inc(x_added, 4)
            loops(dve, quad)
            pairs = nb * HEADS // 2
            dve.wait_ge(l_ps, pairs + 1)
            dve.wait_ge(x_added, 4 * pairs + 4)
            dve.reciprocal(rl[:, :], psM[:, 0:2 * RT]).then_inc(rl_ready, 1)
            dve.wait_ge(rl_ready, pairs + 1)
            for h in range(2):
                dve.wait_ge(out_ps, 2 * pairs + h + 2)
                dve.wait_ge(x_added, 4 * pairs + 2 * h + 4)
                add_rows(nb, h, tail_bank(h))
            dve.wait_ge(x_added, 4 * pairs + 8)

        @block.gpsimd
        def _(pool):
            pool.memset(ones[:], 1.0)
            pool.memset(zero[:], 0.0)
            pool.memset(accf[:, :, :], 1.0)
            pool.memset(x1[:, 0:RT, :], 0.0).then_inc(filled, 1)
            pool.wait_ge(filled, 1)
            pool.memset(Q2[MROW:M2].bitcast(F32), 0.0).then_inc(filled, 1)
            pool.wait_ge(filled, 2)
            pool.wait_ge(wv_st, 64)
            pool.wait_ge(wv_in, 32)
            pool.memset(KL[MROW:M2].bitcast(F32), 0.0).then_inc(filled, 1)
            pool.wait_ge(filled, 3)
            pool.memset(KL[MROW:MROW + 1].bitcast(F32), 1.0).then_inc(filled, 1)
            pool.wait_ge(filled, 4)
            pool.wait_ge(init, 1)
            pool.memset(PR[:, 1, :], 0.0).then_inc(filled, 1)
            pool.wait_ge(xst, 16 * nb)
            pool.wait_ge(xn_in, 16)
            pool.memset(V[:, 28:32, :], 0.0).then_inc(filled, 1)
            pool.wait_ge(cready, NC)
            pool.wait_ge(filled, 6)
            pool.sem_inc(acc_done, 2)
            pool.sem_inc(fold_done, 4)

            def quad(it, b, g, last, final):
                for t in range(HS):
                    pi, c, h = t // (2 * NC), t % (2 * NC) // 2, t % 2
                    p, T = it * 2 + pi, it * HS + t
                    pool.wait_ge(p_ready, T + 2)
                    if c == 0:
                        pool.wait_ge(fold_done, 4 * p + 2 * h + 2)
                        pool.tensor_tensor(acc[:, h, :], PR[:, h, :], zero[:, 0:1].to_broadcast([P, KT * ROWS]), ALU.add).then_inc(acc_done, 1)
                    else:
                        pool.wait_ge(acc_done, T + 1)
                        pool.tensor_tensor(acc[:, h, :], acc[:, h, :], PR[:, h, :], ALU.add).then_inc(acc_done, 1)
                    if c == NC - 1:
                        pool.wait_ge(acc_done, T + 3)
                        pool.tensor_tensor(acc[:, h, 0:512], acc[:, h, 0:512], acc[:, h, 512:1024], ALU.add).then_inc(fold_done, 1)
                        pool.wait_ge(fold_done, 4 * p + 2 * h + 5)
                        pool.wait_ge(l_ps, p + 1)
                        pool.tensor_tensor(accf[:, h, :], acc[:, h, 0:256], acc[:, h, 256:512], ALU.add).then_inc(fold_done, 1)

            loops(pool, quad)


def norm_sems(sem, name):
    return {k: sem(f"{name}_{k}") for k in ("stats", "mean", "var", "sqrt", "rstd", "normed", "t_ps", "t_sb")}


def norm_vector(dve, s, tiles, src, dst, st6, mv, rs):
    for r in range(tiles):
        dve.bn_stats(st6[:, r, :], src(r)).then_inc(s["stats"], 1)
    norm_scale(dve, s, tiles, st6, mv, rs)
    for r in range(tiles):
        dve.tensor_scalar(dst(r), src(r), mv[:, r, 0:1], rs[:, r:r + 1], ALU.subtract, ALU.mult).then_inc(s["normed"], 1)


def norm_scale(dve, s, tiles, st6, mv, rs):
    for r in range(tiles):
        dve.wait_ge(s["stats"], r + 1)
        dve.bn_aggr(mv[:, r, :], st6[:, r, :]).then_inc(s["mean"], 1)
    dve.wait_ge(s["mean"], tiles)
    dve.tensor_scalar(rs[:], mv[:, :, 1], EPS, None, ALU.add).then_inc(s["var"], 1)
    dve.wait_ge(s["sqrt"], 1)
    dve.reciprocal(rs[:], rs[:]).then_inc(s["rstd"], 1)
    dve.wait_ge(s["rstd"], 1)


def norm_sqrt(act, s, rs):
    act.wait_ge(s["var"], 1)
    act.activation(rs[:], rs[:], ACT.Sqrt).then_inc(s["sqrt"], 1)


def transpose_rows(pe, s, tiles, src, bank, ident):
    for r in range(tiles):
        pe.wait_ge(s["normed"], r + 1)
        if r >= 4:
            pe.wait_ge(s["t_sb"], r - 3)
        for t in range(2):
            mm = pe.transpose(bank(r)[:, t * P:t * P + P], src(r)[:, t * P:t * P + P], ident[:, :])
        mm.then_inc(s["t_ps"], 1)


def copy_rows(act, s, tiles, bank, dst):
    for r in range(tiles):
        act.wait_ge(s["t_ps"], r + 1)
        act.activation(dst[:, :, r * P:r * P + P], bank(r)[:, 0:2 * P].rearrange("p (t n) -> p t n", t=2), ACT.Copy).then_inc(s["t_sb"], 1)


def recurrence(nc, nb, top, d, ew):
    x1, ident = top["x1"], top["ident"]
    NR = nb * RT
    N = nb * ROWS
    HALVES = max(1, N // 512)
    W = N // HALVES
    G = 2
    ctx = ExitStack()
    with ctx:
        def sb(name, shape, dt=F32):
            return ctx.enter_context(nc.sbuf_tensor(name, shape, dt))

        def sem(name):
            return ctx.enter_context(nc.semaphore(name))

        u = sb("u", [P, NR, DM])
        uT = sb("uT", [P, 2, N])
        w4 = sb("w4", [P, 4, 2, DM])
        bd = sb("bd", [P, 2, 2, G, P])
        rope = sb("rope", [P, 2, W])
        gb = sb("gb", [P, G])
        dl = sb("dl", [P, G])
        dec = sb("dec", [P, G])
        seq = sb("seq", [P, N])
        dect = sb("dect", [P, G, N])
        selv = sb("selv", [P, 16, P])
        selvr = sb("selvr", [P, 16, P], F32R)
        sely = sb("sely", [P, 4, 32])
        ow = sb("ow", [P, G, DM])
        vecs = sb("vecs", [P, 3, DM])
        t1 = sb("t1", [P, 2, W])
        t2 = sb("t2", [P, 2, W])
        qr = sb("qr", [P, G, N])
        gate = sb("gate", [P, 2, W])
        kk = sb("kk", [P, G, N])
        vh = sb("vh", [P, G, N], F32R)
        vl = sb("vl", [P, G, N], F32R)
        kv = sb("kv", [P, 2, N])
        M = sb("M", [P, 2, N])
        qm = sb("qm", [P, 2, N])
        yT = uT
        st6, mv, rs = sb("st6b", [P, NR, 6]), sb("mvb", [P, NR, 2]), sb("rsb", [P, NR])
        st6c, mvc, rsc = sb("st6c", [P, NR, 6]), sb("mvc", [P, NR, 2]), sb("rsc", [P, NR])
        ps = ctx.enter_context(nc.psum_tensor("ps2", [P, 8, 512], F32))

        w_in = [sem(f"w4_in{i}") for i in range(4)]
        ln = norm_sems(sem, "n2")
        lo = norm_sems(sem, "n3")
        pr_ps = sem("pr_ps")
        ropes, r_ps, qr_ready, gate_ready, kk_ready = (sem(x) for x in ("ropes", "r_ps", "qr_ready", "gate_ready", "kk_ready"))
        vhi, vlo, dec_ready, dect_ready, selr = sem("vhi"), sem("vlo"), sem("dec_ready"), sem("dect_ready"), sem("selr")
        v_ps, kv_ready, m_done, qm_ready, y_ps, y_sb = (sem(x) for x in ("vb_ps", "kv_ready", "m_done", "qm_ready", "y_ps", "y_sb"))
        o_ps, h_ready, scaled, fin, added = sem("o_ps"), sem("h_ready"), sem("scaled"), sem("fin2"), sem("added2")
        ub = sem("ub")
        pairs = [(g, hf) for g in range(G) for hf in range(HALVES)]
        NJ = len(pairs)
        cols = lambda hf: slice(hf * W, hf * W + W)
        block = ctx.enter_context(nc.Block())

        @block.sync
        def _(sp):
            sp.dma_start(w4[:], d["w4"]).then_inc(w_in[0], 16)
            sp.dma_start(rope[:], d["rope"][:, :, 0:W]).then_inc(w_in[1], 16)
            sp.dma_start(gb[:], d["gb"]).then_inc(w_in[1], 16)
            sp.dma_start(dl[:], d["dl"]).then_inc(w_in[1], 16)
            sp.dma_start(seq[:], d["seq"][:, 0:N]).then_inc(w_in[1], 16)
            sp.dma_start(bd[:], d["bd"]).then_inc(w_in[1], 16)
            sp.dma_start(selv[:], d["selv"]).then_inc(w_in[2], 16)
            sp.dma_start(sely[:], d["sely"]).then_inc(w_in[2], 16)
            sp.dma_start(ow[:], d["ow"]).then_inc(w_in[3], 16)
            sp.dma_start(vecs[:], d["vecs"]).then_inc(w_in[3], 16)
            sp.dma_start(ew["sw12"][:], d["sw12"]).then_inc(ew["s_in"], 16)
            for e in range(2):
                sp.dma_start(ew["we"][:, e, :, :, :], d["we"][e]).then_inc(ew["we_in"][e], 16)

        bank = lambda r: ps[:, 4 + r % 4, :]

        @block.tensor
        def _(pe):
            transpose_rows(pe, ln, NR, lambda r: u[:, r, :], bank, ident)
            pe.wait_ge(ln["t_sb"], NR)
            pe.wait_ge(w_in[0], 16)
            pe.wait_ge(w_in[1], 80)

            def project(i, g, hf, out):
                for t in range(2):
                    mm = pe.matmul(out, w4[:, i, t, g * P:g * P + P], uT[:, t, cols(hf)], start=(t == 0), stop=(t == 1))
                return mm
            for n, (g, hf) in enumerate(pairs):
                for i in range(2):
                    if n:
                        pe.wait_ge(ropes, 2 * (2 * (n - 1) + i) + 2)
                    project(i, g, hf, ps[:, i, 0:W]).then_inc(pr_ps, 1)
                if n:
                    pe.wait_ge(gate_ready, n)
                project(3, g, hf, ps[:, 2, 0:W]).then_inc(pr_ps, 1)
                if n:
                    pe.wait_ge(vlo, n)
                project(2, g, hf, ps[:, 3, 0:W]).then_inc(pr_ps, 1)
                for i in range(2):
                    pe.wait_ge(ropes, 2 * (2 * n + i) + 2)
                    if n:
                        pe.wait_ge([qr_ready, kk_ready][i], n)
                    pe.matmul(ps[:, 6 + i, 0:W], bd[:, i, 0, g, :], t1[:, i, :], start=True, stop=False)
                    pe.matmul(ps[:, 6 + i, 0:W], bd[:, i, 1, g, :], t2[:, i, :], start=False, stop=True).then_inc(r_ps, 1)
            pe.wait_ge(qr_ready, NJ)
            pe.wait_ge(kk_ready, NJ)
            pe.wait_ge(vlo, NJ)
            pe.wait_ge(selr, 1)

            def broadcast_v(j, g, dd):
                for hf in range(HALVES):
                    out = ps[:, 2 * (j % 2) + hf, 0:W]
                    pe.matmul(out, selvr[:, dd, :], vh[:, g, cols(hf)], start=True, stop=False)
                    mm = pe.matmul(out, selvr[:, dd, :], vl[:, g, cols(hf)], start=False, stop=True)
                mm.then_inc(v_ps, 1)

            def sum_r(j, g, dd):
                k, e = dd // 4, dd % 4
                for hf in range(HALVES):
                    mm = pe.matmul(ps[32 * k:32 * k + 32, 4 + 2 * g + hf, 0:W], sely[:, e, :], qm[:, j % 2, cols(hf)],
                                   start=(e == 0), stop=(e == 3), skip_group_check=True)
                mm.then_inc(y_ps, 1)

            steps = [(g, dd) for g in range(G) for dd in range(16)]
            for j, (g, dd) in enumerate(steps):
                if j >= 2:
                    pe.wait_ge(kv_ready, j - 1)
                broadcast_v(j, g, dd)
                if j >= 2:
                    pe.wait_ge(qm_ready, j - 1)
                    sum_r(j - 2, *steps[j - 2])
            for j in range(30, 32):
                pe.wait_ge(qm_ready, j + 1)
                sum_r(j, *steps[j])
            pe.wait_ge(y_sb, G)
            pe.wait_ge(w_in[3], 32)
            for r in range(NR):
                if r >= 4:
                    pe.wait_ge(h_ready, r - 3)
                for g in range(G):
                    mm = pe.matmul(ps[:, r % 4, 0:DM], yT[:, g, r * P:r * P + P], ow[:, g, :], start=(g == 0), stop=(g == 1))
                mm.then_inc(o_ps, 1)

        @block.scalar
        def _(act):
            norm_sqrt(act, ln, rs)
            copy_rows(act, ln, NR, bank, uT)
            act.wait_ge(w_in[1], 80)
            act.activation(dec[:], dl[:], ACT.Sigmoid).then_inc(dec_ready, 1)
            act.wait_ge(w_in[2], 32)
            act.activation(selvr[:, :, :], selv[:, :, :], ACT.Copy).then_inc(selr, 1)
            for n, (g, hf) in enumerate(pairs):
                act.wait_ge(pr_ps, 4 * n + 3)
                if n >= 2:
                    act.wait_ge(kk_ready, n - 1)
                act.activation(gate[:, n % 2, :], ps[:, 2, 0:W], ACT.Sigmoid, bias=gb[:, g:g + 1]).then_inc(gate_ready, 1)
                act.wait_ge(pr_ps, 4 * n + 4)
                act.activation(vh[:, g, cols(hf)], ps[:, 3, 0:W], ACT.Copy).then_inc(vhi, 1)
                act.wait_ge(r_ps, 2 * n + 1)
                act.activation(qr[:, g, cols(hf)], ps[:, 6, 0:W], ACT.Copy).then_inc(qr_ready, 1)
                if n == 0:
                    act.wait_ge(ew["s_in"], 16)
                    act.activation(flat4(ew["sws"][:, 0, :, :, :]), flat4(ew["sw12"][:, :, :, :]), ACT.Copy).then_inc(ew["sw_hi"], 1)
                if n == 1:
                    act.wait_ge(ew["we_in"][0], 16)
                    act.activation(flat4(ew["wes"][:, 0, 0, :, :, :]), flat4(ew["we"][:, 0, :, :, :]), ACT.Copy).then_inc(ew["we_hi"], 1)
            for g in range(G):
                act.wait_ge(y_ps, 16 * g + 16)
                act.activation(yT[:, g, :].rearrange("p (a n) -> p a n", a=HALVES), ps[:, 4 + 2 * g:4 + 2 * g + HALVES, 0:W], ACT.Copy).then_inc(y_sb, 1)
            norm_sqrt(act, lo, rsc)

        @block.vector
        def _(dve):
            norm_vector(dve, ln, NR, lambda r: x1[:, RT + r, :], lambda r: u[:, r, :], st6, mv, rs)
            dve.wait_ge(w_in[1], 80)
            dve.wait_ge(dec_ready, 1)
            for g in range(G):
                dve.tensor_scalar(dect[:, g, :], seq[:, :], dec[:, g:g + 1], None, ALU.mult).then_inc(dect_ready, 1)
            for n, (g, hf) in enumerate(pairs):
                for i in range(2):
                    dve.wait_ge(pr_ps, 4 * n + i + 1)
                    if n:
                        dve.wait_ge(r_ps, 2 * (n - 1) + i + 1)
                    dve.tensor_tensor(t1[:, i, :], ps[:, i, 0:W], rope[:, 0, :], ALU.mult).then_inc(ropes, 1)
                    dve.tensor_tensor(t2[:, i, :], ps[:, i, 0:W], rope[:, 1, :], ALU.mult).then_inc(ropes, 1)
                dve.wait_ge(vhi, n + 1)
                dve.tensor_tensor(vl[:, g, cols(hf)], ps[:, 3, 0:W], vh[:, g, cols(hf)].bitcast(F32), ALU.subtract).then_inc(vlo, 1)
                dve.wait_ge(r_ps, 2 * n + 2)
                dve.wait_ge(gate_ready, n + 1)
                dve.scalar_tensor_tensor(out=kk[:, g, cols(hf)], in0=ps[:, 7, 0:W], scalar=0.25, in1=gate[:, n % 2, :],
                                         op0=ALU.mult, op1=ALU.mult).then_inc(kk_ready, 1)
                if n == 0:
                    dve.wait_ge(ew["sw_hi"], 1)
                    dve.tensor_tensor(flat4(ew["sws"][:, 1, :, :, :]), flat4(ew["sw12"][:, :, :, :]),
                                      flat4(ew["sws"][:, 0, :, :, :]).bitcast(F32), ALU.subtract).then_inc(ew["sw_lo"], 1)
                if n == 1:
                    dve.wait_ge(ew["we_hi"], 1)
                    dve.tensor_tensor(flat4(ew["wes"][:, 0, 1, :, :, :]), flat4(ew["we"][:, 0, :, :, :]),
                                      flat4(ew["wes"][:, 0, 0, :, :, :]).bitcast(F32), ALU.subtract).then_inc(ew["we_lo"], 1)
            dve.wait_ge(kk_ready, NJ)
            dve.wait_ge(dect_ready, G)
            for j in range(32):
                g = j // 16
                if j >= 2:
                    dve.wait_ge(m_done, j - 1)
                dve.wait_ge(v_ps, j + 1)
                dve.tensor_tensor(kv[:, j % 2, :].rearrange("p (a n) -> p a n", a=HALVES), ps[:, 2 * (j % 2):2 * (j % 2) + HALVES, 0:W],
                                  kk[:, g, :].rearrange("p (a n) -> p a n", a=HALVES), ALU.mult).then_inc(kv_ready, 1)
                dve.wait_ge(kv_ready, j + 1)
                if j >= 2:
                    dve.wait_ge(qm_ready, j - 1)
                dve.tensor_tensor_scan(M[:, j % 2, :], dect[:, g, :], kv[:, j % 2, :], 0.0, ALU.mult, ALU.add).then_inc(m_done, 1)
            dve.wait_ge(ub, 1)

            def stats(r):
                dve.wait_ge(h_ready, r + 1)
                dve.bn_stats(st6c[:, r, :], u[:, r, :]).then_inc(lo["stats"], 1)

            for r in range(NR):
                dve.wait_ge(o_ps, r + 1)
                dve.tensor_tensor(u[:, r, :], ps[:, r % 4, 0:DM], u[:, r, :], ALU.add).then_inc(h_ready, 1)
                if r > 0:
                    stats(r - 1)
            stats(NR - 1)
            norm_scale(dve, lo, NR, st6c, mvc, rsc)
            for r in range(NR):
                dve.scalar_tensor_tensor(out=u[:, r, :], in0=u[:, r, :], scalar=mvc[:, r, 0:1], in1=vecs[:, 1, :],
                                         op0=ALU.subtract, op1=ALU.mult).then_inc(scaled, 1)
            dve.wait_ge(fin, 1)
            for r in range(NR):
                dve.wait_ge(scaled, r + 1)
                dve.scalar_tensor_tensor(out=x1[:, RT + r, :], in0=u[:, r, :], scalar=rsc[:, r:r + 1], in1=x1[:, RT + r, :],
                                         op0=ALU.mult, op1=ALU.add).then_inc(added, 1)
            dve.wait_ge(added, NR)

        @block.gpsimd
        def _(pool):
            pool.wait_ge(qr_ready, NJ)
            for j in range(32):
                pool.wait_ge(m_done, j + 1)
                if j >= 2:
                    pool.wait_ge(y_ps, j - 1)
                pool.tensor_tensor(qm[:, j % 2, :], M[:, j % 2, :], qr[:, j // 16, :], ALU.mult).then_inc(qm_ready, 1)
            pool.wait_ge(w_in[3], 32)
            pool.tensor_tensor(u[:, :, :], u[:, :, :], vecs[:, 0, :].unsqueeze(1).to_broadcast([P, NR, DM]), ALU.add).then_inc(ub, 1)
            pool.tensor_tensor(x1[:, RT:, :], x1[:, RT:, :], vecs[:, 2, :].unsqueeze(1).to_broadcast([P, NR, DM]), ALU.add).then_inc(fin, 1)


def flat4(t):
    return t.rearrange("p a t n -> p (a t n)")


def experts(nc, nb, top, d, out, ew):
    x2, ident = top["x1"], top["ident"]
    NR = nb * RT
    N = nb * ROWS
    HALVES = max(1, N // 512)
    W = N // HALVES
    E = 8
    ctx = ExitStack()
    with ctx:
        def sb(name, shape, dt=F32):
            return ctx.enter_context(nc.sbuf_tensor(name, shape, dt))

        def sem(name):
            return ctx.enter_context(nc.semaphore(name))

        w = sb("w", [P, NR, DM])
        wT = sb("wT", [P, 2, N])
        gw = sb("gw", [P, 2, E])
        sw3 = sb("sw3", [P, 4, DM])
        sws, we, wes = ew["sws"], ew["we"], ew["wes"]
        wTs = sb("wTs", [P, 2, 2, N], F32R)
        hTs = sb("hTs", [P, 2, 2, N], F32R)
        be = sb("be", [P, 2, 3, 2])
        lg = sb("lg", [P, NR, E])
        mx = sb("mx", [P, NR])
        sm = sb("sm", [P, NR])
        iota = sb("iota", [P, E])
        cand = sb("cand", [P, NR, E])
        sc2 = sb("sc2", [P, NR, E])
        hot = sb("hot", [P, NR, E])
        wm = sb("wm", [P, NR, 2 * E])
        wmT = sb("wmT", [2 * E, N])
        bc = sb("bc", [P, 2, 2, N])
        t1 = sb("e_t1", [P, 2, N])
        hT = sb("hT", [P, 2, N])
        t3 = sb("e_t3", [P, 2, N])
        t3m = sb("e_t3m", [P, 2, N])
        yT = sb("y_T", [P, 2, N])
        zs = sb("zs", [P, 2, W])
        zT = sb("zT", [P, 4, N])
        st6, mv, rs = sb("st6d", [P, NR, 6]), sb("mvd", [P, NR, 2]), sb("rsd", [P, NR])
        ps = ctx.enter_context(nc.psum_tensor("ps3", [P, 8, 512], F32))
        g_in, s3_in = sem("g_in"), sem("s3_in")
        we_in, sw_lo, we_hi, we_lo = ew["we_in"], ew["sw_lo"], ew["we_hi"], ew["we_lo"]
        be_in = [sem(f"be_in{i}") for i in range(2)]
        bc_in = [sem(f"bc_in{i}") for i in range(2)]
        ln = norm_sems(sem, "n4")
        lg_ps, chain, ex, wm_ready, wm_ps, wm_sb, wm_out = (sem(x) for x in ("lg_ps", "chain", "ex", "wm_ready", "wm_ps", "wm_sb", "wm_out"))
        z_ps, z_silu, z_ready = sem("z_ps"), sem("z_silu"), sem("z_ready")
        h_ps, t1_ready, h_ready, x3_ps, t3_ready, t3m_ready, x2_ps, xy_ready, y_ready = (sem("e_" + x) for x in (
            "h_ps", "t1_ready", "h_ready", "x3_ps", "t3_ready", "t3m_ready", "x2_ps", "xy_ready", "y_ready"))
        wt_hi, wt_lo, hh_ready, hl_ready = (sem(x) for x in ("wt_hi", "wt_lo", "hh_ready", "hl_ready"))
        f_ps, added, f_ready, done = sem("f_ps"), sem("x_z_added"), sem("f_ready"), sem("done3")
        bank = lambda r: ps[:, 4 + r % 4, :]
        jobs = [(m, hf) for hf in range(HALVES) for m in range(2)]
        NJ = len(jobs)
        JOBS = 4 * HALVES
        wm_tiles = lambda n: range(NR * (n - JOBS // 4 - 1) // (JOBS // 2), NR * (n - JOBS // 4) // (JOBS // 2))
        middle = range(JOBS // 4 + 1, JOBS // 4 + 1 + JOBS // 2)
        cols = lambda hf: slice(hf * W, hf * W + W)
        block = ctx.enter_context(nc.Block())

        @block.sync
        def _(sp):
            sp.dma_start(gw[:], d["gw"]).then_inc(g_in, 16)
            sp.dma_start(iota[:], d["iota"]).then_inc(g_in, 16)
            sp.dma_start(sw3[:], d["sw3"]).then_inc(s3_in, 16)
            for e in range(2):
                sp.dma_start(be[:, e, :, :], d["be"][e]).then_inc(be_in[e], 16)
            sp.wait_ge(wm_sb, NR)
            sp.dma_start(d["wm_rows"][:, 0:N], wmT[:, :]).then_inc(wm_out, 16)
            sp.wait_ge(wm_out, 16)

            def load_bc(slot, e):
                for k in range(2):
                    sp.dma_start(bc[:, slot, k, :], d["wm_rows"][bass.ds(e + k * E, 1), 0:N].to_broadcast([P, N])).then_inc(bc_in[slot], 16)

            for e in range(2):
                load_bc(e, e)
            with sp.Fori(0, E // 2 - 1) as i:
                for k in range(2):
                    sp.wait_ge(we_lo, i * 2 + k + 1)
                    sp.dma_start(we[:, k, :, :, :], d["we"][bass.ds(i * 2 + 2 + k, 1)].rearrange("o p a t n -> p (o a) t n")).then_inc(we_in[k], 16)
                    sp.wait_ge(xy_ready, (i * 2 + k) * NJ + 2 * NJ)
                    sp.dma_start(be[:, k, :, :], d["be"][bass.ds(i * 2 + 2 + k, 1)].rearrange("o p a m -> p (o a) m")).then_inc(be_in[k], 16)
                    load_bc(k, i * 2 + 2 + k)
            for k in range(2):
                half = slice(k * NR // 2, (k + 1) * NR // 2)
                sp.wait_ge(f_ready, (k + 1) * NR // 2)
                sp.dma_start(out[:, half, :], w[:, half, :]).then_inc(done, 16)
            sp.wait_ge(done, 32)

        @block.tensor
        def _(pe):
            transpose_rows(pe, ln, NR, lambda r: w[:, r, :], bank, ident)
            pe.wait_ge(ln["t_sb"], NR)
            pe.wait_ge(g_in, 32)
            for r in range(NR):
                for t in range(2):
                    mm = pe.matmul(ps[:, 0, r * E:r * E + E], wT[:, t, r * P:r * P + P], gw[:, t, :], start=(t == 0), stop=(t == 1))
            mm.then_inc(lg_ps, 1)
            def split_product(out, stationary, moving):
                passes = [(a, b, t) for a, b in ((0, 0), (1, 0), (0, 1)) for t in range(2)]
                for i, (a, b, t) in enumerate(passes):
                    mm = pe.matmul(out, stationary(a, t), moving(b, t), start=(i == 0), stop=(i == len(passes) - 1))
                return mm

            pe.wait_ge(sw_lo, 1)
            pe.wait_ge(wt_lo, HALVES)
            n = 0
            for m in range(4):
                for hf in range(HALVES):
                    if n >= 2:
                        pe.wait_ge(z_ready, n - 1)
                    for a in range(2):
                        mm = split_product(ps[:, 1 + 2 * (n % 2) + a, 0:W], lambda s, t: sws[:, s, t, a, m * P:m * P + P],
                                           lambda s, t: wTs[:, s, t, cols(hf)])
                    mm.then_inc(z_ps, 1)
                    n += 1
                    if n in middle:
                        pe.wait_ge(wm_ready, 1)
                        for r in wm_tiles(n):
                            if r >= 2:
                                pe.wait_ge(wm_sb, r - 1)
                            pe.transpose(ps[0:2 * E, 6 + r % 2, 0:P], wm[:, r, :], ident[:, :]).then_inc(wm_ps, 1)
            pe.wait_ge(z_ready, 4 * HALVES)
            pe.wait_ge(wm_sb, NR)

            def layer(slot, a, src, m, hf, out):
                return split_product(out, lambda s, t: wes[:, slot, s, a, t, m * P:m * P + P], lambda s, t: src[:, s, t, cols(hf)])

            def expert(e, slot):
                base = e * NJ
                pe.wait_ge(we_hi, e + 1)
                pe.wait_ge(we_lo, e + 1)
                for n, (m, hf) in enumerate(jobs):
                    pe.wait_ge(t1_ready, base + n + 1)
                    layer(slot, 0, wTs, m, hf, ps[:, n % 2, 0:W]).then_inc(h_ps, 1)
                for n, (m, hf) in enumerate(jobs):
                    pe.wait_ge(t3_ready, base + n + 1)
                    layer(slot, 2, wTs, m, hf, ps[:, 2 + n % 2, 0:W]).then_inc(x3_ps, 1)
                for n, (m, hf) in enumerate(jobs):
                    pe.wait_ge(hl_ready, base + NJ + 2 * hf + 2)
                    pe.wait_ge(xy_ready, base + n + 1)
                    layer(slot, 1, hTs, m, hf, ps[:, 4 + n, 0:W]).then_inc(x2_ps, 1)

            pe.sem_inc(x2_ps, 1)
            with pe.Fori(0, E // 2) as i:
                for k in range(2):
                    expert(i * 2 + k, k)
            pe.wait_ge(y_ready, NJ * E + NJ)
            pe.wait_ge(s3_in, 16)
            for r in range(NR):
                if r >= 4:
                    pe.wait_ge(f_ready, r - 3)
                for t in range(4):
                    pe.matmul(ps[:, r % 4, 0:DM], zT[:, t, r * P:r * P + P], sw3[:, t, :], start=(t == 0), stop=(t == 3))
                for t in range(2):
                    mm = pe.transpose(ps[:, 4 + r % 4, t * P:t * P + P], yT[:, t, r * P:r * P + P], ident[:, :])
                mm.then_inc(f_ps, 1)

        @block.scalar
        def _(act):
            norm_sqrt(act, ln, rs)
            copy_rows(act, ln, NR, bank, wT)
            act.wait_ge(ln["t_sb"], NR)
            for hf in range(HALVES):
                act.activation(wTs[:, 0, :, cols(hf)], wT[:, :, cols(hf)], ACT.Copy).then_inc(wt_hi, 1)
            act.wait_ge(chain, 2)
            act.activation(lg[:, :, :], lg[:, :, :], ACT.Exp).then_inc(ex, 1)
            n = 0
            for m in range(4):
                for hf in range(HALVES):
                    act.wait_ge(z_ps, n + 1)
                    if n >= 2:
                        act.wait_ge(z_ready, n - 1)
                    act.activation(zs[:, n % 2, 0:W], ps[:, 1 + 2 * (n % 2), 0:W], ACT.Silu).then_inc(z_silu, 1)
                    n += 1
                    if n in middle:
                        for r in wm_tiles(n):
                            act.wait_ge(wm_ps, r + 1)
                            act.activation(wmT[:, r * P:r * P + P], ps[0:2 * E, 6 + r % 2, 0:P], ACT.Copy).then_inc(wm_sb, 1)
            act.sem_inc(h_ready, NJ)
            def split_weights(e, k, loads):
                act.wait_ge(we_in[k], loads)
                if not isinstance(e, int):
                    act.wait_ge(x2_ps, (e - 1) * NJ + 1)
                act.activation(flat4(wes[:, k, 0, :, :, :]), flat4(we[:, k, :, :, :]), ACT.Copy).then_inc(we_hi, 1)

            def expert(e, k, loads):
                base = e * NJ
                act.wait_ge(be_in[k], loads)
                for n, (m, hf) in enumerate(jobs):
                    act.wait_ge(t1_ready, base + n + 3)
                    act.wait_ge(hl_ready, base + n + 1)
                    act.activation(hT[:, m, cols(hf)], t1[:, m, cols(hf)], ACT.Silu, bias=be[:, k, 0, m:m + 1]).then_inc(h_ready, 1)
                    act.wait_ge(h_ready, base + NJ + n + 1)
                    act.wait_ge(x2_ps, base + 1)
                    act.activation(hTs[:, 0, m, cols(hf)], hT[:, m, cols(hf)], ACT.Copy).then_inc(hh_ready, 1)

            with act.Fori(0, E // 2 - 1) as i:
                for k in range(2):
                    expert(i * 2 + k, k, i * 16 + 16)
                    split_weights(i * 2 + k + 1, 1 - k, (i + k) * 16 + 16)
            expert(E - 2, 0, E // 2 * 16)
            act.wait_ge(x2_ps, (E - 2) * NJ + 1)
            split_weights(E - 1, 1, E // 2 * 16)
            expert(E - 1, 1, E // 2 * 16)

        @block.vector
        def _(dve):
            norm_vector(dve, ln, NR, lambda r: x2[:, RT + r, :], lambda r: w[:, r, :], st6, mv, rs)
            count = [0]

            def link(ins):
                count[0] += 1
                ins.then_inc(chain, 1)
                dve.wait_ge(chain, count[0])

            for hf in range(HALVES):
                dve.wait_ge(wt_hi, hf + 1)
                dve.tensor_tensor(wTs[:, 1, :, cols(hf)], wT[:, :, cols(hf)], wTs[:, 0, :, cols(hf)].bitcast(F32), ALU.subtract).then_inc(wt_lo, 1)
            rows = lambda t: t[:, :].unsqueeze(2).to_broadcast([P, NR, E])
            dve.wait_ge(lg_ps, 1)
            logits = ps[:, 0, 0:NR * E].rearrange("p (r e) -> p r e", e=E)
            link(dve.tensor_reduce(mx[:, :], logits, AX.X, ALU.max))
            link(dve.tensor_tensor(lg[:, :, :], logits, rows(mx), ALU.subtract))
            dve.wait_ge(ex, 1)
            link(dve.tensor_reduce(sm[:, :], lg[:, :, :], AX.X, ALU.add))
            link(dve.reciprocal(sm[:, :], sm[:, :]))
            link(dve.tensor_tensor(lg[:, :, :], lg[:, :, :], rows(sm), ALU.mult))
            order = iota[:, :].unsqueeze(1).to_broadcast([P, NR, E])
            score = lg
            for k in range(2):
                link(dve.tensor_reduce(mx[:, :], score[:, :, :], AX.X, ALU.max))
                link(dve.tensor_tensor(hot[:, :, :], score[:, :, :], rows(mx), ALU.is_ge))
                link(dve.scalar_tensor_tensor(out=cand[:, :, :], in0=hot[:, :, :], scalar=-float(E), in1=order, op0=ALU.mult, op1=ALU.add))
                link(dve.tensor_reduce(mx[:, :], cand[:, :, :], AX.X, ALU.min))
                one = wm[:, :, E:2 * E] if k == 0 else hot[:, :, :]
                link(dve.tensor_tensor(one, cand[:, :, :], rows(mx), ALU.is_equal))
                if k == 0:
                    link(dve.scalar_tensor_tensor(out=sc2[:, :, :], in0=one, scalar=-4.0, in1=lg[:, :, :], op0=ALU.mult, op1=ALU.add))
                    score = sc2
            link(dve.tensor_tensor(wm[:, :, E:2 * E], wm[:, :, E:2 * E], hot[:, :, :], ALU.add))
            dve.tensor_tensor(wm[:, :, 0:E], wm[:, :, E:2 * E], lg[:, :, :], ALU.mult).then_inc(wm_ready, 1)
            n = 0
            for m in range(4):
                for hf in range(HALVES):
                    dve.wait_ge(z_silu, n + 1)
                    dve.tensor_tensor(zT[:, m, cols(hf)], ps[:, 2 + 2 * (n % 2), 0:W], zs[:, n % 2, 0:W], ALU.mult).then_inc(z_ready, 1)
                    n += 1
            dve.sem_inc(t1_ready, 2)
            dve.sem_inc(t3_ready, 2)
            dve.sem_inc(t3m_ready, NJ)
            dve.sem_inc(xy_ready, NJ)

            def split_weights(e, k):
                dve.wait_ge(we_hi, e + 1)
                dve.tensor_tensor(flat4(wes[:, k, 1, :, :, :]), flat4(we[:, k, :, :, :]), flat4(wes[:, k, 0, :, :, :]).bitcast(F32), ALU.subtract).then_inc(we_lo, 1)

            def expert(e, k, bc_loads, be_loads, more=True):
                base = e * NJ
                dve.wait_ge(bc_in[k], bc_loads)
                dve.wait_ge(be_in[k], be_loads)
                for n, (m, hf) in enumerate(jobs):
                    dve.wait_ge(h_ps, base + n + 1)
                    dve.wait_ge(h_ready, base + n + 1)
                    dve.tensor_tensor(t1[:, m, cols(hf)], ps[:, n % 2, 0:W], bc[:, k, 0, cols(hf)], ALU.mult).then_inc(t1_ready, 1)
                for n, (m, hf) in enumerate(jobs):
                    dve.wait_ge(x3_ps, base + n + 1)
                    dve.wait_ge(t3m_ready, base + n + 1)
                    dve.tensor_tensor(t3[:, m, cols(hf)], ps[:, 2 + n % 2, 0:W], bc[:, k, 0, cols(hf)], ALU.mult).then_inc(t3_ready, 1)
                    dve.wait_ge(t3_ready, base + n + 3)
                    dve.wait_ge(y_ready, base + n + 1)
                    dve.scalar_tensor_tensor(out=t3m[:, m, cols(hf)], in0=t3[:, m, cols(hf)], scalar=be[:, k, 2, m:m + 1],
                                             in1=bc[:, k, 1, cols(hf)], op0=ALU.add, op1=ALU.mult).then_inc(t3m_ready, 1)
                if more:
                    split_weights(e + 1, 1 - k)
                for n, (m, hf) in enumerate(jobs):
                    dve.wait_ge(x2_ps, base + n + 2)
                    dve.wait_ge(t3m_ready, base + NJ + n + 1)
                    dve.scalar_tensor_tensor(out=t3m[:, m, cols(hf)], in0=ps[:, 4 + n, 0:W], scalar=be[:, k, 1, m:m + 1],
                                             in1=t3m[:, m, cols(hf)], op0=ALU.add, op1=ALU.mult).then_inc(xy_ready, 1)

            with dve.Fori(0, E // 2 - 1) as i:
                for k in range(2):
                    expert(i * 2 + k, k, i * 32 + 32, i * 16 + 16)
            expert(E - 2, 0, E // 2 * 32, E // 2 * 16)
            expert(E - 1, 1, E // 2 * 32, E // 2 * 16, more=False)
            for r in range(NR):
                dve.wait_ge(f_ps, r + 1)
                dve.tensor_tensor(w[:, r, :], ps[:, r % 4, 0:DM], x2[:, RT + r, :], ALU.add).then_inc(added, 1)
                dve.wait_ge(added, r + 1)
                dve.tensor_tensor(w[:, r, :], w[:, r, :], ps[:, 4 + r % 4, 0:DM], ALU.add).then_inc(f_ready, 1)

        @block.gpsimd
        def _(pool):
            pool.memset(yT[:, :, :], 0.0).then_inc(y_ready, NJ)
            pool.sem_inc(hl_ready, NJ)

            def add_to_y(base):
                for n, (m, hf) in enumerate(jobs):
                    pool.wait_ge(xy_ready, base + n + 1)
                    pool.wait_ge(y_ready, base + n)
                    pool.tensor_tensor(yT[:, m, cols(hf)], yT[:, m, cols(hf)], t3m[:, m, cols(hf)], ALU.add).then_inc(y_ready, 1)

            def split_h(base):
                for n, (m, hf) in enumerate(jobs):
                    pool.wait_ge(hh_ready, base + n + 1)
                    pool.tensor_tensor(hTs[:, 1, m, cols(hf)], hT[:, m, cols(hf)], hTs[:, 0, m, cols(hf)].bitcast(F32), ALU.subtract).then_inc(hl_ready, 1)

            split_h(0)
            with pool.Fori(0, E - 1) as e:
                add_to_y(e * NJ + NJ)
                split_h(e * NJ + NJ)
            add_to_y(E * NJ)


def build(nc, nb, d, x1_out):
    top_ctx = ExitStack()
    with top_ctx:
        def sb(name, shape, dt=F32):
            return top_ctx.enter_context(nc.sbuf_tensor(name, shape, dt))
        x1 = sb("x1", [P, (nb + 1) * RT, DM])
        top = dict(x1=x1, ident=sb("ident_sb", [P, P]), ones=sb("ones_sb", [P, 1]))
        cross_attention(nc, nb, top, d)
        sem = lambda name: top_ctx.enter_context(nc.semaphore(name))
        ew = dict(
            sw12=sb("sw12", [P, 2, 2, 512]),
            sws=sb("sws", [P, 2, 2, 2, 512], F32R),
            we=sb("we", [P, 2, 3, 2, DM]),
            wes=sb("wes", [P, 2, 2, 3, 2, DM], F32R),
            we_in=[sem(f"we_in{i}") for i in range(2)])
        ew |= {x: sem(x) for x in ("s_in", "sw_hi", "sw_lo", "we_hi", "we_lo")}
        recurrence(nc, nb, top, d, ew)
        experts(nc, nb, top, d, x1_out, ew)


NB = 4
SCRATCH = {"xnT": (NB, P, 2, ROWS), "wk_split": (HEADS // 2, P, 4, P), "wv_split": (NG, P, 4, QH * DH), "wm_rows": (16, NB * ROWS)}


def layout(I, nb):
    import numpy as np

    A = {}
    rep = lambda a, shape: np.broadcast_to(a, shape)
    fold = lambda a: a.reshape(2, P, -1).transpose(1, 0, 2)
    x, ctx = I["x"][:nb], I["ctx_768"][:nb]
    A["x"] = x.reshape(nb * RT, P, DM).transpose(1, 0, 2)
    t = ctx.transpose(0, 2, 1)
    c = np.stack([t[:, :P], np.concatenate([t[:, P:], t[:, P:]], 1)], 2)
    A["ctx"] = c.reshape(nb, P, 2, NC, CH).transpose(0, 3, 1, 2, 4)
    rows = lambda W: np.stack([W[:P], np.concatenate([W[P:], W[P:]], 0)], 1)
    A["wk"] = rows(I["L0_xattn_Wk"]).reshape(P, 2048)
    A["wv"] = rows(I["L0_xattn_Wv"]).reshape(P, 2048)
    A["wq"] = I["L0_xattn_Wq"].reshape(2, P, HEADS // 2, P).transpose(2, 1, 0, 3)
    wo = I["L0_xattn_Wo"].reshape(HEADS // 2, 2, 1, DH, DM)
    A["wo"] = rep(wo, (HEADS // 2, 2, 2, DH, DM)).reshape(HEADS // 2, 2, P, DM).transpose(0, 2, 1, 3)
    A["bo"] = rep(I["L0_xattn_bo"], (P, DM))
    A["ident"] = np.eye(P, dtype=np.float32)
    q, k, v, g = (I["L0_attn_" + n] for n in ("q_w", "k_w", "v_w", "g_w"))
    A["w4"] = np.stack([fold(m.T) for m in (q, k, v, g)], 1)
    f = np.float32
    inv = (f(1.0) / f(10000.0) ** (np.arange(8, dtype=f) / f(8))).astype(f)
    ang = np.arange(ROWS, dtype=f)[:, None] * inv[None, :]
    cos, sin = np.cos(ang).astype(f).T, np.sin(ang).astype(f).T
    dd = np.arange(P) % 16
    A["rope"] = np.stack([np.tile(cos[dd // 2], (1, 2)), np.tile(sin[dd // 2], (1, 2)) * np.where(dd % 2, -1, 1).astype(f)[:, None]], 1)
    bd = np.zeros((P, 2, 2, P), f)
    for i, n in enumerate(("Wq", "Wk")):
        for h in range(16):
            s = slice(16 * (h % 8), 16 * (h % 8) + 16)
            bd[s, i, h // 8, s] = I["L0_attn_" + n][h].T
    A["bd"] = np.stack([bd, bd[np.arange(P) ^ 1]], 2)
    A["gb"] = I["L0_attn_g_b"].reshape(2, P).T
    A["dl"] = I["L0_attn_base_decay_logits"].reshape(2, P).T
    A["seq"] = rep((np.arange(NB * ROWS) % ROWS != 0).astype(f), (P, NB * ROWS))
    p = np.arange(P)
    same = (p[:, None] // 16 == p[None, :] // 16)
    A["selv"] = np.stack([(same & (p[:, None] % 16 == e)).astype(f) for e in range(16)], 1)
    j = np.arange(32)
    A["sely"] = np.stack([((p[:, None] // 16 == j[None, :] // 4) & (j[None, :] % 4 == e)).astype(f) for e in range(4)], 1)
    order = 16 * (p % 32 // 4) + 4 * (p // 32) + p % 4
    A["ow"] = np.stack([I["L0_attn_out_w"].T[P * g + order] for g in range(2)], 1)
    A["vecs"] = np.stack([rep(I["L0_attn_" + n], (P, DM)) for n in ("out_b", "ln_g", "ln_b")], 1)
    A["gw"] = fold(I["L0_ffn_gate_w"].T)
    A["iota"] = rep(np.arange(8, dtype=f), (P, 8))
    A["we"] = np.stack([np.stack([fold(I["L0_ffn_" + n][e].T) for n in ("w1", "w2", "w3")], 1) for e in range(8)], 0)
    A["be"] = np.stack([I["L0_ffn_" + n].reshape(8, 2, P).transpose(0, 2, 1) for n in ("b1", "b2", "b3")], 2)
    A["sw12"] = np.stack([fold(I["L0_ffn_" + n].T) for n in ("sw1", "sw2")], 2)
    A["sw3"] = I["L0_ffn_sw3"].T.reshape(4, P, DM).transpose(1, 0, 2)
    return {n: np.ascontiguousarray(a, dtype=f) for n, a in A.items()}


def kernel(**inputs):
    import numpy as np
    from concourse import bacc
    from concourse.bass_utils import run_bass_kernel_spmd

    arrays = layout({n: np.asarray(a) for n, a in inputs.items()}, NB)
    nc = bacc.Bacc("TRN2", target_bir_lowering=False, num_devices=1)
    d = {n: nc.dram_tensor("in_" + n, a.shape, F32, kind="ExternalInput").ap() for n, a in arrays.items()}
    d |= {n: nc.dram_tensor(n, shape, F32).ap() for n, shape in SCRATCH.items()}
    out = nc.dram_tensor("out_0", (P, NB * RT, DM), F32, kind="ExternalOutput").ap()
    build(nc, NB, d, out)
    r = run_bass_kernel_spmd(nc, [{"in_" + n: a for n, a in arrays.items()}], core_ids=[0])
    return np.ascontiguousarray(r.results[0]["out_0"].transpose(1, 0, 2).reshape(NB, ROWS, DM))
```
